# Optimizing a Trainium2 kernel written in Bass

```python
import numpy as np
import jax
import jax.numpy as jnp

def _softmax(x, axis=-1):
    return jax.nn.softmax(x, axis=axis)

def _gelu(x):
    return jax.nn.gelu(x, approximate=True)

def _silu(x):
    return jax.nn.silu(x)

def _sigmoid(x):
    return jax.nn.sigmoid(x)

def _layernorm(x, axis=-1, eps=1e-05):
    m = jnp.mean(x, axis=axis, keepdims=True)
    v = jnp.var(x, axis=axis, keepdims=True)
    return (x - m) / jnp.sqrt(v + eps)

def _scatter_add(tgt, idx, src, axis=0):
    return tgt.at[idx].add(src)

def _segment_sum(src, seg, n):
    return jax.ops.segment_sum(src, seg, n)
kernel_name = 'mk_xattn_seq_d1_seqx_r4_04629a'

def setup_inputs(seed: int=0):
    np.random.seed(seed)
    _w = jnp.asarray

    def _rec_inputs():
        import jax
        import jax.numpy as jnp
        _rk = jax.random.key(seed)
        x = -0.0005207 + 1.001 * jax.random.normal(jax.random.fold_in(_rk, 1), (4, 1024, 256), jnp.float32)
        _lenS = 1024 - jax.random.randint(jax.random.fold_in(_rk, 7), (4,), 0, max(1, 1024 // 4) + 1, jnp.int32)
        _lenS2 = 77 - jax.random.randint(jax.random.fold_in(_rk, 8), (4,), 0, max(1, 77 // 4) + 1, jnp.int32)
        _ctx_1024P = jax.random.normal(jax.random.fold_in(_rk, 11), (4, 16, 256), jnp.float32)
        _ctx_1024c = jax.random.dirichlet(jax.random.fold_in(_rk, 511), 0.3 * jnp.ones((16,), jnp.float32), (4, 77))
        _ctx_1024t = jnp.einsum('bsk,bkd->bsd', _ctx_1024c, _ctx_1024P)
        _ctx_1024t = _ctx_1024t * jax.lax.rsqrt(jnp.mean(jnp.square(_ctx_1024t)) + 1e-12) * 0.953939
        ctx_1024 = 4.13588e-05 + 0.999923 * (_ctx_1024t + 0.3 * jax.random.normal(jax.random.fold_in(_rk, 611), (4, 77, 256), jnp.float32))
        return (x, ctx_1024)
    x, ctx_1024 = _rec_inputs()

    def _L0_xattn_setup():
        import jax, jax.numpy as jnp
        import numpy as np
        D, H, E, K, DFF = (256, 16, 8, 2, 1024)
        B, L, T = (4, 128, 512)
        EPS = 1e-05

        def _xavier(key, shape):
            fan_in, fan_out = (shape[-1], shape[-2])
            a = jnp.sqrt(6.0 / (fan_in + fan_out))
            return jax.random.uniform(key, shape, jnp.float32, -a, a)

        def _ln(x, g, b):
            m = x.mean(-1, keepdims=True)
            v = ((x - m) ** 2).mean(-1, keepdims=True)
            return (x - m) / jnp.sqrt(v + EPS) * g + b

        def _mha(q_in, kv_in, in_w, in_b, out_w, out_b):
            wq, wk, wv = jnp.split(in_w, 3, axis=0)
            bq, bk, bv = jnp.split(in_b, 3, axis=0)
            dh = D // H

            def heads(x, w, b):
                y = x @ w.T + b
                return y.reshape(x.shape[0], x.shape[1], H, dh).transpose(0, 2, 1, 3)
            q = heads(q_in, wq, bq)
            k = heads(kv_in, wk, bk)
            v = heads(kv_in, wv, bv)
            scores = jnp.einsum('bhqd,bhkd->bhqk', q, k) / jnp.sqrt(jnp.float32(dh))
            attn = jax.nn.softmax(scores, axis=-1)
            out = jnp.einsum('bhqk,bhkd->bhqd', attn, v)
            out = out.transpose(0, 2, 1, 3).reshape(q_in.shape[0], q_in.shape[1], D)
            return out @ out_w.T + out_b

        def _fuse_moe(x, ln_g, ln_b, rw, rb, fc1_w, fc1_b, fc2_w, fc2_b):
            h = _ln(x, ln_g, ln_b)
            logits = h @ rw.T + rb
            vals, idx = jax.lax.top_k(logits, K)
            gates = jax.nn.softmax(vals, axis=-1)
            N = x.shape[0] * x.shape[1]
            hf = h.reshape(N, D)
            h1 = jax.nn.gelu(jnp.einsum('nd,efd->enf', hf, fc1_w) + fc1_b[:, None, :], approximate=False)
            eo = jnp.einsum('enf,edf->end', h1, fc2_w) + fc2_b[:, None, :]
            idx_f = idx.reshape(N, K)
            gates_f = gates.reshape(N, K)
            gathered = eo[idx_f, jnp.arange(N)[:, None], :]
            mixed = (gathered * gates_f[..., None]).sum(axis=1).reshape(x.shape)
            return x + mixed
        key = jax.random.key(seed)
        ks = jax.random.split(key, 16)
        inp = {'latents': jax.random.normal(ks[0], (B, L, D), jnp.float32), 'tokens': jax.random.normal(ks[1], (B, T, D), jnp.float32), 'sa_ln_g': jnp.ones((D,)), 'sa_ln_b': jnp.zeros((D,)), 'sa_in_w': _xavier(ks[2], (3 * D, D)), 'sa_in_b': jnp.zeros((3 * D,)), 'sa_out_w': _xavier(ks[3], (D, D)), 'sa_out_b': jnp.zeros((D,)), 'ca_q_ln_g': jnp.ones((D,)), 'ca_q_ln_b': jnp.zeros((D,)), 'ca_kv_ln_g': jnp.ones((D,)), 'ca_kv_ln_b': jnp.zeros((D,)), 'ca_in_w': _xavier(ks[4], (3 * D, D)), 'ca_in_b': jnp.zeros((3 * D,)), 'ca_out_w': _xavier(ks[5], (D, D)), 'ca_out_b': jnp.zeros((D,)), 'moe_ln_g': jnp.ones((D,)), 'moe_ln_b': jnp.zeros((D,)), 'router_w': _xavier(ks[6], (E, D)), 'router_b': jnp.zeros((E,)), 'e_fc1_w': jax.vmap(lambda k: _xavier(k, (DFF, D)))(jax.random.split(ks[7], E)), 'e_fc1_b': jnp.zeros((E, DFF)), 'e_fc2_w': jax.vmap(lambda k: _xavier(k, (D, DFF)))(jax.random.split(ks[8], E)), 'e_fc2_b': jnp.zeros((E, D))}
        return inp
    _L0_xattn_all = _L0_xattn_setup()
    _L0_xattn_in = {k: v for k, v in _L0_xattn_all.items() if k in ('sa_ln_g', 'sa_ln_b', 'sa_in_w', 'sa_in_b', 'sa_out_w', 'sa_out_b', 'ca_q_ln_g', 'ca_q_ln_b', 'ca_kv_ln_g', 'ca_kv_ln_b', 'ca_in_w', 'ca_in_b', 'ca_out_w', 'ca_out_b', 'moe_ln_g', 'moe_ln_b', 'router_w', 'router_b', 'e_fc1_w', 'e_fc1_b', 'e_fc2_w', 'e_fc2_b')}
    del _L0_xattn_all
    return {'x': x, 'ctx_1024': ctx_1024, 'L0_xattn_sa_ln_g': _L0_xattn_in['sa_ln_g'], 'L0_xattn_sa_ln_b': _L0_xattn_in['sa_ln_b'], 'L0_xattn_sa_in_w': _L0_xattn_in['sa_in_w'], 'L0_xattn_sa_in_b': _L0_xattn_in['sa_in_b'], 'L0_xattn_sa_out_w': _L0_xattn_in['sa_out_w'], 'L0_xattn_sa_out_b': _L0_xattn_in['sa_out_b'], 'L0_xattn_ca_q_ln_g': _L0_xattn_in['ca_q_ln_g'], 'L0_xattn_ca_q_ln_b': _L0_xattn_in['ca_q_ln_b'], 'L0_xattn_ca_kv_ln_g': _L0_xattn_in['ca_kv_ln_g'], 'L0_xattn_ca_kv_ln_b': _L0_xattn_in['ca_kv_ln_b'], 'L0_xattn_ca_in_w': _L0_xattn_in['ca_in_w'], 'L0_xattn_ca_in_b': _L0_xattn_in['ca_in_b'], 'L0_xattn_ca_out_w': _L0_xattn_in['ca_out_w'], 'L0_xattn_ca_out_b': _L0_xattn_in['ca_out_b'], 'L0_xattn_moe_ln_g': _L0_xattn_in['moe_ln_g'], 'L0_xattn_moe_ln_b': _L0_xattn_in['moe_ln_b'], 'L0_xattn_router_w': _L0_xattn_in['router_w'], 'L0_xattn_router_b': _L0_xattn_in['router_b'], 'L0_xattn_e_fc1_w': _L0_xattn_in['e_fc1_w'], 'L0_xattn_e_fc1_b': _L0_xattn_in['e_fc1_b'], 'L0_xattn_e_fc2_w': _L0_xattn_in['e_fc2_w'], 'L0_xattn_e_fc2_b': _L0_xattn_in['e_fc2_b']}

def reference(x, ctx_1024, L0_xattn_sa_ln_g, L0_xattn_sa_ln_b, L0_xattn_sa_in_w, L0_xattn_sa_in_b, L0_xattn_sa_out_w, L0_xattn_sa_out_b, L0_xattn_ca_q_ln_g, L0_xattn_ca_q_ln_b, L0_xattn_ca_kv_ln_g, L0_xattn_ca_kv_ln_b, L0_xattn_ca_in_w, L0_xattn_ca_in_b, L0_xattn_ca_out_w, L0_xattn_ca_out_b, L0_xattn_moe_ln_g, L0_xattn_moe_ln_b, L0_xattn_router_w, L0_xattn_router_b, L0_xattn_e_fc1_w, L0_xattn_e_fc1_b, L0_xattn_e_fc2_w, L0_xattn_e_fc2_b):
    import jax
    import jax.numpy as jnp

    def _L0_xattn_ref(latents, tokens, sa_ln_g, sa_ln_b, sa_in_w, sa_in_b, sa_out_w, sa_out_b, ca_q_ln_g, ca_q_ln_b, ca_kv_ln_g, ca_kv_ln_b, ca_in_w, ca_in_b, ca_out_w, ca_out_b, moe_ln_g, moe_ln_b, router_w, router_b, e_fc1_w, e_fc1_b, e_fc2_w, e_fc2_b):
        import jax, jax.numpy as jnp
        import numpy as np
        D, H, E, K, DFF = (256, 16, 8, 2, 1024)
        B, L, T = (4, 128, 512)
        EPS = 1e-05

        def _xavier(key, shape):
            fan_in, fan_out = (shape[-1], shape[-2])
            a = jnp.sqrt(6.0 / (fan_in + fan_out))
            return jax.random.uniform(key, shape, jnp.float32, -a, a)

        def _ln(x, g, b):
            m = x.mean(-1, keepdims=True)
            v = ((x - m) ** 2).mean(-1, keepdims=True)
            return (x - m) / jnp.sqrt(v + EPS) * g + b

        def _mha(q_in, kv_in, in_w, in_b, out_w, out_b):
            wq, wk, wv = jnp.split(in_w, 3, axis=0)
            bq, bk, bv = jnp.split(in_b, 3, axis=0)
            dh = D // H

            def heads(x, w, b):
                y = x @ w.T + b
                return y.reshape(x.shape[0], x.shape[1], H, dh).transpose(0, 2, 1, 3)
            q = heads(q_in, wq, bq)
            k = heads(kv_in, wk, bk)
            v = heads(kv_in, wv, bv)
            scores = jnp.einsum('bhqd,bhkd->bhqk', q, k) / jnp.sqrt(jnp.float32(dh))
            attn = jax.nn.softmax(scores, axis=-1)
            out = jnp.einsum('bhqk,bhkd->bhqd', attn, v)
            out = out.transpose(0, 2, 1, 3).reshape(q_in.shape[0], q_in.shape[1], D)
            return out @ out_w.T + out_b

        def _fuse_moe(x, ln_g, ln_b, rw, rb, fc1_w, fc1_b, fc2_w, fc2_b):
            h = _ln(x, ln_g, ln_b)
            logits = h @ rw.T + rb
            vals, idx = jax.lax.top_k(logits, K)
            gates = jax.nn.softmax(vals, axis=-1)
            N = x.shape[0] * x.shape[1]
            hf = h.reshape(N, D)
            h1 = jax.nn.gelu(jnp.einsum('nd,efd->enf', hf, fc1_w) + fc1_b[:, None, :], approximate=False)
            eo = jnp.einsum('enf,edf->end', h1, fc2_w) + fc2_b[:, None, :]
            idx_f = idx.reshape(N, K)
            gates_f = gates.reshape(N, K)
            gathered = eo[idx_f, jnp.arange(N)[:, None], :]
            mixed = (gathered * gates_f[..., None]).sum(axis=1).reshape(x.shape)
            return x + mixed
        q = _ln(latents, sa_ln_g, sa_ln_b)
        x = latents + _mha(q, q, sa_in_w, sa_in_b, sa_out_w, sa_out_b)
        qc = _ln(x, ca_q_ln_g, ca_q_ln_b)
        kv = _ln(tokens, ca_kv_ln_g, ca_kv_ln_b)
        x = x + _mha(qc, kv, ca_in_w, ca_in_b, ca_out_w, ca_out_b)
        return _fuse_moe(x, moe_ln_g, moe_ln_b, router_w, router_b, e_fc1_w, e_fc1_b, e_fc2_w, e_fc2_b)
    x = _L0_xattn_ref(x, ctx_1024, L0_xattn_sa_ln_g, L0_xattn_sa_ln_b, L0_xattn_sa_in_w, L0_xattn_sa_in_b, L0_xattn_sa_out_w, L0_xattn_sa_out_b, L0_xattn_ca_q_ln_g, L0_xattn_ca_q_ln_b, L0_xattn_ca_kv_ln_g, L0_xattn_ca_kv_ln_b, L0_xattn_ca_in_w, L0_xattn_ca_in_b, L0_xattn_ca_out_w, L0_xattn_ca_out_b, L0_xattn_moe_ln_g, L0_xattn_moe_ln_b, L0_xattn_router_w, L0_xattn_router_b, L0_xattn_e_fc1_w, L0_xattn_e_fc1_b, L0_xattn_e_fc2_w, L0_xattn_e_fc2_b)
    return x

_drawn_inputs = setup_inputs


def setup_inputs(seed=0):
    import zlib

    import numpy as np

    out = dict(_drawn_inputs(seed))
    spreads = {'L0_xattn_sa_ln_g': (1.0, 0.6),
     'L0_xattn_sa_ln_b': (0.0, 0.1),
     'L0_xattn_sa_in_b': (0.0, 0.1),
     'L0_xattn_sa_out_b': (0.0, 0.1),
     'L0_xattn_ca_q_ln_g': (1.0, 0.2),
     'L0_xattn_ca_q_ln_b': (0.0, 0.412),
     'L0_xattn_ca_kv_ln_g': (1.0, 0.2),
     'L0_xattn_ca_kv_ln_b': (0.0, 0.1),
     'L0_xattn_ca_in_b': (0.0, 0.1),
     'L0_xattn_ca_out_b': (0.0, 0.1),
     'L0_xattn_moe_ln_g': (1.0, 0.2),
     'L0_xattn_moe_ln_b': (0.0, 0.1),
     'L0_xattn_router_b': (0.0, 0.1),
     'L0_xattn_e_fc1_b': (0.0, 0.1),
     'L0_xattn_e_fc2_b': (0.0, 0.1)}
    factors = {}
    for name, (base, spread) in spreads.items():
        noise = np.random.default_rng([zlib.crc32(name.encode()), seed]).standard_normal(out[name].shape)
        drawn = base * np.exp(spread * noise) if base else spread * noise
        out[name] = jnp.asarray(drawn.astype(out[name].dtype))
    for name, factor in factors.items():
        out[name] = (out[name] * factor).astype(out[name].dtype)
    return out
```

```python
from contextlib import ExitStack

import numpy as np

import concourse.bass as bass
from concourse import mybir

F32 = mybir.dt.float32
BF16 = mybir.dt.bfloat16
F16 = mybir.dt.float16
I32 = mybir.dt.int32
ALU = mybir.AluOpType
ACT = mybir.ActivationFunctionType
AX_X = mybir.AxisListType.X

P = 128
D = 256
DC = D // P
HEADS = 16
DH = D // HEADS
BATCH = 4
SEQ = 1024
CTX = 77
N = BATCH * SEQ
NT = N // P
E = 8
TOP = 2
F = 1024
FC = F // P
EPS = 1e-5
TPB = 4
HG = 4
GROUPS = BATCH * HEADS // HG
VW = 2 * DH
PARTS = 3
Q_STACK = [0, 0, 0, 1, 1, 2]
K_STACK = [0, 1, 2, 0, 1, 0]
SR = len(Q_STACK) * DH
SLOT_TILES = TOP * NT + E
SLOTS = SLOT_TILES * P
W_SCALE = 64.0
BIG = 3.0e38


def tokens_phase(nc, name, x_dram, rows, blocks, *, ln_g, ln_b, ident_dram,
                 attn=None, qk=None, v=None, router=None):
    W = TPB * rows
    qk_chunks = qk[0].shape[1] // P if qk else 0
    with ExitStack() as ctx:
        def sb(n, shape, dt):
            return ctx.enter_context(nc.sbuf_tensor(f"{name}_{n}", shape, dt))

        def ps(n, shape):
            return ctx.enter_context(nc.psum_tensor(f"{name}_{n}", shape, F32))

        def sem(n):
            return ctx.enter_context(nc.semaphore(f"{name}_{n}"))

        ident = sb("ident", [P, P], F32)
        g_col = sb("g_col", [P, DC], F32)
        b_col = sb("b_col", [P, DC], F32)
        x_sb = sb("x", [rows, TPB, D], F32)
        stats = sb("stats", [rows, TPB, 6], F32)
        mean2 = sb("mean2", [rows, TPB], F32)
        diff = sb("diff", [rows, TPB], F32)
        m2 = sb("m2", [rows, TPB], F32)
        mean = sb("mean", [rows, TPB], F32)
        dd = sb("dd", [rows, TPB], F32)
        var_sum = sb("var_sum", [rows, TPB], F32)
        var = sb("var", [rows, TPB], F32)
        std = sb("std", [rows, TPB], F32)
        r0 = sb("r0", [rows, TPB], F32)
        r0sq = sb("r0sq", [rows, TPB], F32)
        newton = sb("newton", [rows, TPB], F32)
        newton2 = sb("newton2", [rows, TPB], F32)
        rstd = sb("rstd", [rows, TPB], F32)
        xhat = sb("xhat", [rows, TPB, D], F32)
        xT = sb("xT", [P, DC, W], F32)
        psT = ps("psT", [P, DC, 512])
        consts = sem("consts")
        x_loaded = sem("x_loaded")
        x_used = sem("x_used")
        dve = sem("dve")
        std_ready = sem("std_ready")
        xhat_ready = sem("xhat_ready")
        transposed = sem("transposed")
        xT_ready = sem("xT_ready")
        stored = sem("stored")
        n_consts = 3
        if attn:
            o_dram, w_out_t, b_out, x_out = attn
            oT = sb("oT", [P, DC, W], F32)
            sT = sb("sT", [P, DC, W], F32)
            rT = sb("rT", [P, DC, W], F32)
            onT = sb("onT", [P, DC, W], F32)
            wo = sb("wo", [P, DC, D], F32)
            bo = sb("bo", [rows, D], F32)
            xb = sb("xb", [rows, TPB, D], F32)
            x1 = sb("x1", [rows, TPB, D], F32)
            psY = ps("psY", [rows, TPB, D])
            o_loaded = sem("o_loaded")
            on_ready = sem("on_ready")
            projected = sem("projected")
            x1_ready = sem("x1_ready")
            x1_stored = sem("x1_stored")
            n_consts += 2
        x_ln = x1 if attn else x_sb
        if qk:
            w_qk = sb("w_qk", [P, DC, qk_chunks * P], F32)
            b_qk = sb("b_qk", [P, qk_chunks], F32)
            qf = sb("qf", [P, qk_chunks, W], F32)
            rest = sb("rest", [P, qk_chunks, W], F32)
            part = [sb(f"part{i}", [P, qk_chunks, W], BF16) for i in range(PARTS)]
            psQK = ps("psQK", [P, 2, 512])
            qk_done = sem("qk_done")
            qf_ready = sem("qf_ready")
            parts_ready = sem("parts_ready")
            parts_stored = sem("parts_stored")
            n_consts += 2
        if v:
            w_v = sb("w_v", [P, DC, D], F32)
            b_v = sb("b_v", [rows, D], F32)
            v_sb = sb("v_sb", [rows, TPB, HEADS, VW], F32)
            psV = ps("psV", [rows, TPB, D])
            v_done = sem("v_done")
            v_ones = sem("v_ones")
            v_ready = sem("v_ready")
            n_consts += 2
        if router:
            w_r = sb("w_r", [P, DC, E], F32)
            b_r = sb("b_r", [rows, E], F32)
            psL = ps("psL", [rows, TPB, E])
            logits_done = sem("logits_done")
            logits_ready = sem("logits_ready")
            n_consts += 2
        n_stores = (1 if v else 0) + (1 if router else 0)
        LN_OPS = TPB + 12
        SPLIT_OPS = 1 if qk else 0
        N_ATT = 1 if attn else 0
        N_DVE = N_ATT + LN_OPS + SPLIT_OPS

        def loop(eng, body):
            if blocks == 1:
                body(0)
            else:
                with eng.Fori(0, blocks) as blk:
                    body(blk)

        x_rows = x_dram.rearrange("(b t p) d -> b p t d", p=rows, t=TPB)
        with nc.Block() as block:

            @block.sync
            def _(sp):
                sp.dma_start(ident[:], ident_dram).then_inc(consts, 16)
                sp.dma_start(g_col[:], ln_g).then_inc(consts, 16)
                sp.dma_start(b_col[:], ln_b).then_inc(consts, 16)

                def wide(dst, vec):
                    sp.dma_start(dst, vec.rearrange("(a n) -> a n", a=1).broadcast_to(
                        [rows, vec.shape[0]])).then_inc(consts, 16)
                if attn:
                    sp.dma_start(wo[:], w_out_t.rearrange("(c p) n -> p c n", p=P)).then_inc(consts, 16)
                    wide(bo[:], b_out)
                if qk:
                    sp.dma_start(w_qk[:], qk[0].rearrange("(c p) n -> p c n", p=P)).then_inc(consts, 16)
                    sp.dma_start(b_qk[:], qk[1]).then_inc(consts, 16)
                if v:
                    sp.dma_start(w_v[:], v[0].rearrange("(c p) n -> p c n", p=P)).then_inc(consts, 16)
                    wide(b_v[:], v[1])
                if router:
                    sp.dma_start(w_r[:], router[0].rearrange("(c p) n -> p c n", p=P)).then_inc(consts, 16)
                    wide(b_r[:], router[1])

                def body(blk):
                    if attn:
                        sp.wait_ge(x_used, blk)
                    else:
                        sp.wait_ge(xhat_ready, blk * TPB)
                    sp.dma_start(x_sb[:], x_rows[bass.ds(blk, 1)].rearrange("b p t d -> p (b t) d")
                                 ).then_inc(x_loaded, 16)
                    if attn:
                        for dst, which in ((oT, 0), (sT, 1)):
                            sp.dma_start(dst[:], o_dram[which].rearrange("(c p) n -> p c n", p=P)[
                                :, :, bass.ds(blk * W, W)]).then_inc(o_loaded, 16)
                        sp.wait_ge(x1_ready, blk + 1)
                        sp.dma_start(x_out.rearrange("(b t p) d -> b p t d", p=rows, t=TPB)[
                            bass.ds(blk, 1)].rearrange("b p t d -> p (b t) d"), x1[:]).then_inc(x1_stored, 16)
                    if router:
                        sp.wait_ge(xhat_ready, blk * TPB + TPB)
                        sp.dma_start(router[3][:, bass.ds(blk * TPB, TPB), :], xhat[:]).then_inc(stored, 16)
                    if v:
                        sp.wait_ge(v_ready, blk * TPB + TPB)
                        sp.dma_start(v[2].rearrange("(b t p) n -> b p t n", p=rows, t=TPB)[
                            bass.ds(blk, 1)].rearrange("b p t n -> p (b t) n"),
                            v_sb[:].rearrange("p t h w -> p t (h w)")).then_inc(stored, 16)
                loop(sp, body)
                if n_stores:
                    sp.wait_ge(stored, 16 * n_stores * blocks)
                if attn:
                    sp.wait_ge(x1_stored, 16 * blocks)

            @block.gpsimd
            def _(pool):
                if v:
                    pool.memset(v_sb[:], 1.0).then_inc(v_ones, 1)

                def body(blk):
                    for i in range(PARTS):
                        pool.wait_ge(parts_ready, blk * PARTS + i + 1)
                        pool.dma_start(qk[2][i].rearrange("(c p) n -> p c n", p=P)[
                            :, :, bass.ds(blk * W, W)], part[i][:]).then_inc(parts_stored, 16)
                if qk:
                    loop(pool, body)
                    pool.wait_ge(parts_stored, 16 * PARTS * blocks)

            @block.vector
            def _(dv):
                dv.wait_ge(consts, 16 * n_consts)
                if v:
                    dv.wait_ge(v_ones, 1)

                def body(blk):
                    k = 0

                    def step(ins):
                        nonlocal k
                        k += 1
                        return ins.then_inc(dve, 1)

                    def own():
                        dv.wait_ge(dve, blk * N_DVE + k)
                    if attn:
                        dv.wait_ge(projected, blk)
                        dv.wait_ge(o_loaded, blk * 32 + 32)
                        step(dv.reciprocal(rT[:], sT[:]))
                        own()
                        dv.tensor_tensor(onT[:], oT[:], rT[:], ALU.mult).then_inc(on_ready, 1)
                        dv.wait_ge(x_loaded, blk * 16 + 16)
                        dv.tensor_tensor(xb[:], x_sb[:], bo[:, None, :].broadcast_to([rows, TPB, D]),
                                         ALU.add).then_inc(x_used, 1)
                        dv.wait_ge(x_used, blk + 1)
                        dv.wait_ge(x1_stored, blk * 16)
                        dv.wait_ge(projected, blk + 1)
                        dv.tensor_tensor(x1[:], psY[:], xb[:], ALU.add).then_inc(x1_ready, 1)
                        dv.wait_ge(x1_ready, blk + 1)
                    else:
                        dv.wait_ge(x_loaded, blk * 16 + 16)
                    for t in range(TPB):
                        step(dv.bn_stats(stats[:, t, :], x_ln[:, t, :]))
                    own()
                    step(dv.tensor_tensor(mean2[:], stats[:, :, 1], stats[:, :, 4], ALU.add))
                    step(dv.tensor_tensor(diff[:], stats[:, :, 1], stats[:, :, 4], ALU.subtract))
                    step(dv.tensor_tensor(m2[:], stats[:, :, 2], stats[:, :, 5], ALU.add))
                    own()
                    step(dv.tensor_scalar(mean[:], mean2[:], 0.5, None, ALU.mult))
                    step(dv.scalar_tensor_tensor(dd[:], diff[:], D / 4, diff[:], ALU.mult, ALU.mult))
                    own()
                    step(dv.tensor_tensor(var_sum[:], dd[:], m2[:], ALU.add))
                    own()
                    step(dv.tensor_scalar(var[:], var_sum[:], 1.0 / D, EPS, ALU.mult, ALU.add))
                    dv.wait_ge(std_ready, blk + 1)
                    step(dv.reciprocal(r0[:], std[:]))
                    own()
                    step(dv.tensor_tensor(r0sq[:], r0[:], r0[:], ALU.mult))
                    own()
                    step(dv.tensor_tensor(newton[:], r0sq[:], var[:], ALU.mult))
                    own()
                    step(dv.tensor_scalar(newton2[:], newton[:], -0.5, 1.5, ALU.mult, ALU.add))
                    own()
                    step(dv.tensor_tensor(rstd[:], newton2[:], r0[:], ALU.mult))
                    own()
                    dv.wait_ge(transposed, blk)
                    if router:
                        dv.wait_ge(stored, blk * 16)
                    for t in range(TPB):
                        dv.tensor_scalar(xhat[:, t, :], x_ln[:, t, :], mean[:, t:t + 1],
                                         rstd[:, t:t + 1], ALU.subtract, ALU.mult).then_inc(xhat_ready, 1)
                    if v:
                        dv.wait_ge(v_done, blk + 1)
                        dv.wait_ge(stored, blk * 16 * n_stores)
                        for t in range(TPB):
                            dv.tensor_tensor(
                                v_sb[:, t, :, 0:DH], psV[:, t, :].rearrange("p (h w) -> p h w", h=HEADS),
                                b_v[:].rearrange("p (h w) -> p h w", h=HEADS), ALU.add).then_inc(v_ready, 1)
                    if qk:
                        dv.wait_ge(parts_stored, blk * 16 * PARTS)
                        dv.wait_ge(qf_ready, blk * qk_chunks + qk_chunks)
                        dv.tensor_copy(part[0][:], qf[:]).then_inc(parts_ready, 1)
                        dv.wait_ge(parts_ready, blk * PARTS + 1)
                        step(dv.tensor_tensor(rest[:], qf[:], part[0][:], ALU.subtract))
                        own()
                        dv.tensor_copy(part[1][:], rest[:]).then_inc(parts_ready, 1)
                        dv.wait_ge(parts_ready, blk * PARTS + 2)
                        dv.tensor_tensor(part[2][:], rest[:], part[1][:], ALU.subtract
                                         ).then_inc(parts_ready, 1)
                    if router:
                        dv.wait_ge(logits_done, blk + 1)
                        dv.tensor_tensor(router[2][:, bass.ds(blk * TPB, TPB), :], psL[:],
                                         b_r[:, None, :].broadcast_to([rows, TPB, E]), ALU.add
                                         ).then_inc(logits_ready, 1)
                    assert k == N_DVE, (k, N_DVE)
                loop(dv, body)

            VAR_AT = N_ATT + TPB + 7

            @block.scalar
            def _(act):
                act.wait_ge(consts, 16 * n_consts)

                def body(blk):
                    act.wait_ge(dve, blk * N_DVE + VAR_AT)
                    act.activation(std[:], var[:], ACT.Sqrt).then_inc(std_ready, 1)
                    act.wait_ge(transposed, blk + 1)
                    if v:
                        act.wait_ge(v_done, blk)
                    if qk:
                        act.wait_ge(qk_done, blk * qk_chunks)
                    if router:
                        act.wait_ge(logits_done, blk)
                    for c in range(DC):
                        act.activation(xT[:, c, :], psT[:, c, 0:W], ACT.Identity, bias=b_col[:, c:c + 1],
                                       scale=g_col[:, c:c + 1]).then_inc(xT_ready, 1)
                    for s in range(qk_chunks):
                        if s == 0:
                            act.wait_ge(parts_ready, blk * PARTS)
                        act.wait_ge(qk_done, blk * qk_chunks + s + 1)
                        act.activation(qf[:, s, :], psQK[:, s % 2, 0:W], ACT.Identity,
                                       bias=b_qk[:, s:s + 1]).then_inc(qf_ready, 1)
                loop(act, body)

            @block.tensor
            def _(pe):
                pe.wait_ge(consts, 16 * n_consts)

                def body(blk):
                    if attn:
                        pe.wait_ge(x1_ready, blk)
                        pe.wait_ge(on_ready, blk + 1)
                        for t in range(TPB):
                            for c in range(DC):
                                mm = pe.matmul(psY[:, t, :], onT[:, c, t * rows:(t + 1) * rows], wo[:, c, :],
                                               start=(c == 0), stop=(c == DC - 1))
                        mm.then_inc(projected, 1)
                    pe.wait_ge(xT_ready, blk * DC)
                    for t in range(TPB):
                        pe.wait_ge(xhat_ready, blk * TPB + t + 1)
                        for c in range(DC):
                            mm = pe.transpose(psT[:, c, t * rows:(t + 1) * rows],
                                              xhat[:, t, c * P:(c + 1) * P], ident[0:rows, 0:rows])
                    mm.then_inc(transposed, 1)
                    pe.wait_ge(xT_ready, blk * DC + DC)
                    for s in range(qk_chunks):
                        pe.wait_ge(qf_ready, blk * qk_chunks + max(s - 1, 0))
                        for c in range(DC):
                            mm = pe.matmul(psQK[:, s % 2, 0:W], w_qk[:, c, s * P:(s + 1) * P], xT[:, c, :],
                                           start=(c == 0), stop=(c == DC - 1))
                        mm.then_inc(qk_done, 1)
                    if v:
                        pe.wait_ge(v_ready, blk * TPB)
                        for t in range(TPB):
                            for c in range(DC):
                                mm = pe.matmul(psV[:, t, :], xT[:, c, t * rows:(t + 1) * rows], w_v[:, c, :],
                                               start=(c == 0), stop=(c == DC - 1))
                        mm.then_inc(v_done, 1)
                    if router:
                        pe.wait_ge(logits_ready, blk)
                        for t in range(TPB):
                            for c in range(DC):
                                mm = pe.matmul(psL[:, t, :], xT[:, c, t * rows:(t + 1) * rows], w_r[:, c, :],
                                               start=(c == 0), stop=(c == DC - 1))
                        mm.then_inc(logits_done, 1)
                loop(pe, body)


def attention_phase(nc, name, q_parts, k_parts, v_dram, o_dram, ident_dram, *, keys, key_tiles):
    kp = keys // key_tiles
    steps = key_tiles * HG
    q_tiles = SEQ // P
    if key_tiles > 1:
        fills = HG * q_tiles * 2
        maxima = 1
        spread = [0] * 6 + [3] * 21 + [1] + [0] * 4
    else:
        fills = HG * 2
        maxima = q_tiles // 2
        spread = [2] * 4
    assert sum(spread) == fills and len(spread) == steps
    with ExitStack() as ctx:
        def sb(n, shape, dt):
            return ctx.enter_context(nc.sbuf_tensor(f"{name}_{n}", shape, dt))

        def ps(n, shape):
            return ctx.enter_context(nc.psum_tensor(f"{name}_{n}", shape, F32))

        def sem(n):
            return ctx.enter_context(nc.semaphore(f"{name}_{n}"))

        ident = sb("ident", [P, P], F32)
        q_st = [sb(f"q{u}", [SR + 1, HG, SEQ], BF16) for u in range(2)]
        k_st = [sb(f"k{u}", [SR + 1, HG, keys], BF16) for u in range(2)]
        v_st = [sb(f"v{u}", [kp, key_tiles, HG * VW], F32) for u in range(2)]
        maxs = sb("maxs", [P, fills * maxima], F32)
        maxs2 = sb("maxs2", [P, HG * q_tiles], F32)
        max_row = sb("max_row", [HG * q_tiles, P], BF16)
        probs = [[sb(f"p{z}_{h}", [kp, SEQ], F32) for h in range(HG)] for z in range(2)]
        o_sb = [sb(f"o{u}", [P, SEQ], F32) for u in range(2)]
        ps_s = [ps(f"s{z}", [kp, SEQ]) for z in range(2)]
        ps_m = [ps(f"m{z}", [P, 512]) for z in range(2)]
        ps_o = ps("o", [P, SEQ])

        consts = sem("consts")
        ones = sem("ones")
        loaded = [sem(f"loaded{u}") for u in range(2)]
        filled = sem("filled")
        taken = [sem(f"taken{z}") for z in range(2)]
        paired = sem("paired")
        turned = sem("turned")
        row_ready = sem("row_ready")
        row_placed = sem("row_placed")
        scored = sem("scored")
        exps = [sem(f"exps{z}") for z in range(2)]
        weighted = [sem(f"weighted{z}") for z in range(2)]
        o_taken = sem("o_taken")
        stored = [sem(f"stored{u}") for u in range(2)]

        LOADS = 16 * (2 * len(Q_STACK) + 1)
        STORES = 16 * 2 * HG
        batches = key_tiles

        def prior(i, u, per_group, n):
            return i * per_group + (u * per_group + n) // 2, (u * per_group + n) % 2

        def loop(eng, body):
            with eng.Fori(0, GROUPS // 2 - 1) as i:
                body(i, 0, True)
                body(i, 1, True)
            body(GROUPS // 2 - 1, 0, True)
            body(GROUPS // 2 - 1, 1, False)

        with nc.Block() as block:

            @block.sync
            def _(sp):
                sp.dma_start(ident[:], ident_dram).then_inc(consts, 16)

                def load(b, hg, u):
                    for s in range(len(Q_STACK)):
                        for st, parts, stack, width in ((q_st, q_parts, Q_STACK, SEQ),
                                                        (k_st, k_parts, K_STACK, keys)):
                            sp.dma_start(
                                st[u][s * DH:(s + 1) * DH, :, :],
                                parts[stack[s]].rearrange("(g h d) n -> g d h n", h=HG, d=DH)[
                                    bass.ds(hg, 1), :, :, bass.ds(b * width, width)].rearrange(
                                        "g d h n -> (g d) h n")).then_inc(loaded[u], 16)
                    sp.dma_start(
                        v_st[u][:], v_dram.rearrange("(b t p) n -> b p t n", t=key_tiles, p=kp)[
                            bass.ds(b, 1), :, :, bass.ds(hg * HG * VW, HG * VW)].rearrange(
                                "b p t n -> p (b t) n")).then_inc(loaded[u], 16)

                def place_row(i, u):
                    sp.wait_ge(row_ready, 2 * i + u + 1)
                    sp.dma_start(q_st[u][SR:SR + 1, :, :].rearrange("a h n -> a (h n)"),
                                 max_row[:]).then_inc(row_placed, 16)

                load(0, 0, 0)
                load(0, 1, 1)
                place_row(0, 0)

                def body(i, b, hg, next_b, next_hg, more):
                    for u in range(2):
                        if more or u == 0:
                            place_row(i + u, 1 - u)
                        if more:
                            before, zp = prior(i, u, batches, key_tiles - 1)
                            sp.wait_ge(weighted[zp], before + 1)
                            load(next_b, next_hg + u, u)

                with sp.Fori(0, BATCH - 1) as b:
                    body(b * 2, b, 0, b, 2, True)
                    body(b * 2 + 1, b, 2, b + 1, 0, True)
                body(2 * BATCH - 2, BATCH - 1, 0, BATCH - 1, 2, True)
                body(2 * BATCH - 1, BATCH - 1, 2, None, None, False)

            @block.gpsimd
            def _(pool):
                for u in range(2):
                    pool.memset(k_st[u][SR:SR + 1, :, :], 1.0).then_inc(ones, 1)

                def store(i, b, hg, u):
                    pool.wait_ge(o_taken, (2 * i + u) * 2 + 2)
                    for h in range(HG):
                        for which in (1, 0):
                            pool.dma_start(
                                o_dram[which].rearrange("(g h d) n -> g h d n", h=HG, d=DH)[
                                    bass.ds(hg, 1), h, :, bass.ds(b * SEQ, SEQ)].rearrange(
                                        "g d n -> (g d) n"),
                                o_sb[u][h * VW + which * DH:h * VW + (which + 1) * DH, :]
                            ).then_inc(stored[u], 16)

                with pool.Fori(0, BATCH) as b:
                    for hg in range(HEADS // HG):
                        store(b * 2 + hg // 2, b, hg, hg % 2)
                for u in range(2):
                    pool.wait_ge(stored[u], STORES * GROUPS // 2)

            @block.tensor
            def _(pe):
                pe.wait_ge(consts, 16)
                pe.wait_ge(ones, 2)

                def fill(i, u, f):
                    if f == 0:
                        pe.wait_ge(loaded[u], i * LOADS + LOADS)
                        pe.wait_ge(row_ready, 2 * i + u)
                    before, z = prior(i, u, fills, f)
                    pe.wait_ge(taken[z], before)
                    if key_tiles > 1:
                        h, qt, half = f // (2 * q_tiles), f // 2 % q_tiles, f % 2
                        mm = pe.matmul(ps_m[z][:], q_st[u][0:SR, h, qt * P:(qt + 1) * P],
                                       k_st[u][0:SR, h, half * 512:(half + 1) * 512], start=True, stop=True)
                    else:
                        h = f // 2
                        for n in range(maxima):
                            qt = f % 2 * maxima + n
                            mm = pe.matmul(ps_m[z][:, n * keys:(n + 1) * keys],
                                           q_st[u][0:SR, h, qt * P:(qt + 1) * P],
                                           k_st[u][0:SR, h, :], start=True, stop=True)
                    mm.then_inc(filled, 1)

                def turn(i, u):
                    pe.wait_ge(paired, 2 * i + u + 1)
                    pe.transpose(ps_m[0][0:HG * q_tiles, 0:P], maxs2[:], ident[:]).then_inc(turned, 1)

                def score(i, u, s):
                    kt, h = s // HG, s % HG
                    if s == 0:
                        pe.wait_ge(row_placed, (2 * i + u) * 16 + 16)
                    before, z = prior(i, u, steps, s)
                    pe.wait_ge(exps[z], before)
                    for half in range(2):
                        mm = pe.matmul(ps_s[z][:, half * 512:(half + 1) * 512],
                                       k_st[u][:, h, kt * kp:(kt + 1) * kp],
                                       q_st[u][:, h, half * 512:(half + 1) * 512], start=True, stop=True)
                    mm.then_inc(scored, 1)

                def weigh(i, u, kt):
                    if kt == 0:
                        pe.wait_ge(o_taken, (2 * i + u) * 2)
                    for s in (kt * HG + HG - 2, kt * HG + HG - 1):
                        before, z = prior(i, u, steps, s)
                        pe.wait_ge(exps[z], before + 1)
                    zp = prior(i, u, batches, kt)[1]
                    for half in range(2):
                        for h in range(HG):
                            mm = pe.matmul(ps_o[h * VW:(h + 1) * VW, half * 512:(half + 1) * 512],
                                           v_st[u][:, kt, h * VW:(h + 1) * VW],
                                           probs[zp][h][:, half * 512:(half + 1) * 512],
                                           start=(kt == 0), stop=(kt == key_tiles - 1))
                    mm.then_inc(weighted[zp], 1)

                for f in range(fills):
                    fill(0, 0, f)
                turn(0, 0)

                def body(i, u, more):
                    f = 0
                    for s in range(steps):
                        score(i, u, s)
                        if more:
                            for _ in range(spread[s]):
                                fill(i + u, 1 - u, f)
                                f += 1
                            if f == fills and spread[s]:
                                turn(i + u, 1 - u)
                        if s % HG == HG - 1 and s > HG:
                            weigh(i, u, s // HG - 1)
                    weigh(i, u, key_tiles - 1)
                loop(pe, body)

            @block.scalar
            def _(act):
                act.preload_act_table(ACT.Exp)

                def body(i, u, more):
                    for s in range(steps):
                        kt, h = s // HG, s % HG
                        before, zp = prior(i, u, batches, kt)
                        if h == 0:
                            act.wait_ge(weighted[zp], before)
                        act.wait_ge(scored, (2 * i + u) * steps + s + 1)
                        z = prior(i, u, steps, s)[1]
                        act.activation(probs[zp][h][:], ps_s[z][:], ACT.Exp, scale=float(DH) ** -0.5
                                       ).then_inc(exps[z], 1)
                loop(act, body)

            @block.vector
            def _(dv):
                def take(i, u, f):
                    before, z = prior(i, u, fills, f)
                    dv.wait_ge(filled, (2 * i + u) * fills + f + 1)
                    src = ps_m[z][:, 0:512] if key_tiles > 1 else ps_m[z][:, 0:maxima * keys].rearrange(
                        "p (t k) -> p t k", t=maxima)
                    dv.tensor_reduce(maxs[:, f * maxima:(f + 1) * maxima], src, AX_X, ALU.max
                                     ).then_inc(taken[z], 1)

                def rows(i, u):
                    for z in range(2):
                        dv.wait_ge(taken[z], (2 * i + u) * (fills // 2) + fills // 2)
                    if key_tiles > 1:
                        dv.tensor_reduce(maxs2[:], maxs[:].rearrange("p (m a) -> p m a", a=2), AX_X,
                                         ALU.max).then_inc(paired, 1)
                    else:
                        dv.tensor_copy(maxs2[:], maxs[:]).then_inc(paired, 1)
                    dv.wait_ge(turned, 2 * i + u + 1)
                    dv.wait_ge(row_placed, (2 * i + u) * 16)
                    dv.tensor_scalar(max_row[:], ps_m[0][0:HG * q_tiles, 0:P], -1.0, None, ALU.mult
                                     ).then_inc(row_ready, 1)

                def evacuate(i, u):
                    before, zp = prior(i, u, batches, key_tiles - 1)
                    dv.wait_ge(weighted[zp], before + 1)
                    dv.wait_ge(stored[u], i * STORES)
                    for half in range(2):
                        dv.tensor_copy(o_sb[u][:, half * 512:(half + 1) * 512],
                                       ps_o[:, half * 512:(half + 1) * 512]).then_inc(o_taken, 1)

                for f in range(fills):
                    take(0, 0, f)
                rows(0, 0)

                def body(i, u, more):
                    if more:
                        for f in range(fills):
                            take(i + u, 1 - u, f)
                        rows(i + u, 1 - u)
                    evacuate(i, u)
                loop(dv, body)


def route_phase(nc, logits, xhat_all, gates, slots, tile_expert, xs_dram, c_dram):
    with ExitStack() as ctx:
        def sb(n, shape, dt=F32):
            return ctx.enter_context(nc.sbuf_tensor(f"route_{n}", shape, dt))

        def sem(n):
            return ctx.enter_context(nc.semaphore(f"route_{n}"))

        TE = [P, NT, E]
        rev = sb("rev", [P, E])
        tri = sb("tri", [P, P])
        ones = sb("ones", [P, P])
        tile_no = sb("tile_no", [1, SLOT_TILES])
        zeros = sb("zeros", [P, D])
        best = [sb(f"best{k}", [P, NT]) for k in range(TOP)]
        tie = sb("tie", TE)
        cand = sb("cand", TE)
        first = sb("first", [P, NT])
        sel = [sb(f"sel{k}", TE) for k in range(TOP)]
        others = sb("others", TE)
        chosen = sb("chosen", [P, NT * E])
        gap = sb("gap", [P, NT])
        gap_exp = sb("gap_exp", [P, NT])
        gap_sum = sb("gap_sum", [P, NT])
        totals = sb("totals", TE)
        upto = sb("upto", TE)
        before = sb("before", TE)
        padded = sb("padded", [P, E])
        padded_i = sb("padded_i", [P, E], I32)
        tiles_i = sb("tiles_i", [P, E], I32)
        tiles = sb("tiles", [P, E])
        tile_end = sb("tile_end", [P, E])
        tile_start = sb("tile_start", [P, E])
        slot_start = sb("slot_start", [P, E])
        place = sb("place", TE)
        place2 = sb("place2", TE)
        picked = [sb(f"picked{k}", TE) for k in range(TOP)]
        slot_f = sb("slot_f", [P, TOP, NT])
        past = sb("past", [1, SLOT_TILES, E])
        past_n = sb("past_n", [1, SLOT_TILES])
        past_c = sb("past_c", [1, SLOT_TILES])
        ps_rank = ctx.enter_context(nc.psum_tensor("route_rank", [P, 512], F32))
        ps_total = ctx.enter_context(nc.psum_tensor("route_total", [P, 512], F32))
        consts = sem("consts")
        zeroed = sem("zeroed")
        cleared = sem("cleared")
        dve = sem("dve")
        counted = sem("counted")
        gap_ready = sem("gap_ready")
        chosen_ready = sem("chosen_ready")
        exp_ready = sem("exp_ready")
        slots_ready = sem("slots_ready")
        scattered = sem("scattered")

        def wide_e(ap):
            return ap[:, :, None].broadcast_to(TE)

        def wide_t(ap):
            return ap[:, None, :].broadcast_to(TE)

        with nc.Block() as block:

            @block.sync
            def _(sp):
                for dst, key in ((rev, "rev"), (tri, "tri"), (ones, "ones"), (tile_no, "tile_no")):
                    sp.dma_start(dst[:], c_dram[key]).then_inc(consts, 16)
                sp.wait_ge(zeroed, 1)
                sp.dma_start(xs_dram.rearrange("(p t) d -> p t d", p=P),
                             zeros[:, None, :].broadcast_to([P, SLOT_TILES, D])).then_inc(cleared, 16)
                sp.wait_ge(cleared, 16)

            @block.scalar
            def _(act):
                act.wait_ge(gap_ready, 1)
                act.activation(gap_exp[:], gap[:], ACT.Exp).then_inc(exp_ready, 1)

            @block.tensor
            def _(pe):
                pe.wait_ge(chosen_ready, 1)
                pe.matmul(ps_rank[:, 0:NT * E], tri[:], chosen[:], start=True, stop=True)
                pe.matmul(ps_total[:, 0:NT * E], ones[:], chosen[:], start=True, stop=True
                          ).then_inc(counted, 1)

            @block.vector
            def _(dv):
                k = 0

                def step(ins):
                    nonlocal k
                    k += 1
                    ins.then_inc(dve, 1)

                def own():
                    dv.wait_ge(dve, k)

                dv.memset(zeros[:], 0.0).then_inc(zeroed, 1)
                dv.wait_ge(zeroed, 1)
                dv.wait_ge(consts, 64)
                src = logits
                for c in range(TOP):
                    step(dv.tensor_reduce(best[c][:], src[:], AX_X, ALU.max))
                    own()
                    step(dv.tensor_tensor(tie[:], src[:], wide_e(best[c]), ALU.is_equal))
                    own()
                    step(dv.tensor_tensor(cand[:], tie[:], wide_t(rev), ALU.mult))
                    own()
                    step(dv.tensor_reduce(first[:], cand[:], AX_X, ALU.max))
                    own()
                    step(dv.tensor_tensor(sel[c][:], wide_t(rev), wide_e(first), ALU.is_equal))
                    own()
                    if c == 0:
                        step(dv.scalar_tensor_tensor(others[:], sel[0][:], -BIG, src[:], ALU.mult, ALU.add))
                        own()
                        src = others
                dv.tensor_tensor(gap[:], best[1][:], best[0][:], ALU.subtract).then_inc(gap_ready, 1)
                dv.tensor_tensor(chosen[:].rearrange("p (t e) -> p t e", e=E), sel[0][:], sel[1][:], ALU.add
                                 ).then_inc(chosen_ready, 1)
                dv.wait_ge(exp_ready, 1)
                step(dv.tensor_scalar(gap_sum[:], gap_exp[:], 1.0, None, ALU.add))
                own()
                step(dv.reciprocal(gates[:, 0, :], gap_sum[:]))
                own()
                step(dv.tensor_tensor(gates[:, 1, :], gates[:, 0, :], gap_exp[:], ALU.mult))
                dv.wait_ge(counted, 1)
                step(dv.tensor_copy(totals[:], ps_total[:, 0:NT * E].rearrange("p (t e) -> p t e", e=E)))
                own()
                for e in range(E):
                    step(dv.tensor_tensor_scan(upto[:, :, e], totals[:, :, e], zeros[:, 0:NT], 0.0,
                                               ALU.add, ALU.add))
                own()
                step(dv.tensor_tensor(before[:], upto[:], totals[:], ALU.subtract))
                step(dv.tensor_scalar(padded[:], upto[:, NT - 1, :], float(P - 1), None, ALU.add))
                own()
                step(dv.tensor_copy(padded_i[:], padded[:]))
                own()
                step(dv.tensor_scalar(tiles_i[:], padded_i[:], P.bit_length() - 1, None,
                                      ALU.logical_shift_right))
                own()
                step(dv.tensor_copy(tiles[:], tiles_i[:]))
                own()
                step(dv.tensor_tensor_scan(tile_end[:], tiles[:], zeros[:, 0:E], 0.0, ALU.add, ALU.add))
                own()
                step(dv.tensor_tensor(tile_start[:], tile_end[:], tiles[:], ALU.subtract))
                own()
                step(dv.tensor_scalar(slot_start[:], tile_start[:], float(P), None, ALU.mult))
                own()
                step(dv.tensor_tensor(place[:], ps_rank[:, 0:NT * E].rearrange("p (t e) -> p t e", e=E),
                                      before[:], ALU.add))
                own()
                step(dv.tensor_tensor(place2[:], place[:], wide_t(slot_start), ALU.add))
                own()
                for c in range(TOP):
                    step(dv.tensor_tensor(picked[c][:], sel[c][:], place2[:], ALU.mult))
                own()
                for c in range(TOP):
                    step(dv.tensor_reduce(slot_f[:, c, :], picked[c][:], AX_X, ALU.add))
                own()
                dv.tensor_copy(slots[:], slot_f[:]).then_inc(slots_ready, 1)
                step(dv.tensor_tensor(past[:], tile_no[:, :, None].broadcast_to([1, SLOT_TILES, E]),
                                      tile_end[0:1, None, :].broadcast_to([1, SLOT_TILES, E]), ALU.is_ge))
                own()
                step(dv.tensor_reduce(past_n[:], past[:], AX_X, ALU.add))
                own()
                step(dv.tensor_scalar(past_c[:], past_n[:], float(E - 1), None, ALU.min))
                own()
                step(dv.tensor_copy(tile_expert[:], past_c[:]))
                own()

            @block.gpsimd
            def _(pool):
                pool.wait_ge(cleared, 16)
                pool.wait_ge(slots_ready, 1)
                for t in range(NT):
                    for c in range(TOP):
                        pool.indirect_dma_start(
                            out=xs_dram, out_offset=bass.IndirectOffsetOnAxis(ap=slots[:, c, t:t + 1], axis=0),
                            in_=xhat_all[:, t, :], in_offset=None).then_inc(scattered, 16)
                pool.wait_ge(scattered, 16 * NT * TOP)


def weights_phase(nc, w1_dram, w2_dram, w_parts):
    with ExitStack() as ctx:
        CH = 2048
        stage = [ctx.enter_context(nc.sbuf_tensor(f"w_stage{u}", [P, CH], F32)) for u in range(2)]
        loaded = [ctx.enter_context(nc.semaphore(f"w_loaded{u}")) for u in range(2)]
        high = ctx.enter_context(nc.semaphore("w_high"))
        low = ctx.enter_context(nc.semaphore("w_low"))
        chunks = [(e, w) for e in range(E) for w in range(2)]
        with nc.Block() as block:

            @block.sync
            def _(sp):
                for n, (e, w) in enumerate(chunks):
                    if n >= 2:
                        sp.wait_ge(low, n - 1)
                    src = (w1_dram, w2_dram)[w][e].rearrange("(c p) n -> p c n", p=P)
                    sp.dma_start(stage[n % 2][:].rearrange("p (c n) -> p c n", c=src.shape[1]), src
                                 ).then_inc(loaded[n % 2], 16)

            @block.scalar
            def _(act):
                for n, (e, w) in enumerate(chunks):
                    act.wait_ge(loaded[n % 2], 16 * (n // 2 + 1))
                    act.activation(w_parts[w][0][:, e, :], stage[n % 2][:], ACT.Copy, scale=W_SCALE
                                   ).then_inc(high, 1)

            @block.vector
            def _(dv):
                for n, (e, w) in enumerate(chunks):
                    dv.wait_ge(high, n + 1)
                    dv.scalar_tensor_tensor(w_parts[w][1][:, e, :], stage[n % 2][:], W_SCALE,
                                            w_parts[w][0][:, e, :], ALU.mult, ALU.subtract).then_inc(low, 1)


def expert_phase(nc, xs_dram, eo_dram, tile_expert, w_parts, b1_dram, b2_dram, ln_g, ln_b, ident_dram):
    (w1h, w1l), (w2h, w2l) = w_parts
    with ExitStack() as ctx:
        def sb(n, shape, dt=F32):
            return ctx.enter_context(nc.sbuf_tensor(f"moe_{n}", shape, dt))

        def two(n, shape, dt=F32):
            return [sb(f"{n}{u}", shape, dt) for u in range(2)]

        def ps(n, shape):
            return [ctx.enter_context(nc.psum_tensor(f"moe_{n}{u}", shape, F32)) for u in range(2)]

        def sem(n):
            return ctx.enter_context(nc.semaphore(f"moe_{n}"))

        def sems(n):
            return [sem(f"{n}{u}") for u in range(2)]

        ident = sb("ident", [P, P])
        g_col = sb("g_col", [P, DC])
        b_col = sb("b_col", [P, DC])
        xs = two("xs", [P, D])
        b1 = two("b1", [P, FC])
        b2 = two("b2", [P, D])
        hf = two("hf", [P, DC, P])
        hh = two("hh", [P, DC, P], F16)
        hl = two("hl", [P, DC, P], F16)
        h1 = two("h1", [P, FC, P])
        h1h = two("h1h", [P, FC, P], F16)
        h1l = two("h1l", [P, FC, P], F16)
        eo = two("eo", [P, D])
        ps_x = ps("psx", [P, 512])
        ps_h = ps("psh", [P, FC, P])
        ps_e = ps("pse", [P, 512])
        consts = sem("consts")
        xs_loaded = sems("xs_loaded")
        b_loaded = sems("b_loaded")
        turned = sems("turned")
        hf_ready = sems("hf_ready")
        hh_ready = sems("hh_ready")
        h_ready = sems("h_ready")
        up = sems("up")
        gelus = sems("gelus")
        h1h_ready = sems("h1h_ready")
        h1_ready = sems("h1_ready")
        down = sems("down")
        eo_ready = sems("eo_ready")
        stored = sems("stored")

        T = SLOT_TILES
        xs_t = xs_dram.rearrange("(t p) d -> p t d", p=P)
        eo_t = eo_dram.rearrange("(t p) d -> p t d", p=P)
        with nc.Block() as block:

            @block.sync
            def _(sp):
                sp.dma_start(ident[:], ident_dram).then_inc(consts, 16)
                sp.dma_start(g_col[:], ln_g).then_inc(consts, 16)
                sp.dma_start(b_col[:], ln_b).then_inc(consts, 16)

                with sp.Fori(0, T // 2) as i:
                    for u in range(2):
                        sp.wait_ge(turned[u], i)
                        sp.dma_start(xs[u][:], xs_t[:, bass.ds(2 * i + u, 1), :].rearrange(
                            "p t d -> p (t d)")).then_inc(xs_loaded[u], 16)
                        e = sp.value_load(tile_expert[0:1, bass.ds(2 * i + u, 1)], min_val=0, max_val=E - 1)
                        sp.wait_ge(eo_ready[u], i)
                        sp.dma_start(b2[u][:], b2_dram[bass.ds(e, 1), :].broadcast_to([P, D])
                                     ).then_inc(b_loaded[u], 16)
                        sp.dma_start(b1[u][:], b1_dram[bass.ds(e, 1)].rearrange("e p c -> p (e c)")
                                     ).then_inc(b_loaded[u], 16)

            @block.gpsimd
            def _(pool):
                with pool.Fori(0, T // 2) as i:
                    for u in range(2):
                        pool.wait_ge(eo_ready[u], i + 1)
                        pool.dma_start(eo_t[:, bass.ds(2 * i + u, 1), :].rearrange("p t d -> p (t d)"),
                                       eo[u][:]).then_inc(stored[u], 16)
                for u in range(2):
                    pool.wait_ge(stored[u], 16 * T // 2)

            @block.tensor
            def _(pe):
                pe.wait_ge(consts, 48)

                def turn(i, u):
                    pe.wait_ge(hf_ready[u], i)
                    pe.wait_ge(xs_loaded[u], i * 16 + 16)
                    for c in range(DC):
                        mm = pe.transpose(ps_x[u][:, c * P:(c + 1) * P], xs[u][:, c * P:(c + 1) * P], ident[:])
                    mm.then_inc(turned[u], 1)

                def layer1(i, u):
                    e = pe.value_load(tile_expert[0:1, bass.ds(2 * i + u, 1)], min_val=0, max_val=E - 1)
                    for fc in range(FC):
                        for c in range(DC):
                            at = bass.ds(e * (DC * F) + (c * F + fc * P), P)
                            w_high = w1h[:].rearrange("p e n -> p (e n)")[:, at]
                            w_low = w1l[:].rearrange("p e n -> p (e n)")[:, at]
                            out = ps_h[u][:, fc, :]
                            pe.matmul(out, w_high, hh[u][:, c, :], start=(c == 0), stop=False)
                            pe.matmul(out, w_high, hl[u][:, c, :], start=False, stop=False)
                            mm = pe.matmul(out, w_low, hh[u][:, c, :], start=False, stop=(c == DC - 1))
                        if fc % (FC // 2) == FC // 2 - 1:
                            mm.then_inc(up[u], 1)

                def layer2(i, u):
                    pe.wait_ge(eo_ready[u], i)
                    pe.wait_ge(h1_ready[u], i + 1)
                    e = tile_e[u]
                    for fc in range(FC):
                        at = bass.ds(e * (FC * D) + fc * D, D)
                        w_high = w2h[:].rearrange("p e n -> p (e n)")[:, at]
                        w_low = w2l[:].rearrange("p e n -> p (e n)")[:, at]
                        out = ps_e[u][:, 0:D]
                        pe.matmul(out, h1h[u][:, fc, :], w_high, start=(fc == 0), stop=False)
                        pe.matmul(out, h1h[u][:, fc, :], w_low, start=False, stop=False)
                        mm = pe.matmul(out, h1l[u][:, fc, :], w_high, start=False, stop=(fc == FC - 1))
                    mm.then_inc(down[u], 1)

                tile_e = [None, None]

                def expert_of(i, u):
                    tile_e[u] = pe.value_load(tile_expert[0:1, bass.ds(2 * i + u, 1)],
                                              min_val=0, max_val=E - 1)

                def up_waits(i, u):
                    pe.wait_ge(h_ready[u], i + 1)
                    pe.wait_ge(gelus[u], i * FC)

                turn(0, 0)
                turn(0, 1)
                up_waits(0, 0)
                layer1(0, 0)

                def body(i, u, more2, more1):
                    if more1:
                        up_waits(i + u, 1 - u)
                    if more2:
                        turn(i + 1, u)
                    if more1:
                        layer1(i + u, 1 - u)
                    expert_of(i, u)
                    layer2(i, u)

                with pe.Fori(0, T // 2 - 1) as i:
                    body(i, 0, True, True)
                    body(i, 1, True, True)
                body(T // 2 - 1, 0, False, True)
                body(T // 2 - 1, 1, False, False)

            @block.scalar
            def _(act):
                act.preload_act_table(ACT.Gelu)
                with act.Fori(0, T // 2) as i:
                    for u in range(2):
                        act.wait_ge(h1_ready[u], i)
                        act.wait_ge(b_loaded[u], i * 32 + 32)
                        for fc in range(FC):
                            if fc % (FC // 2) == 0:
                                act.wait_ge(up[u], i * 2 + fc // (FC // 2) + 1)
                            act.activation(h1[u][:, fc, :], ps_h[u][:, fc, :], ACT.Gelu,
                                           bias=b1[u][:, fc:fc + 1], scale=1.0 / W_SCALE).then_inc(gelus[u], 1)

            @block.vector
            def _(dv):
                dv.wait_ge(consts, 48)

                def normed(i, u):
                    dv.wait_ge(turned[u], i + 1)
                    for c in range(DC):
                        mm = dv.tensor_scalar(hf[u][:, c, :], ps_x[u][:, c * P:(c + 1) * P], g_col[:, c:c + 1],
                                              b_col[:, c:c + 1], ALU.mult, ALU.add)
                    mm.then_inc(hf_ready[u], 1)
                    dv.wait_ge(hf_ready[u], i + 1)
                    dv.wait_ge(up[u], 2 * i)
                    dv.tensor_copy(hh[u][:], hf[u][:]).then_inc(hh_ready[u], 1)
                    dv.wait_ge(hh_ready[u], i + 1)
                    dv.tensor_tensor(hl[u][:], hf[u][:], hh[u][:], ALU.subtract).then_inc(h_ready[u], 1)

                def hidden(i, u):
                    dv.wait_ge(down[u], i)
                    dv.wait_ge(gelus[u], i * FC + FC)
                    dv.tensor_copy(h1h[u][:], h1[u][:]).then_inc(h1h_ready[u], 1)
                    dv.wait_ge(h1h_ready[u], i + 1)
                    dv.tensor_tensor(h1l[u][:], h1[u][:], h1h[u][:], ALU.subtract).then_inc(h1_ready[u], 1)

                def output(i, u):
                    dv.wait_ge(stored[u], i * 16)
                    dv.wait_ge(down[u], i + 1)
                    dv.scalar_tensor_tensor(eo[u][:], ps_e[u][:, 0:D], 1.0 / W_SCALE, b2[u][:],
                                            ALU.mult, ALU.add).then_inc(eo_ready[u], 1)

                normed(0, 0)
                normed(0, 1)
                hidden(0, 0)

                def body(i, u, more2, more1):
                    if more2:
                        normed(i + 1, u)
                    if more1:
                        hidden(i + u, 1 - u)
                    output(i, u)

                with dv.Fori(0, T // 2 - 1) as i:
                    body(i, 0, True, True)
                    body(i, 1, True, True)
                body(T // 2 - 1, 0, False, True)
                body(T // 2 - 1, 1, False, False)


def combine_phase(nc, x_dram, eo_dram, gates, slots, out_dram):
    with ExitStack() as ctx:
        DEPTH = 4
        rows = [[ctx.enter_context(nc.sbuf_tensor(f"mix_rows{c}_{z}", [P, D], F32)) for z in range(DEPTH)]
                for c in range(TOP)]
        x_sb = [ctx.enter_context(nc.sbuf_tensor(f"mix_x{z}", [P, TPB, D], F32)) for z in range(2)]
        half = ctx.enter_context(nc.sbuf_tensor("mix_half", [P, 2, D], F32))
        out_sb = [ctx.enter_context(nc.sbuf_tensor(f"mix_out{z}", [P, TPB, D], F32)) for z in range(2)]

        def sem(n):
            return ctx.enter_context(nc.semaphore(f"mix_{n}"))
        gathered = [sem(f"gathered{z}") for z in range(DEPTH)]
        x_loaded = [sem(f"x_loaded{z}") for z in range(2)]
        half_ready = sem("half_ready")
        mixed = sem("mixed")
        stored = [sem(f"stored{z}") for z in range(2)]
        x_b = x_dram.rearrange("(b t p) d -> b p t d", t=TPB, p=P)
        out_b = out_dram.rearrange("(b t p) d -> b p t d", t=TPB, p=P)
        blocks = NT // TPB
        with nc.Block() as block:

            @block.gpsimd
            def _(pool):
                for t in range(NT):
                    if t >= DEPTH:
                        pool.wait_ge(mixed, t - DEPTH + 1)
                    for c in range(TOP):
                        pool.indirect_dma_start(
                            out=rows[c][t % DEPTH][:], out_offset=None, in_=eo_dram,
                            in_offset=bass.IndirectOffsetOnAxis(ap=slots[:, c, t:t + 1], axis=0)
                        ).then_inc(gathered[t % DEPTH], 16)

            @block.sync
            def _(sp):
                for b in range(blocks):
                    if b >= 2:
                        sp.wait_ge(mixed, (b - 1) * TPB)
                    sp.dma_start(x_sb[b % 2][:], x_b[b]).then_inc(x_loaded[b % 2], 16)
                    if b >= 1:
                        sp.wait_ge(mixed, b * TPB)
                        sp.dma_start(out_b[b - 1], out_sb[(b - 1) % 2][:]).then_inc(stored[(b - 1) % 2], 16)
                sp.wait_ge(mixed, NT)
                sp.dma_start(out_b[blocks - 1], out_sb[(blocks - 1) % 2][:]).then_inc(
                    stored[(blocks - 1) % 2], 16)
                for z in range(2):
                    sp.wait_ge(stored[z], 16 * blocks // 2)

            @block.vector
            def _(dv):
                for t in range(NT):
                    b, j = t // TPB, t % TPB
                    dv.wait_ge(gathered[t % DEPTH], 16 * TOP * (t // DEPTH + 1))
                    if j == 0:
                        dv.wait_ge(x_loaded[b % 2], 16 * (b // 2 + 1))
                        if b >= 2:
                            dv.wait_ge(stored[b % 2], 16 * (b // 2))
                    dv.scalar_tensor_tensor(half[:, t % 2, :], rows[0][t % DEPTH][:], gates[:, 0, t:t + 1],
                                            x_sb[b % 2][:, j, :], ALU.mult, ALU.add).then_inc(half_ready, 1)
                    dv.wait_ge(half_ready, t + 1)
                    dv.scalar_tensor_tensor(out_sb[b % 2][:, j, :], rows[1][t % DEPTH][:],
                                            gates[:, 1, t:t + 1], half[:, t % 2, :], ALU.mult, ALU.add
                                            ).then_inc(mixed, 1)


def build(nc, a, out):
    def scratch(name, shape, dt):
        return nc.dram_tensor("dram_" + name, shape, dt, kind="Internal").ap()

    q1 = scratch("sa_qk_parts", (PARTS, 2 * D, N), BF16)
    v1 = scratch("sa_v", (N, HEADS * VW), F32)
    k2 = scratch("ca_k_parts", (PARTS, D, BATCH * CTX), BF16)
    v2 = scratch("ca_v", (BATCH * CTX, HEADS * VW), F32)
    q2 = scratch("ca_q_parts", (PARTS, D, N), BF16)
    o1 = scratch("sa_o", (2, D, N), F32)
    o2 = scratch("ca_o", (2, D, N), F32)
    x1 = scratch("x1", (N, D), F32)
    x2 = scratch("x2", (N, D), F32)
    xs = scratch("slot_rows", (SLOTS, D), F32)
    eo = scratch("slot_outputs", (SLOTS, D), F32)
    ident = a["ident"]

    tokens_phase(nc, "kv", a["ctx"], CTX, 1, ln_g=a["ca_kv_ln_g"], ln_b=a["ca_kv_ln_b"], ident_dram=ident,
                 qk=(a["ca_wk"], a["ca_bk"], k2), v=(a["ca_wv"], a["ca_bv"], v2))
    tokens_phase(nc, "qkv", a["x"], P, N // (TPB * P), ln_g=a["sa_ln_g"], ln_b=a["sa_ln_b"],
                 ident_dram=ident, qk=(a["sa_wqk"], a["sa_bqk"], q1), v=(a["sa_wv"], a["sa_bv"], v1))
    attention_phase(nc, "sa", q1[:, 0:D, :], q1[:, D:2 * D, :], v1, o1, ident, keys=SEQ, key_tiles=SEQ // P)
    tokens_phase(nc, "mid", a["x"], P, N // (TPB * P), ln_g=a["ca_q_ln_g"], ln_b=a["ca_q_ln_b"],
                 ident_dram=ident, attn=(o1, a["sa_wo"], a["sa_bo"], x1), qk=(a["ca_wq"], a["ca_bq"], q2))
    attention_phase(nc, "ca", q2, k2, v2, o2, ident, keys=CTX, key_tiles=1)
    with ExitStack() as ctx:
        gates = ctx.enter_context(nc.sbuf_tensor("gates", [P, TOP, NT], F32))
        slots = ctx.enter_context(nc.sbuf_tensor("slots", [P, TOP, NT], I32))
        tile_expert = ctx.enter_context(nc.sbuf_tensor("tile_expert", [1, SLOT_TILES], I32))
        with (nc.sbuf_tensor("logits", [P, NT, E], F32) as logits,
              nc.sbuf_tensor("xhat_all", [P, NT, D], F32) as xhat_all):
            tokens_phase(nc, "last", x1, P, N // (TPB * P), ln_g=a["moe_ln_g"], ln_b=a["moe_ln_b"],
                         ident_dram=ident, attn=(o2, a["ca_wo"], a["ca_bo"], x2),
                         router=(a["w_r"], a["b_r"], logits, xhat_all))
            route_phase(nc, logits, xhat_all, gates, slots, tile_expert, xs, a)
        with ExitStack() as wctx:
            w_parts = [[wctx.enter_context(nc.sbuf_tensor(f"w{w + 1}_{part}", [P, E, DC * F], F16))
                        for part in ("high", "low")] for w in range(2)]
            weights_phase(nc, a["w1"], a["w2"], w_parts)
            expert_phase(nc, xs, eo, tile_expert, w_parts, a["b1"], a["b2"], a["moe_ln_g"], a["moe_ln_b"],
                         ident)
        combine_phase(nc, x2, eo, gates, slots, out)


def laid_out(inputs):
    a = {n.removeprefix("L0_xattn_"): np.asarray(v) for n, v in inputs.items()}

    def column(v):
        return v.reshape(-1, P).T
    out = {"x": a["x"].reshape(N, D), "ctx": a["ctx_1024"].reshape(BATCH * CTX, D)}
    for n in ("sa_ln_g", "sa_ln_b", "ca_q_ln_g", "ca_q_ln_b", "ca_kv_ln_g", "ca_kv_ln_b", "moe_ln_g", "moe_ln_b"):
        out[n] = column(a[n])
    out["sa_wqk"], out["sa_bqk"] = a["sa_in_w"][:2 * D].T, column(a["sa_in_b"][:2 * D])
    out["ca_wq"], out["ca_bq"] = a["ca_in_w"][:D].T, column(a["ca_in_b"][:D])
    out["ca_wk"], out["ca_bk"] = a["ca_in_w"][D:2 * D].T, column(a["ca_in_b"][D:2 * D])
    for n in ("sa", "ca"):
        out[n + "_wv"], out[n + "_bv"] = a[n + "_in_w"][2 * D:].T, a[n + "_in_b"][2 * D:]
        out[n + "_wo"], out[n + "_bo"] = a[n + "_out_w"].T, a[n + "_out_b"]
    out["w_r"], out["b_r"] = a["router_w"].T, a["router_b"]
    out["w1"], out["w2"] = a["e_fc1_w"].transpose(0, 2, 1), a["e_fc2_w"].transpose(0, 2, 1)
    out["b1"], out["b2"] = a["e_fc1_b"].reshape(E, FC, P).transpose(0, 2, 1), a["e_fc2_b"]
    return out


def constants():
    return {
        "ident": np.eye(P, dtype=np.float32),
        "rev": np.tile(np.arange(E, 0, -1, dtype=np.float32), (P, 1)),
        "tri": np.triu(np.ones((P, P), np.float32), 1),
        "ones": np.ones((P, P), np.float32),
        "tile_no": np.arange(SLOT_TILES, dtype=np.float32)[None, :],
    }


def kernel(**inputs):
    import concourse.bacc as bacc
    from concourse.bass_utils import run_bass_kernel_spmd

    nc = bacc.Bacc("TRN2", target_bir_lowering=False, num_devices=1)
    arrays, aps = {}, {}
    for name, value in (laid_out(inputs) | constants()).items():
        value = np.ascontiguousarray(value)
        arrays[f"in_{name}"] = value
        aps[name] = nc.dram_tensor(f"in_{name}", value.shape, mybir.dt.from_np(value.dtype),
                                   kind="ExternalInput").ap()
    out = nc.dram_tensor("out", (N, D), F32, kind="ExternalOutput").ap()
    build(nc, aps, out)
    got = run_bass_kernel_spmd(nc, [arrays], core_ids=[0])
    return got.results[0]["out"].reshape(BATCH, SEQ, D)
```

```python
from contextlib import ExitStack

import numpy as np

import concourse.bass as bass
from concourse import mybir

F32 = mybir.dt.float32
BF16 = mybir.dt.bfloat16
F16 = mybir.dt.float16
I32 = mybir.dt.int32
ALU = mybir.AluOpType
ACT = mybir.ActivationFunctionType
AX_X = mybir.AxisListType.X

P = 128
D = 256
DC = D // P
HEADS = 16
DH = D // HEADS
BATCH = 4
SEQ = 1024
CTX = 77
N = BATCH * SEQ
NT = N // P
E = 8
TOP = 2
F = 1024
FC = F // P
EPS = 1e-5
TPB = 4
HG = 4
GROUPS = BATCH * HEADS // HG
VW = 2 * DH
PARTS = 3
Q_STACK = [0, 0, 0, 1, 1, 2]
K_STACK = [0, 1, 2, 0, 1, 0]
SR = len(Q_STACK) * DH
SLOT_TILES = TOP * NT + E
SLOTS = SLOT_TILES * P
W_SCALE = 64.0
BIG = 3.0e38


def tokens_phase(nc, name, x_dram, rows, blocks, *, ln_g, ln_b, ident_dram,
                 attn=None, qk=None, v=None, router=None):
    W = TPB * rows
    qk_chunks = qk[0].shape[1] // P if qk else 0
    with ExitStack() as ctx:
        def sb(n, shape, dt):
            return ctx.enter_context(nc.sbuf_tensor(f"{name}_{n}", shape, dt))

        def ps(n, shape):
            return ctx.enter_context(nc.psum_tensor(f"{name}_{n}", shape, F32))

        def sem(n):
            return ctx.enter_context(nc.semaphore(f"{name}_{n}"))

        ident = sb("ident", [P, P], F32)
        g_col = sb("g_col", [P, DC], F32)
        b_col = sb("b_col", [P, DC], F32)
        x_sb = sb("x", [rows, TPB, D], F32)
        stats = sb("stats", [rows, TPB, 6], F32)
        mean2 = sb("mean2", [rows, TPB], F32)
        diff = sb("diff", [rows, TPB], F32)
        m2 = sb("m2", [rows, TPB], F32)
        mean = sb("mean", [rows, TPB], F32)
        dd = sb("dd", [rows, TPB], F32)
        var_sum = sb("var_sum", [rows, TPB], F32)
        var = sb("var", [rows, TPB], F32)
        std = sb("std", [rows, TPB], F32)
        r0 = sb("r0", [rows, TPB], F32)
        r0sq = sb("r0sq", [rows, TPB], F32)
        newton = sb("newton", [rows, TPB], F32)
        newton2 = sb("newton2", [rows, TPB], F32)
        rstd = sb("rstd", [rows, TPB], F32)
        xhat = sb("xhat", [rows, TPB, D], F32)
        xT = sb("xT", [P, DC, W], F32)
        psT = ps("psT", [P, DC, 512])
        consts = sem("consts")
        x_loaded = sem("x_loaded")
        x_used = sem("x_used")
        dve = sem("dve")
        std_ready = sem("std_ready")
        xhat_ready = sem("xhat_ready")
        transposed = sem("transposed")
        xT_ready = sem("xT_ready")
        stored = sem("stored")
        n_consts = 3
        if attn:
            o_dram, w_out_t, b_out, x_out = attn
            oT = sb("oT", [P, DC, W], F32)
            sT = sb("sT", [P, DC, W], F32)
            rT = sb("rT", [P, DC, W], F32)
            onT = sb("onT", [P, DC, W], F32)
            wo = sb("wo", [P, DC, D], F32)
            bo = sb("bo", [rows, D], F32)
            xb = sb("xb", [rows, TPB, D], F32)
            x1 = sb("x1", [rows, TPB, D], F32)
            psY = ps("psY", [rows, TPB, D])
            o_loaded = sem("o_loaded")
            on_ready = sem("on_ready")
            projected = sem("projected")
            x1_ready = sem("x1_ready")
            x1_stored = sem("x1_stored")
            n_consts += 2
        x_ln = x1 if attn else x_sb
        if qk:
            w_qk = sb("w_qk", [P, DC, qk_chunks * P], F32)
            b_qk = sb("b_qk", [P, qk_chunks], F32)
            qf = sb("qf", [P, qk_chunks, W], F32)
            rest = sb("rest", [P, qk_chunks, W], F32)
            part = [sb(f"part{i}", [P, qk_chunks, W], BF16) for i in range(PARTS)]
            psQK = ps("psQK", [P, 2, 512])
            qk_done = sem("qk_done")
            qf_ready = sem("qf_ready")
            parts_ready = sem("parts_ready")
            parts_stored = sem("parts_stored")
            n_consts += 2
        if v:
            w_v = sb("w_v", [P, DC, D], F32)
            b_v = sb("b_v", [rows, D], F32)
            v_sb = sb("v_sb", [rows, TPB, HEADS, VW], F32)
            psV = ps("psV", [rows, TPB, D])
            v_done = sem("v_done")
            v_ones = sem("v_ones")
            v_ready = sem("v_ready")
            n_consts += 2
        if router:
            w_r = sb("w_r", [P, DC, E], F32)
            b_r = sb("b_r", [rows, E], F32)
            psL = ps("psL", [rows, TPB, E])
            logits_done = sem("logits_done")
            logits_ready = sem("logits_ready")
            n_consts += 2
        n_stores = (1 if v else 0) + (1 if router else 0)
        LN_OPS = TPB + 12
        SPLIT_OPS = 1 if qk else 0
        N_ATT = 1 if attn else 0
        N_DVE = N_ATT + LN_OPS + SPLIT_OPS

        def loop(eng, body):
            if blocks == 1:
                body(0)
            else:
                with eng.Fori(0, blocks) as blk:
                    body(blk)

        x_rows = x_dram.rearrange("(b t p) d -> b p t d", p=rows, t=TPB)
        with nc.Block() as block:

            @block.sync
            def _(sp):
                sp.dma_start(ident[:], ident_dram).then_inc(consts, 16)
                sp.dma_start(g_col[:], ln_g).then_inc(consts, 16)
                sp.dma_start(b_col[:], ln_b).then_inc(consts, 16)

                def wide(dst, vec):
                    sp.dma_start(dst, vec.rearrange("(a n) -> a n", a=1).broadcast_to(
                        [rows, vec.shape[0]])).then_inc(consts, 16)
                if attn:
                    sp.dma_start(wo[:], w_out_t.rearrange("(c p) n -> p c n", p=P)).then_inc(consts, 16)
                    wide(bo[:], b_out)
                if qk:
                    sp.dma_start(w_qk[:], qk[0].rearrange("(c p) n -> p c n", p=P)).then_inc(consts, 16)
                    sp.dma_start(b_qk[:], qk[1]).then_inc(consts, 16)
                if v:
                    sp.dma_start(w_v[:], v[0].rearrange("(c p) n -> p c n", p=P)).then_inc(consts, 16)
                    wide(b_v[:], v[1])
                if router:
                    sp.dma_start(w_r[:], router[0].rearrange("(c p) n -> p c n", p=P)).then_inc(consts, 16)
                    wide(b_r[:], router[1])

                def body(blk):
                    if attn:
                        sp.wait_ge(x_used, blk)
                    else:
                        sp.wait_ge(xhat_ready, blk * TPB)
                    sp.dma_start(x_sb[:], x_rows[bass.ds(blk, 1)].rearrange("b p t d -> p (b t) d")
                                 ).then_inc(x_loaded, 16)
                    if attn:
                        for dst, which in ((oT, 0), (sT, 1)):
                            sp.dma_start(dst[:], o_dram[which].rearrange("(c p) n -> p c n", p=P)[
                                :, :, bass.ds(blk * W, W)]).then_inc(o_loaded, 16)
                        sp.wait_ge(x1_ready, blk + 1)
                        sp.dma_start(x_out.rearrange("(b t p) d -> b p t d", p=rows, t=TPB)[
                            bass.ds(blk, 1)].rearrange("b p t d -> p (b t) d"), x1[:]).then_inc(x1_stored, 16)
                    if router:
                        sp.wait_ge(xhat_ready, blk * TPB + TPB)
                        sp.dma_start(router[3][:, bass.ds(blk * TPB, TPB), :], xhat[:]).then_inc(stored, 16)
                    if v:
                        sp.wait_ge(v_ready, blk * TPB + TPB)
                        sp.dma_start(v[2].rearrange("(b t p) n -> b p t n", p=rows, t=TPB)[
                            bass.ds(blk, 1)].rearrange("b p t n -> p (b t) n"),
                            v_sb[:].rearrange("p t h w -> p t (h w)")).then_inc(stored, 16)
                loop(sp, body)
                if n_stores:
                    sp.wait_ge(stored, 16 * n_stores * blocks)
                if attn:
                    sp.wait_ge(x1_stored, 16 * blocks)

            @block.gpsimd
            def _(pool):
                if v:
                    pool.memset(v_sb[:], 1.0).then_inc(v_ones, 1)

                def body(blk):
                    for i in range(PARTS):
                        pool.wait_ge(parts_ready, blk * PARTS + i + 1)
                        pool.dma_start(qk[2][i].rearrange("(c p) n -> p c n", p=P)[
                            :, :, bass.ds(blk * W, W)], part[i][:]).then_inc(parts_stored, 16)
                if qk:
                    loop(pool, body)
                    pool.wait_ge(parts_stored, 16 * PARTS * blocks)

            @block.vector
            def _(dv):
                dv.wait_ge(consts, 16 * n_consts)
                if v:
                    dv.wait_ge(v_ones, 1)

                def body(blk):
                    k = 0

                    def step(ins):
                        nonlocal k
                        k += 1
                        return ins.then_inc(dve, 1)

                    def own():
                        dv.wait_ge(dve, blk * N_DVE + k)
                    if attn:
                        dv.wait_ge(projected, blk)
                        dv.wait_ge(o_loaded, blk * 32 + 32)
                        step(dv.reciprocal(rT[:], sT[:]))
                        own()
                        dv.tensor_tensor(onT[:], oT[:], rT[:], ALU.mult).then_inc(on_ready, 1)
                        dv.wait_ge(x_loaded, blk * 16 + 16)
                        dv.tensor_tensor(xb[:], x_sb[:], bo[:, None, :].broadcast_to([rows, TPB, D]),
                                         ALU.add).then_inc(x_used, 1)
                        dv.wait_ge(x_used, blk + 1)
                        dv.wait_ge(x1_stored, blk * 16)
                        dv.wait_ge(projected, blk + 1)
                        dv.tensor_tensor(x1[:], psY[:], xb[:], ALU.add).then_inc(x1_ready, 1)
                        dv.wait_ge(x1_ready, blk + 1)
                    else:
                        dv.wait_ge(x_loaded, blk * 16 + 16)
                    for t in range(TPB):
                        step(dv.bn_stats(stats[:, t, :], x_ln[:, t, :]))
                    own()
                    step(dv.tensor_tensor(mean2[:], stats[:, :, 1], stats[:, :, 4], ALU.add))
                    step(dv.tensor_tensor(diff[:], stats[:, :, 1], stats[:, :, 4], ALU.subtract))
                    step(dv.tensor_tensor(m2[:], stats[:, :, 2], stats[:, :, 5], ALU.add))
                    own()
                    step(dv.tensor_scalar(mean[:], mean2[:], 0.5, None, ALU.mult))
                    step(dv.scalar_tensor_tensor(dd[:], diff[:], D / 4, diff[:], ALU.mult, ALU.mult))
                    own()
                    step(dv.tensor_tensor(var_sum[:], dd[:], m2[:], ALU.add))
                    own()
                    step(dv.tensor_scalar(var[:], var_sum[:], 1.0 / D, EPS, ALU.mult, ALU.add))
                    dv.wait_ge(std_ready, blk + 1)
                    step(dv.reciprocal(r0[:], std[:]))
                    own()
                    step(dv.tensor_tensor(r0sq[:], r0[:], r0[:], ALU.mult))
                    own()
                    step(dv.tensor_tensor(newton[:], r0sq[:], var[:], ALU.mult))
                    own()
                    step(dv.tensor_scalar(newton2[:], newton[:], -0.5, 1.5, ALU.mult, ALU.add))
                    own()
                    step(dv.tensor_tensor(rstd[:], newton2[:], r0[:], ALU.mult))
                    own()
                    dv.wait_ge(transposed, blk)
                    if router:
                        dv.wait_ge(stored, blk * 16)
                    for t in range(TPB):
                        dv.tensor_scalar(xhat[:, t, :], x_ln[:, t, :], mean[:, t:t + 1],
                                         rstd[:, t:t + 1], ALU.subtract, ALU.mult).then_inc(xhat_ready, 1)
                    if v:
                        dv.wait_ge(v_done, blk + 1)
                        dv.wait_ge(stored, blk * 16 * n_stores)
                        for t in range(TPB):
                            dv.tensor_tensor(
                                v_sb[:, t, :, 0:DH], psV[:, t, :].rearrange("p (h w) -> p h w", h=HEADS),
                                b_v[:].rearrange("p (h w) -> p h w", h=HEADS), ALU.add).then_inc(v_ready, 1)
                    if qk:
                        dv.wait_ge(parts_stored, blk * 16 * PARTS)
                        dv.wait_ge(qf_ready, blk * qk_chunks + qk_chunks)
                        dv.tensor_copy(part[0][:], qf[:]).then_inc(parts_ready, 1)
                        dv.wait_ge(parts_ready, blk * PARTS + 1)
                        step(dv.tensor_tensor(rest[:], qf[:], part[0][:], ALU.subtract))
                        own()
                        dv.tensor_copy(part[1][:], rest[:]).then_inc(parts_ready, 1)
                        dv.wait_ge(parts_ready, blk * PARTS + 2)
                        dv.tensor_tensor(part[2][:], rest[:], part[1][:], ALU.subtract
                                         ).then_inc(parts_ready, 1)
                    if router:
                        dv.wait_ge(logits_done, blk + 1)
                        dv.tensor_tensor(router[2][:, bass.ds(blk * TPB, TPB), :], psL[:],
                                         b_r[:, None, :].broadcast_to([rows, TPB, E]), ALU.add
                                         ).then_inc(logits_ready, 1)
                    assert k == N_DVE, (k, N_DVE)
                loop(dv, body)

            VAR_AT = N_ATT + TPB + 7

            @block.scalar
            def _(act):
                act.wait_ge(consts, 16 * n_consts)

                def body(blk):
                    act.wait_ge(dve, blk * N_DVE + VAR_AT)
                    act.activation(std[:], var[:], ACT.Sqrt).then_inc(std_ready, 1)
                    act.wait_ge(transposed, blk + 1)
                    if v:
                        act.wait_ge(v_done, blk)
                    if qk:
                        act.wait_ge(qk_done, blk * qk_chunks)
                    if router:
                        act.wait_ge(logits_done, blk)
                    for c in range(DC):
                        act.activation(xT[:, c, :], psT[:, c, 0:W], ACT.Identity, bias=b_col[:, c:c + 1],
                                       scale=g_col[:, c:c + 1]).then_inc(xT_ready, 1)
                    for s in range(qk_chunks):
                        if s == 0:
                            act.wait_ge(parts_ready, blk * PARTS)
                        act.wait_ge(qk_done, blk * qk_chunks + s + 1)
                        act.activation(qf[:, s, :], psQK[:, s % 2, 0:W], ACT.Identity,
                                       bias=b_qk[:, s:s + 1]).then_inc(qf_ready, 1)
                loop(act, body)

            @block.tensor
            def _(pe):
                pe.wait_ge(consts, 16 * n_consts)

                def body(blk):
                    if attn:
                        pe.wait_ge(x1_ready, blk)
                        pe.wait_ge(on_ready, blk + 1)
                        for t in range(TPB):
                            for c in range(DC):
                                mm = pe.matmul(psY[:, t, :], onT[:, c, t * rows:(t + 1) * rows], wo[:, c, :],
                                               start=(c == 0), stop=(c == DC - 1))
                        mm.then_inc(projected, 1)
                    pe.wait_ge(xT_ready, blk * DC)
                    for t in range(TPB):
                        pe.wait_ge(xhat_ready, blk * TPB + t + 1)
                        for c in range(DC):
                            mm = pe.transpose(psT[:, c, t * rows:(t + 1) * rows],
                                              xhat[:, t, c * P:(c + 1) * P], ident[0:rows, 0:rows])
                    mm.then_inc(transposed, 1)
                    pe.wait_ge(xT_ready, blk * DC + DC)
                    for s in range(qk_chunks):
                        pe.wait_ge(qf_ready, blk * qk_chunks + max(s - 1, 0))
                        for c in range(DC):
                            mm = pe.matmul(psQK[:, s % 2, 0:W], w_qk[:, c, s * P:(s + 1) * P], xT[:, c, :],
                                           start=(c == 0), stop=(c == DC - 1))
                        mm.then_inc(qk_done, 1)
                    if v:
                        pe.wait_ge(v_ready, blk * TPB)
                        for t in range(TPB):
                            for c in range(DC):
                                mm = pe.matmul(psV[:, t, :], xT[:, c, t * rows:(t + 1) * rows], w_v[:, c, :],
                                               start=(c == 0), stop=(c == DC - 1))
                        mm.then_inc(v_done, 1)
                    if router:
                        pe.wait_ge(logits_ready, blk)
                        for t in range(TPB):
                            for c in range(DC):
                                mm = pe.matmul(psL[:, t, :], xT[:, c, t * rows:(t + 1) * rows], w_r[:, c, :],
                                               start=(c == 0), stop=(c == DC - 1))
                        mm.then_inc(logits_done, 1)
                loop(pe, body)


def attention_phase(nc, name, q_parts, k_parts, v_dram, o_dram, ident_dram, *, keys, key_tiles,
                    clear_dram=None):
    kp = keys // key_tiles
    q_tiles = SEQ // P
    HALF = SEQ // 2
    batches = key_tiles * 2
    steps = batches * HG
    fills = steps // 2
    entries = 1 if key_tiles > 1 else 2
    groups = entries * HEADS // HG
    bodies = BATCH // entries
    loads_heads = HG if key_tiles > 1 else HEADS
    slots = groups * HG // loads_heads
    row_lead = 6
    lead = fills + row_lead
    fill_tiles = HG * q_tiles // fills
    PSLOTS = 4
    assert fills % 2 == 0 and fill_tiles * keys <= SEQ
    own_sems = []
    with ExitStack() as ctx:
        def sb(n, shape, dt):
            return ctx.enter_context(nc.sbuf_tensor(f"{name}_{n}", shape, dt))

        def ps(n, shape):
            return ctx.enter_context(nc.psum_tensor(f"{name}_{n}", shape, F32))

        def sem(n):
            own_sems.append(nc.alloc_semaphore(f"{name}_{n}"))
            return own_sems[-1]

        def sems(n, count=2):
            return [sem(f"{n}{z}") for z in range(count)]

        ident = sb("ident", [P, P], F32)
        q_st = [sb(f"q{u}", [SR + 1, loads_heads, SEQ], BF16) for u in range(slots)]
        k_st = [sb(f"k{u}", [SR + 1, loads_heads, keys], BF16) for u in range(slots)]
        v_st = [sb(f"v{u}", [kp, key_tiles, loads_heads * VW], F32) for u in range(slots)]
        maxs = [sb(f"maxs{z}", [P, HG * q_tiles], F32) for z in range(2)]
        max_row = [sb(f"max_row{z}", [HG * q_tiles, P], BF16) for z in range(2)]
        probs = [[sb(f"p{z}_{h}", [kp, HALF], F32) for h in range(HG)] for z in range(PSLOTS)]
        o_sb = [sb(f"o{e}", [P, HEADS // HG, SEQ], F32) for e in range(entries)]
        ps_s = [ps(f"pss{z}", [kp, HALF]) for z in range(2)]
        ps_m = [ps(f"psm{z}", [P, 2, 512]) for z in range(2)]
        ps_o = [ps(f"pso{half}", [P, HALF]) for half in range(2)]

        consts = sem("consts")
        ones = sem("ones")
        loaded = sems("loaded", slots)
        filled = sem("filled")
        taken = sems("taken")
        turned = sem("turned")
        row_ready = sem("row_ready")
        row_placed = sems("row_placed")
        scored = sem("scored")
        exps = sems("exps")
        weighted = sems("weighted", PSLOTS)
        o_taken = sems("o_taken")
        stored = sems("stored", entries)
        if clear_dram is not None:
            zeros = sb("zeros", [P, D], F32)
            zeros_ready = sem("zeros_ready")
            cleared = sem("cleared")
            clear_parts = clear_dram.rearrange("(i p t) d -> i p t d", i=bodies, p=P)

        LOADS = 16 * (2 * len(Q_STACK) + 1)
        STORES = 16 * 2 * HG
        G_BATCHES = groups * batches

        def count(body, n, per_body, turns):
            assert per_body % turns == 0
            return body * (per_body // turns) + n // turns

        def home(G):
            at = G * HG // loads_heads
            return at % slots, G * HG % loads_heads

        def loop(eng, body):
            if bodies > 2:
                with eng.Fori(0, bodies - 1) as i:
                    body(i, False)
            else:
                for i in range(bodies - 1):
                    body(i, False)
            body(bodies - 1, True)

        with nc.Block() as block:

            @block.sync
            def _(sp):
                sp.dma_start(ident[:], ident_dram).then_inc(consts, 16)

                def load(b, hg, u):
                    for s in range(len(Q_STACK)):
                        for st, parts, stack, width in ((q_st, q_parts, Q_STACK, SEQ),
                                                        (k_st, k_parts, K_STACK, keys)):
                            rows = parts[stack[s]][hg * HG * DH:(hg * HG + loads_heads) * DH,
                                                   bass.ds(b * width, width)]
                            sp.dma_start(st[u][s * DH:(s + 1) * DH, :, :],
                                         rows.rearrange("(h d) n -> d h n", d=DH)).then_inc(loaded[u], 16)
                    sp.dma_start(
                        v_st[u][:], v_dram.rearrange("(b t p) n -> b p t n", t=key_tiles, p=kp)[
                            bass.ds(b, 1), :, :, hg * HG * VW:(hg * HG + loads_heads) * VW].rearrange(
                                "b p t n -> p (b t) n")).then_inc(loaded[u], 16)

                def place_row(body, G):
                    u, h0 = home(G)
                    sp.wait_ge(row_ready, body * groups + G + 1)
                    sp.dma_start(q_st[u][SR:SR + 1, h0:h0 + HG, :].rearrange("a h n -> a (h n)"),
                                 max_row[G % 2][:]).then_inc(row_placed[G % 2], 16)

                groups_per_load = loads_heads // HG
                for u in range(slots):
                    load(u * groups_per_load // (HEADS // HG), u * groups_per_load % (HEADS // HG), u)
                ahead = lead // fills
                for G in range(ahead):
                    place_row(0, G)

                def body(i, last):
                    if clear_dram is not None:
                        sp.dma_start(clear_parts[bass.ds(i, 1)].rearrange("i p t d -> p (i t) d"),
                                     zeros[:, None, :].broadcast_to([P, clear_parts.shape[2], D])
                                     ).then_inc(cleared, 16)
                    for G in range(groups):
                        if not last or G + ahead < groups:
                            place_row(i, G + ahead)
                        if not last and (G + 1) % groups_per_load == 0:
                            n = (G + 1) * batches - 1
                            sp.wait_ge(weighted[n % PSLOTS], count(i, n, G_BATCHES, PSLOTS) + 1)
                            load(i * entries + entries + G // (HEADS // HG),
                                 (G + 1 - groups_per_load) % (HEADS // HG), home(G)[0])
                if clear_dram is not None:
                    sp.wait_ge(zeros_ready, 1)
                loop(sp, body)
                if clear_dram is not None:
                    sp.wait_ge(cleared, 16 * bodies)

            @block.gpsimd
            def _(pool):
                if clear_dram is not None:
                    pool.memset(zeros[:], 0.0).then_inc(zeros_ready, 1)
                    pool.wait_ge(zeros_ready, 1)
                for u in range(slots):
                    pool.memset(k_st[u][SR:SR + 1, :, :], 1.0).then_inc(ones, 1)
                with pool.Fori(0, bodies) as i:
                    for e in range(entries):
                        for half in range(2):
                            pool.wait_ge(o_taken[half], (i * entries + e + 1) * (HEADS // HG))
                        for h in range(HG):
                            for which in range(2):
                                pool.dma_start(
                                    o_dram[which].rearrange("(g h d) n -> d h g n", h=HG, d=DH)[
                                        :, h, :, bass.ds((i * entries + e) * SEQ, SEQ)],
                                    o_sb[e][h * VW + which * DH:h * VW + (which + 1) * DH, :, :]
                                ).then_inc(stored[e], 16)
                for e in range(entries):
                    pool.wait_ge(stored[e], STORES * bodies)

            @block.tensor
            def _(pe):
                pe.wait_ge(consts, 16)
                pe.wait_ge(ones, slots)

                def fill(body, n):
                    G, f = divmod(n, fills)
                    u, h0 = home(G)
                    if f == 0 and h0 == 0:
                        pe.wait_ge(loaded[u], (body + G // groups) * LOADS + LOADS)
                    if f == 1:
                        pe.wait_ge(row_ready, body * groups + G)
                    z = n % 2
                    pe.wait_ge(taken[z], count(body, n, groups * fills, 2))
                    for j in range(fill_tiles):
                        h, qt = divmod(f * fill_tiles + j, q_tiles)
                        lhs = q_st[u][0:SR, h0 + h, qt * P:(qt + 1) * P]
                        if key_tiles > 1:
                            for half in range(2):
                                mm = pe.matmul(ps_m[z][:, half, :], lhs,
                                               k_st[u][0:SR, h0 + h, half * HALF:(half + 1) * HALF],
                                               start=True, stop=True)
                        else:
                            bank, at = divmod(j, fill_tiles // 2)
                            mm = pe.matmul(ps_m[z][:, bank, at * keys:(at + 1) * keys], lhs,
                                           k_st[u][0:SR, h0 + h, :], start=True, stop=True)
                    mm.then_inc(filled, 1)

                def turn(body, G):
                    for n in ((G + 1) * fills - 2, (G + 1) * fills - 1):
                        pe.wait_ge(taken[n % 2], count(body, n, groups * fills, 2) + 1)
                    pe.transpose(ps_m[1][0:HG * q_tiles, 0, 0:P], maxs[G % 2][:], ident[:]
                                 ).then_inc(turned, 1)

                def advance(body, n, last):
                    if not last or n < groups * fills:
                        fill(body, n)
                    if n % fills == 0 and n > 0 and (not last or n <= groups * fills):
                        turn(body, n // fills - 1)

                def score(body, S):
                    G, s = divmod(S, steps)
                    u, h0 = home(G)
                    kt, half, h = s // (2 * HG), s // HG % 2, s % HG
                    if s == 0:
                        pe.wait_ge(row_placed[G % 2], count(body, G, groups, 2) * 16 + 16)
                    z = S % 2
                    pe.wait_ge(exps[z], count(body, S, groups * steps, 2))
                    pe.matmul(ps_s[z][:], k_st[u][:, h0 + h, kt * kp:(kt + 1) * kp],
                              q_st[u][:, h0 + h, half * HALF:(half + 1) * HALF],
                              start=True, stop=True).then_inc(scored, 1)

                def weigh(body, n):
                    G, bt = divmod(n, batches)
                    u, h0 = home(G)
                    kt, half = divmod(bt, 2)
                    if kt == 0:
                        pe.wait_ge(o_taken[half], body * groups + G)
                    for S in (n * HG + HG - 2, n * HG + HG - 1):
                        pe.wait_ge(exps[S % 2], count(body, S, groups * steps, 2) + 1)
                    for h in range(HG):
                        mm = pe.matmul(ps_o[half][h * VW:(h + 1) * VW, :],
                                       v_st[u][:, kt, (h0 + h) * VW:(h0 + h + 1) * VW],
                                       probs[n % PSLOTS][h][:], start=(kt == 0), stop=(kt == key_tiles - 1))
                    mm.then_inc(weighted[n % PSLOTS], 1)

                for n in range(lead):
                    advance(0, n, False)

                def body(i, last):
                    for S in range(groups * steps):
                        score(i, S)
                        if S % 2 == 0:
                            advance(i, S // 2 + lead, last)
                        if S % HG == 1 and S > HG:
                            weigh(i, S // HG - 1)
                    weigh(i, G_BATCHES - 1)
                loop(pe, body)

            @block.scalar
            def _(act):
                act.preload_act_table(ACT.Exp)

                def evacuate(body, G, half):
                    n = G * batches + batches - 2 + half
                    e, hg = divmod(G, HEADS // HG)
                    act.wait_ge(stored[e], body * STORES)
                    act.wait_ge(weighted[n % PSLOTS], count(body, n, G_BATCHES, PSLOTS) + 1)
                    act.activation(o_sb[e][:, hg, half * HALF:(half + 1) * HALF], ps_o[half][:], ACT.Copy
                                   ).then_inc(o_taken[half], 1)

                def body(i, last):
                    for S in range(groups * steps):
                        n, h = divmod(S, HG)
                        if h == 0:
                            act.wait_ge(weighted[n % PSLOTS], count(i, n, G_BATCHES, PSLOTS))
                        act.wait_ge(scored, i * (groups * steps) + S + 1)
                        act.activation(probs[n % PSLOTS][h][:], ps_s[S % 2][:], ACT.Exp,
                                       scale=float(DH) ** -0.5).then_inc(exps[S % 2], 1)
                        G, s = divmod(S, steps)
                        if s == steps - 1:
                            evacuate(i, G, 0)
                        if s == HG - 1 and G > 0:
                            evacuate(i, G - 1, 1)
                    evacuate(i, groups - 1, 1)
                loop(act, body)

            @block.vector
            def _(dv):
                def take(body, n):
                    G, f = divmod(n, fills)
                    z = n % 2
                    dv.wait_ge(filled, body * (groups * fills) + n + 1)
                    if key_tiles > 1:
                        dv.tensor_reduce(maxs[G % 2][:, f:f + 1], ps_m[z][:].rearrange("p b k -> p (b k)"),
                                         AX_X, ALU.max).then_inc(taken[z], 1)
                    else:
                        half = fill_tiles // 2
                        dv.tensor_reduce(
                            maxs[G % 2][:, f * fill_tiles:(f + 1) * fill_tiles].rearrange(
                                "p (b t) -> p b t", b=2),
                            ps_m[z][:, :, 0:half * keys].rearrange("p b (t k) -> p b t k", k=keys),
                            AX_X, ALU.max).then_inc(taken[z], 1)

                def negate(body, G):
                    dv.wait_ge(turned, body * groups + G + 1)
                    dv.wait_ge(row_placed[G % 2], count(body, G, groups, 2) * 16)
                    dv.tensor_scalar(max_row[G % 2][:], ps_m[1][0:HG * q_tiles, 0, 0:P], -1.0, None,
                                     ALU.mult).then_inc(row_ready, 1)

                def advance(body, n, last):
                    if not last or n < groups * fills:
                        take(body, n)
                    if n % fills == 0 and n > 0 and (not last or n <= groups * fills):
                        negate(body, n // fills - 1)

                for n in range(lead):
                    advance(0, n, False)

                def body(i, last):
                    for S in range(0, groups * steps, 2):
                        advance(i, S // 2 + lead, last)
                loop(dv, body)

    nc.clear_and_free_semaphores(own_sems)
    nc.all_engine_barrier()


def route_phase(nc, logits, xhat_all, gates, slots, tile_expert, xs_dram, c_dram, w_drams, w_parts):
    with ExitStack() as ctx:
        def sb(n, shape, dt=F32):
            return ctx.enter_context(nc.sbuf_tensor(f"route_{n}", shape, dt))

        def sem(n):
            return ctx.enter_context(nc.semaphore(f"route_{n}"))

        TE = [P, NT, E]
        rev = sb("rev", [P, E])
        tri = sb("tri", [P, P])
        ones = sb("ones", [P, P])
        tile_no = sb("tile_no", [1, SLOT_TILES])
        zeros = sb("zeros", [P, NT])
        best = [sb(f"best{k}", [P, NT]) for k in range(TOP)]
        tie = sb("tie", TE)
        cand = sb("cand", TE)
        first = sb("first", [P, NT])
        sel = [sb(f"sel{k}", TE) for k in range(TOP)]
        others = sb("others", TE)
        chosen = sb("chosen", [P, NT * E])
        gap = sb("gap", [P, NT])
        gap_exp = sb("gap_exp", [P, NT])
        gap_sum = sb("gap_sum", [P, NT])
        totals = sb("totals", TE)
        upto = sb("upto", TE)
        before = sb("before", TE)
        padded = sb("padded", [P, E])
        padded_i = sb("padded_i", [P, E], I32)
        tiles_i = sb("tiles_i", [P, E], I32)
        tiles = sb("tiles", [P, E])
        tile_end = sb("tile_end", [P, E])
        tile_start = sb("tile_start", [P, E])
        slot_start = sb("slot_start", [P, E])
        place = sb("place", TE)
        place2 = sb("place2", TE)
        picked = [sb(f"picked{k}", TE) for k in range(TOP)]
        slot_f = sb("slot_f", [P, TOP, NT])
        past = sb("past", [1, SLOT_TILES, E])
        past_n = sb("past_n", [1, SLOT_TILES])
        past_c = sb("past_c", [1, SLOT_TILES])
        ps_rank = ctx.enter_context(nc.psum_tensor("route_rank", [P, 512], F32))
        ps_total = ctx.enter_context(nc.psum_tensor("route_total", [P, 512], F32))
        consts = sem("consts")
        zeroed = sem("zeroed")
        dve = sem("dve")
        counted = sem("counted")
        gap_ready = sem("gap_ready")
        chosen_ready = sem("chosen_ready")
        exp_ready = sem("exp_ready")
        slots_ready = sem("slots_ready")
        scattered = sem("scattered")

        PIECE = 1024
        STAGES = 3
        stage = [sb(f"stage{z}", [P, PIECE]) for z in range(STAGES)]
        w_loaded = [sem(f"w_loaded{z}") for z in range(STAGES)]
        high = sem("high")
        low = sem("low")
        pieces = [(e, w, at) for e in range(E) for w in range(2) for at in range(0, DC * F, PIECE)]

        def load_weights(sp):
            for n, (e, w, at) in enumerate(pieces):
                if n >= STAGES:
                    sp.wait_ge(low, n - STAGES + 1)
                rows = w_drams[w][e].rearrange("(c p) n -> p c n", p=P)
                width = rows.shape[2]
                sp.dma_start(stage[n % STAGES][:].rearrange("p (c n) -> p c n", n=width),
                             rows[:, at // width:(at + PIECE) // width, :]).then_inc(w_loaded[n % STAGES], 16)

        def cut_high(act):
            for n, (e, w, at) in enumerate(pieces):
                act.wait_ge(w_loaded[n % STAGES], 16 * (n // STAGES + 1))
                act.activation(w_parts[w][0][:, e, at:at + PIECE], stage[n % STAGES][:], ACT.Copy,
                               scale=W_SCALE).then_inc(high, 1)

        def cut_low(dv):
            for n, (e, w, at) in enumerate(pieces):
                dv.wait_ge(high, n + 1)
                dv.scalar_tensor_tensor(w_parts[w][1][:, e, at:at + PIECE], stage[n % STAGES][:], W_SCALE,
                                        w_parts[w][0][:, e, at:at + PIECE], ALU.mult, ALU.subtract
                                        ).then_inc(low, 1)

        def wide_e(ap):
            return ap[:, :, None].broadcast_to(TE)

        def wide_t(ap):
            return ap[:, None, :].broadcast_to(TE)

        with nc.Block() as block:

            @block.sync
            def _(sp):
                for dst, key in ((rev, "rev"), (tri, "tri"), (ones, "ones"), (tile_no, "tile_no")):
                    sp.dma_start(dst[:], c_dram[key]).then_inc(consts, 16)
                load_weights(sp)

            @block.scalar
            def _(act):
                act.wait_ge(gap_ready, 1)
                act.activation(gap_exp[:], gap[:], ACT.Exp).then_inc(exp_ready, 1)
                cut_high(act)

            @block.tensor
            def _(pe):
                pe.wait_ge(chosen_ready, 1)
                pe.matmul(ps_rank[:, 0:NT * E], tri[:], chosen[:], start=True, stop=True)
                pe.matmul(ps_total[:, 0:NT * E], ones[:], chosen[:], start=True, stop=True
                          ).then_inc(counted, 1)

            @block.vector
            def _(dv):
                k = 0

                def step(ins):
                    nonlocal k
                    k += 1
                    ins.then_inc(dve, 1)

                def own():
                    dv.wait_ge(dve, k)

                dv.memset(zeros[:], 0.0).then_inc(zeroed, 1)
                dv.wait_ge(zeroed, 1)
                dv.wait_ge(consts, 64)
                src = logits
                for c in range(TOP):
                    step(dv.tensor_reduce(best[c][:], src[:], AX_X, ALU.max))
                    own()
                    step(dv.tensor_tensor(tie[:], src[:], wide_e(best[c]), ALU.is_equal))
                    own()
                    step(dv.tensor_tensor(cand[:], tie[:], wide_t(rev), ALU.mult))
                    own()
                    step(dv.tensor_reduce(first[:], cand[:], AX_X, ALU.max))
                    own()
                    step(dv.tensor_tensor(sel[c][:], wide_t(rev), wide_e(first), ALU.is_equal))
                    own()
                    if c == 0:
                        step(dv.scalar_tensor_tensor(others[:], sel[0][:], -BIG, src[:], ALU.mult, ALU.add))
                        own()
                        src = others
                dv.tensor_tensor(gap[:], best[1][:], best[0][:], ALU.subtract).then_inc(gap_ready, 1)
                dv.tensor_tensor(chosen[:].rearrange("p (t e) -> p t e", e=E), sel[0][:], sel[1][:], ALU.add
                                 ).then_inc(chosen_ready, 1)
                dv.wait_ge(exp_ready, 1)
                step(dv.tensor_scalar(gap_sum[:], gap_exp[:], 1.0, None, ALU.add))
                own()
                step(dv.reciprocal(gates[:, 0, :], gap_sum[:]))
                own()
                step(dv.tensor_tensor(gates[:, 1, :], gates[:, 0, :], gap_exp[:], ALU.mult))
                dv.wait_ge(counted, 1)
                step(dv.tensor_copy(totals[:], ps_total[:, 0:NT * E].rearrange("p (t e) -> p t e", e=E)))
                own()
                for e in range(E):
                    step(dv.tensor_tensor_scan(upto[:, :, e], totals[:, :, e], zeros[:, 0:NT], 0.0,
                                               ALU.add, ALU.add))
                own()
                step(dv.tensor_tensor(before[:], upto[:], totals[:], ALU.subtract))
                step(dv.tensor_scalar(padded[:], upto[:, NT - 1, :], float(P - 1), None, ALU.add))
                own()
                step(dv.tensor_copy(padded_i[:], padded[:]))
                own()
                step(dv.tensor_scalar(tiles_i[:], padded_i[:], P.bit_length() - 1, None,
                                      ALU.logical_shift_right))
                own()
                step(dv.tensor_copy(tiles[:], tiles_i[:]))
                own()
                step(dv.tensor_tensor_scan(tile_end[:], tiles[:], zeros[:, 0:E], 0.0, ALU.add, ALU.add))
                own()
                step(dv.tensor_tensor(tile_start[:], tile_end[:], tiles[:], ALU.subtract))
                own()
                step(dv.tensor_scalar(slot_start[:], tile_start[:], float(P), None, ALU.mult))
                own()
                step(dv.tensor_tensor(place[:], ps_rank[:, 0:NT * E].rearrange("p (t e) -> p t e", e=E),
                                      before[:], ALU.add))
                own()
                step(dv.tensor_tensor(place2[:], place[:], wide_t(slot_start), ALU.add))
                own()
                for c in range(TOP):
                    step(dv.tensor_tensor(picked[c][:], sel[c][:], place2[:], ALU.mult))
                own()
                for c in range(TOP):
                    step(dv.tensor_reduce(slot_f[:, c, :], picked[c][:], AX_X, ALU.add))
                own()
                dv.tensor_copy(slots[:], slot_f[:]).then_inc(slots_ready, 1)
                step(dv.tensor_tensor(past[:], tile_no[:, :, None].broadcast_to([1, SLOT_TILES, E]),
                                      tile_end[0:1, None, :].broadcast_to([1, SLOT_TILES, E]), ALU.is_ge))
                own()
                step(dv.tensor_reduce(past_n[:], past[:], AX_X, ALU.add))
                own()
                step(dv.tensor_scalar(past_c[:], past_n[:], float(E - 1), None, ALU.min))
                own()
                step(dv.tensor_copy(tile_expert[:], past_c[:]))
                own()
                cut_low(dv)

            @block.gpsimd
            def _(pool):
                pool.wait_ge(slots_ready, 1)
                for t in range(NT):
                    for c in range(TOP):
                        pool.indirect_dma_start(
                            out=xs_dram, out_offset=bass.IndirectOffsetOnAxis(ap=slots[:, c, t:t + 1], axis=0),
                            in_=xhat_all[:, t, :], in_offset=None).then_inc(scattered, 16)
                pool.wait_ge(scattered, 16 * NT * TOP)


def expert_phase(nc, xs_dram, eo_dram, tile_expert, w_parts, b1_dram, b2_dram, ln_g, ln_b, ident_dram):
    (w1h, w1l), (w2h, w2l) = w_parts
    with ExitStack() as ctx:
        def sb(n, shape, dt=F32):
            return ctx.enter_context(nc.sbuf_tensor(f"moe_{n}", shape, dt))

        def two(n, shape, dt=F32):
            return [sb(f"{n}{u}", shape, dt) for u in range(2)]

        def ps(n, shape):
            return [ctx.enter_context(nc.psum_tensor(f"moe_{n}{u}", shape, F32)) for u in range(2)]

        def sem(n):
            return ctx.enter_context(nc.semaphore(f"moe_{n}"))

        def sems(n):
            return [sem(f"{n}{u}") for u in range(2)]

        ident = sb("ident", [P, P])
        g_col = sb("g_col", [P, DC])
        b_col = sb("b_col", [P, DC])
        xs = two("xs", [P, D])
        b1 = two("b1", [P, FC])
        b2 = two("b2", [P, D])
        hf = two("hf", [P, DC, P])
        hh = two("hh", [P, DC, P], F16)
        hl = two("hl", [P, DC, P], F16)
        h1 = two("h1", [P, FC, P])
        h1h = two("h1h", [P, FC, P], F16)
        h1l = two("h1l", [P, FC, P], F16)
        eo = two("eo", [P, D])
        ps_x = ps("psx", [P, 512])
        ps_h = ps("psh", [P, FC, P])
        ps_e = ps("pse", [P, 512])
        consts = sem("consts")
        xs_loaded = sems("xs_loaded")
        b1_loaded = sems("b1_loaded")
        b2_loaded = sems("b2_loaded")
        turned = sems("turned")
        hf_ready = sems("hf_ready")
        hh_ready = sems("hh_ready")
        h_ready = sems("h_ready")
        up = sems("up")
        gelus = sems("gelus")
        h1h_ready = sems("h1h_ready")
        h1_ready = sems("h1_ready")
        down = sems("down")
        eo_ready = sems("eo_ready")
        stored = sems("stored")

        T = SLOT_TILES
        xs_t = xs_dram.rearrange("(t p) d -> p t d", p=P)
        eo_t = eo_dram.rearrange("(t p) d -> p t d", p=P)
        with nc.Block() as block:

            @block.sync
            def _(sp):
                sp.dma_start(ident[:], ident_dram).then_inc(consts, 16)
                sp.dma_start(g_col[:], ln_g).then_inc(consts, 16)
                sp.dma_start(b_col[:], ln_b).then_inc(consts, 16)

                def expert_of(t):
                    return sp.value_load(tile_expert[0:1, bass.ds(t, 1)], min_val=0, max_val=E - 1)

                def load_rows(t, u):
                    sp.dma_start(xs[u][:], xs_t[:, bass.ds(t, 1), :].rearrange("p t d -> p (t d)")
                                 ).then_inc(xs_loaded[u], 16)

                def load_b1(e, u):
                    sp.dma_start(b1[u][:], b1_dram[bass.ds(e, 1)].rearrange("e p c -> p (e c)")
                                 ).then_inc(b1_loaded[u], 16)

                load_rows(0, 0)
                load_rows(1, 1)
                load_b1(expert_of(0), 0)

                def body(i, u, more2, more1):
                    if more2:
                        sp.wait_ge(turned[u], i + 1)
                        load_rows(2 * i + u + 2, u)
                    if more1:
                        e = expert_of(2 * i + u + 1)
                        sp.wait_ge(gelus[1 - u], (i + u) * FC)
                        load_b1(e, 1 - u)
                    e = expert_of(2 * i + u)
                    sp.wait_ge(eo_ready[u], i)
                    sp.dma_start(b2[u][:], b2_dram[bass.ds(e, 1), :].broadcast_to([P, D])
                                 ).then_inc(b2_loaded[u], 16)

                with sp.Fori(0, T // 2 - 1) as i:
                    body(i, 0, True, True)
                    body(i, 1, True, True)
                body(T // 2 - 1, 0, False, True)
                body(T // 2 - 1, 1, False, False)

            @block.gpsimd
            def _(pool):
                with pool.Fori(0, T // 2) as i:
                    for u in range(2):
                        pool.wait_ge(eo_ready[u], i + 1)
                        pool.dma_start(eo_t[:, bass.ds(2 * i + u, 1), :].rearrange("p t d -> p (t d)"),
                                       eo[u][:]).then_inc(stored[u], 16)
                for u in range(2):
                    pool.wait_ge(stored[u], 16 * T // 2)

            @block.tensor
            def _(pe):
                pe.wait_ge(consts, 48)

                def turn(i, u):
                    pe.wait_ge(hf_ready[u], i)
                    pe.wait_ge(xs_loaded[u], i * 16 + 16)
                    for c in range(DC):
                        mm = pe.transpose(ps_x[u][:, c * P:(c + 1) * P], xs[u][:, c * P:(c + 1) * P], ident[:])
                    mm.then_inc(turned[u], 1)

                def layer1(i, u, e):
                    for fc in range(FC):
                        for c in range(DC):
                            at = bass.ds(e * (DC * F) + (c * F + fc * P), P)
                            w_high = w1h[:].rearrange("p e n -> p (e n)")[:, at]
                            w_low = w1l[:].rearrange("p e n -> p (e n)")[:, at]
                            out = ps_h[u][:, fc, :]
                            pe.matmul(out, w_high, hh[u][:, c, :], start=(c == 0), stop=False)
                            pe.matmul(out, w_high, hl[u][:, c, :], start=False, stop=False)
                            mm = pe.matmul(out, w_low, hh[u][:, c, :], start=False, stop=(c == DC - 1))
                        if fc % (FC // 2) == FC // 2 - 1:
                            mm.then_inc(up[u], 1)

                def layer2(i, u, e):
                    pe.wait_ge(eo_ready[u], i)
                    pe.wait_ge(h1_ready[u], i + 1)
                    for fc in range(FC):
                        at = bass.ds(e * (FC * D) + fc * D, D)
                        w_high = w2h[:].rearrange("p e n -> p (e n)")[:, at]
                        w_low = w2l[:].rearrange("p e n -> p (e n)")[:, at]
                        out = ps_e[u][:, 0:D]
                        pe.matmul(out, h1h[u][:, fc, :], w_high, start=(fc == 0), stop=False)
                        pe.matmul(out, h1h[u][:, fc, :], w_low, start=False, stop=False)
                        mm = pe.matmul(out, h1l[u][:, fc, :], w_high, start=False, stop=(fc == FC - 1))
                    mm.then_inc(down[u], 1)

                def experts_of(i, count):
                    _, experts = nc.values_load_multi_w_load_instructions(
                        tile_expert[0:1, bass.ds(2 * i, count)], engines=[mybir.EngineType.PE],
                        min_val=0, max_val=E - 1)
                    return experts

                def up_waits(i, u):
                    pe.wait_ge(h_ready[u], i + 1)
                    pe.wait_ge(gelus[u], i * FC)

                turn(0, 0)
                turn(0, 1)
                first, = experts_of(0, 1)
                up_waits(0, 0)
                layer1(0, 0, first)

                def body(i, u, e, more2, more1):
                    if more1:
                        up_waits(i + u, 1 - u)
                    if more2:
                        turn(i + 1, u)
                    if more1:
                        layer1(i + u, 1 - u, e[u + 1])
                    layer2(i, u, e[u])

                with pe.Fori(0, T // 2 - 1) as i:
                    e = experts_of(i, 3)
                    body(i, 0, e, True, True)
                    body(i, 1, e, True, True)
                e = experts_of(T // 2 - 1, 2)
                body(T // 2 - 1, 0, e, False, True)
                body(T // 2 - 1, 1, e, False, False)

            @block.scalar
            def _(act):
                act.preload_act_table(ACT.Gelu)
                with act.Fori(0, T // 2) as i:
                    for u in range(2):
                        act.wait_ge(h1_ready[u], i)
                        act.wait_ge(b1_loaded[u], i * 16 + 16)
                        for fc in range(FC):
                            if fc % (FC // 2) == 0:
                                act.wait_ge(up[u], i * 2 + fc // (FC // 2) + 1)
                            act.activation(h1[u][:, fc, :], ps_h[u][:, fc, :], ACT.Gelu,
                                           bias=b1[u][:, fc:fc + 1], scale=1.0 / W_SCALE).then_inc(gelus[u], 1)

            @block.vector
            def _(dv):
                dv.wait_ge(consts, 48)

                def normed(i, u):
                    dv.wait_ge(turned[u], i + 1)
                    for c in range(DC):
                        mm = dv.tensor_scalar(hf[u][:, c, :], ps_x[u][:, c * P:(c + 1) * P], g_col[:, c:c + 1],
                                              b_col[:, c:c + 1], ALU.mult, ALU.add)
                    mm.then_inc(hf_ready[u], 1)
                    dv.wait_ge(hf_ready[u], i + 1)
                    dv.wait_ge(up[u], 2 * i)
                    dv.tensor_copy(hh[u][:], hf[u][:]).then_inc(hh_ready[u], 1)
                    dv.wait_ge(hh_ready[u], i + 1)
                    dv.tensor_tensor(hl[u][:], hf[u][:], hh[u][:], ALU.subtract).then_inc(h_ready[u], 1)

                def hidden(i, u):
                    dv.wait_ge(down[u], i)
                    dv.wait_ge(gelus[u], i * FC + FC)
                    dv.tensor_copy(h1h[u][:], h1[u][:]).then_inc(h1h_ready[u], 1)
                    dv.wait_ge(h1h_ready[u], i + 1)
                    dv.tensor_tensor(h1l[u][:], h1[u][:], h1h[u][:], ALU.subtract).then_inc(h1_ready[u], 1)

                def output(i, u):
                    dv.wait_ge(stored[u], i * 16)
                    dv.wait_ge(b2_loaded[u], i * 16 + 16)
                    dv.wait_ge(down[u], i + 1)
                    dv.scalar_tensor_tensor(eo[u][:], ps_e[u][:, 0:D], 1.0 / W_SCALE, b2[u][:],
                                            ALU.mult, ALU.add).then_inc(eo_ready[u], 1)

                normed(0, 0)
                normed(0, 1)
                hidden(0, 0)

                def body(i, u, more2, more1):
                    if more2:
                        normed(i + 1, u)
                    if more1:
                        hidden(i + u, 1 - u)
                    output(i, u)

                with dv.Fori(0, T // 2 - 1) as i:
                    body(i, 0, True, True)
                    body(i, 1, True, True)
                body(T // 2 - 1, 0, False, True)
                body(T // 2 - 1, 1, False, False)


def combine_phase(nc, x_dram, eo_dram, gates, slots, out_dram):
    with ExitStack() as ctx:
        DEPTH = 4
        rows = [[ctx.enter_context(nc.sbuf_tensor(f"mix_rows{c}_{z}", [P, D], F32)) for z in range(DEPTH)]
                for c in range(TOP)]
        x_sb = [ctx.enter_context(nc.sbuf_tensor(f"mix_x{z}", [P, TPB, D], F32)) for z in range(2)]
        half = ctx.enter_context(nc.sbuf_tensor("mix_half", [P, 2, D], F32))
        out_sb = [ctx.enter_context(nc.sbuf_tensor(f"mix_out{z}", [P, TPB, D], F32)) for z in range(2)]

        def sem(n):
            return ctx.enter_context(nc.semaphore(f"mix_{n}"))
        mixed = sem("mixed")
        half_ready = sem("half_ready")
        stored = [sem(f"stored{z}") for z in range(2)]
        x_loaded = [sem(f"x_loaded{z}") for z in range(2)]
        gathered = [sem(f"gathered{z}") for z in range(DEPTH)]
        x_b = x_dram.rearrange("(b t p) d -> b p t d", t=TPB, p=P)
        out_b = out_dram.rearrange("(b t p) d -> b p t d", t=TPB, p=P)
        blocks = NT // TPB
        with nc.Block() as block:

            @block.gpsimd
            def _(pool):
                for t in range(NT):
                    if t >= DEPTH:
                        pool.wait_ge(mixed, t - DEPTH + 1)
                    for c in range(TOP):
                        pool.indirect_dma_start(
                            out=rows[c][t % DEPTH][:], out_offset=None, in_=eo_dram,
                            in_offset=bass.IndirectOffsetOnAxis(ap=slots[:, c, t:t + 1], axis=0)
                        ).then_inc(gathered[t % DEPTH], 16)

            @block.sync
            def _(sp):
                for b in range(blocks):
                    if b >= 2:
                        sp.wait_ge(mixed, (b - 1) * TPB)
                    sp.dma_start(x_sb[b % 2][:], x_b[b]).then_inc(x_loaded[b % 2], 16)
                    if b >= 1:
                        sp.wait_ge(mixed, b * TPB)
                        sp.dma_start(out_b[b - 1], out_sb[(b - 1) % 2][:]).then_inc(stored[(b - 1) % 2], 16)
                sp.wait_ge(mixed, NT)
                sp.dma_start(out_b[blocks - 1], out_sb[(blocks - 1) % 2][:]).then_inc(
                    stored[(blocks - 1) % 2], 16)
                for z in range(2):
                    sp.wait_ge(stored[z], 16 * blocks // 2)

            @block.vector
            def _(dv):
                for t in range(NT):
                    b, j = t // TPB, t % TPB
                    dv.wait_ge(gathered[t % DEPTH], 16 * TOP * (t // DEPTH + 1))
                    if j == 0:
                        dv.wait_ge(x_loaded[b % 2], 16 * (b // 2 + 1))
                        if b >= 2:
                            dv.wait_ge(stored[b % 2], 16 * (b // 2))
                    dv.scalar_tensor_tensor(half[:, t % 2, :], rows[0][t % DEPTH][:], gates[:, 0, t:t + 1],
                                            x_sb[b % 2][:, j, :], ALU.mult, ALU.add).then_inc(half_ready, 1)
                    dv.wait_ge(half_ready, t + 1)
                    dv.scalar_tensor_tensor(out_sb[b % 2][:, j, :], rows[1][t % DEPTH][:],
                                            gates[:, 1, t:t + 1], half[:, t % 2, :], ALU.mult, ALU.add
                                            ).then_inc(mixed, 1)


def build(nc, a, out):
    def scratch(name, shape, dt):
        return nc.dram_tensor("dram_" + name, shape, dt, kind="Internal").ap()

    q1 = scratch("sa_qk_parts", (PARTS, 2 * D, N), BF16)
    v1 = scratch("sa_v", (N, HEADS * VW), F32)
    k2 = scratch("ca_k_parts", (PARTS, D, BATCH * CTX), BF16)
    v2 = scratch("ca_v", (BATCH * CTX, HEADS * VW), F32)
    q2 = scratch("ca_q_parts", (PARTS, D, N), BF16)
    o1 = scratch("sa_o", (2, D, N), F32)
    o2 = scratch("ca_o", (2, D, N), F32)
    x1 = scratch("x1", (N, D), F32)
    x2 = scratch("x2", (N, D), F32)
    xs = scratch("slot_rows", (SLOTS, D), F32)
    eo = scratch("slot_outputs", (SLOTS, D), F32)
    ident = a["ident"]

    tokens_phase(nc, "kv", a["ctx"], CTX, 1, ln_g=a["ca_kv_ln_g"], ln_b=a["ca_kv_ln_b"], ident_dram=ident,
                 qk=(a["ca_wk"], a["ca_bk"], k2), v=(a["ca_wv"], a["ca_bv"], v2))
    tokens_phase(nc, "qkv", a["x"], P, N // (TPB * P), ln_g=a["sa_ln_g"], ln_b=a["sa_ln_b"],
                 ident_dram=ident, qk=(a["sa_wqk"], a["sa_bqk"], q1), v=(a["sa_wv"], a["sa_bv"], v1))
    attention_phase(nc, "sa", q1[:, 0:D, :], q1[:, D:2 * D, :], v1, o1, ident, keys=SEQ, key_tiles=SEQ // P,
                    clear_dram=xs)
    tokens_phase(nc, "mid", a["x"], P, N // (TPB * P), ln_g=a["ca_q_ln_g"], ln_b=a["ca_q_ln_b"],
                 ident_dram=ident, attn=(o1, a["sa_wo"], a["sa_bo"], x1), qk=(a["ca_wq"], a["ca_bq"], q2))
    attention_phase(nc, "ca", q2, k2, v2, o2, ident, keys=CTX, key_tiles=1)
    with ExitStack() as ctx:
        gates = ctx.enter_context(nc.sbuf_tensor("gates", [P, TOP, NT], F32))
        slots = ctx.enter_context(nc.sbuf_tensor("slots", [P, TOP, NT], I32))
        tile_expert = ctx.enter_context(nc.sbuf_tensor("tile_expert", [1, SLOT_TILES], I32))
        with ExitStack() as wctx:
            with (nc.sbuf_tensor("logits", [P, NT, E], F32, side="right") as logits,
                  nc.sbuf_tensor("xhat_all", [P, NT, D], F32, side="right") as xhat_all):
                tokens_phase(nc, "last", x1, P, N // (TPB * P), ln_g=a["moe_ln_g"], ln_b=a["moe_ln_b"],
                             ident_dram=ident, attn=(o2, a["ca_wo"], a["ca_bo"], x2),
                             router=(a["w_r"], a["b_r"], logits, xhat_all))
                w_parts = [[wctx.enter_context(nc.sbuf_tensor(f"w{w + 1}_{part}", [P, E, DC * F], F16))
                            for part in ("high", "low")] for w in range(2)]
                route_phase(nc, logits, xhat_all, gates, slots, tile_expert, xs, a,
                            (a["w1"], a["w2"]), w_parts)
            expert_phase(nc, xs, eo, tile_expert, w_parts, a["b1"], a["b2"], a["moe_ln_g"], a["moe_ln_b"],
                         ident)
        combine_phase(nc, x2, eo, gates, slots, out)


def laid_out(inputs):
    a = {n.removeprefix("L0_xattn_"): np.asarray(v) for n, v in inputs.items()}

    def column(v):
        return v.reshape(-1, P).T
    out = {"x": a["x"].reshape(N, D), "ctx": a["ctx_1024"].reshape(BATCH * CTX, D)}
    for n in ("sa_ln_g", "sa_ln_b", "ca_q_ln_g", "ca_q_ln_b", "ca_kv_ln_g", "ca_kv_ln_b", "moe_ln_g", "moe_ln_b"):
        out[n] = column(a[n])
    out["sa_wqk"], out["sa_bqk"] = a["sa_in_w"][:2 * D].T, column(a["sa_in_b"][:2 * D])
    out["ca_wq"], out["ca_bq"] = a["ca_in_w"][:D].T, column(a["ca_in_b"][:D])
    out["ca_wk"], out["ca_bk"] = a["ca_in_w"][D:2 * D].T, column(a["ca_in_b"][D:2 * D])
    for n in ("sa", "ca"):
        out[n + "_wv"], out[n + "_bv"] = a[n + "_in_w"][2 * D:].T, a[n + "_in_b"][2 * D:]
        out[n + "_wo"], out[n + "_bo"] = a[n + "_out_w"].T, a[n + "_out_b"]
    out["w_r"], out["b_r"] = a["router_w"].T, a["router_b"]
    out["w1"], out["w2"] = a["e_fc1_w"].transpose(0, 2, 1), a["e_fc2_w"].transpose(0, 2, 1)
    out["b1"], out["b2"] = a["e_fc1_b"].reshape(E, FC, P).transpose(0, 2, 1), a["e_fc2_b"]
    return out


def constants():
    return {
        "ident": np.eye(P, dtype=np.float32),
        "rev": np.tile(np.arange(E, 0, -1, dtype=np.float32), (P, 1)),
        "tri": np.triu(np.ones((P, P), np.float32), 1),
        "ones": np.ones((P, P), np.float32),
        "tile_no": np.arange(SLOT_TILES, dtype=np.float32)[None, :],
    }


def kernel(**inputs):
    import concourse.bacc as bacc
    from concourse.bass_utils import run_bass_kernel_spmd

    nc = bacc.Bacc("TRN2", target_bir_lowering=False, num_devices=1)
    arrays, aps = {}, {}
    for name, value in (laid_out(inputs) | constants()).items():
        value = np.ascontiguousarray(value)
        arrays[f"in_{name}"] = value
        aps[name] = nc.dram_tensor(f"in_{name}", value.shape, mybir.dt.from_np(value.dtype),
                                   kind="ExternalInput").ap()
    out = nc.dram_tensor("out", (N, D), F32, kind="ExternalOutput").ap()
    build(nc, aps, out)
    got = run_bass_kernel_spmd(nc, [arrays], core_ids=[0])
    return got.results[0]["out"].reshape(BATCH, SEQ, D)
```

```python
from contextlib import ExitStack, contextmanager

import numpy as np

import concourse.bass as bass
from concourse import mybir

F32 = mybir.dt.float32
BF16 = mybir.dt.bfloat16
F16 = mybir.dt.float16
I32 = mybir.dt.int32
ALU = mybir.AluOpType
ACT = mybir.ActivationFunctionType
AX_X = mybir.AxisListType.X

P = 128
D = 256
DC = D // P
HEADS = 16
DH = D // HEADS
BATCH = 4
SEQ = 1024
CTX = 77
N = BATCH * SEQ
NT = N // P
E = 8
TOP = 2
F = 1024
FC = F // P
EPS = 1e-5
TPB = 4
HG = 4
GROUPS = BATCH * HEADS // HG
VW = 2 * DH
PARTS = 3
Q_STACK = [0, 0, 0, 1, 1, 2]
K_STACK = [0, 1, 2, 0, 1, 0]
SR = len(Q_STACK) * DH
ST = 2 * P
SLOT_TILES = (TOP * N + E * (ST - 1)) // ST
SLOTS = SLOT_TILES * ST
ROWS = SLOTS // P
W_SCALE = 64.0
BIG = 3.0e38


@contextmanager
def semaphores(nc, phase):
    made = []

    def sem(n):
        made.append(nc.alloc_semaphore(f"{phase}_{n}"))
        return made[-1]
    yield sem
    nc.clear_and_free_semaphores(made)
    nc.all_engine_barrier()


def tokens_program(nc, ctx, block, psum, name, x_dram, rows, blocks, *, ln_g, ln_b, ident_dram,
                   attn=None, qk=None, v=None, router=None, weights=None):
    W = TPB * rows
    QC = qk[0].shape[1] // P if qk else 0
    def sb(n, shape, dt=F32):
        return ctx.enter_context(nc.sbuf_tensor(f"{name}_{n}", shape, dt))

    def two(n, shape, dt=F32):
        return [sb(f"{n}{u}", shape, dt) for u in range(2)]

    def ps(n, shape):
        if n not in psum:
            psum[n] = ctx.enter_context(nc.psum_tensor(f"{name}_{n}", [P, *shape[1:]], F32))
        return psum[n][0:shape[0]]

    sem = ctx.enter_context(semaphores(nc, name))

    def sems(n):
        return [sem(f"{n}{u}") for u in range(2)]

    ident = sb("ident", [P, P])
    g_col = sb("g_col", [P, DC])
    b_col = sb("b_col", [P, DC])
    x_sb = two("x", [rows, TPB, D])
    stats = two("stats", [rows, TPB, 6])
    mean2, diff, m2, mean, dd, var_sum, var, std, r0, r0sq, newton, newton2, rstd = (
        two(n, [rows, TPB]) for n in ("mean2", "diff", "m2", "mean", "dd", "var_sum", "var", "std",
                                      "r0", "r0sq", "newton", "newton2", "rstd"))
    xhat = two("xhat", [rows, TPB, D])
    xT = two("xT", [P, DC, W])
    psT = ps("psT", [P, DC, 512])
    consts = sem("consts")
    late_consts = sem("late_consts")
    x_loaded = sems("x_loaded")
    ln = sems("ln")
    std_ready = sems("std_ready")
    xhat_ready = sems("xhat_ready")
    transposed = sems("transposed")
    xT_ready = sems("xT_ready")
    n_consts = 3
    n_late = 0
    if attn:
        o_dram, sums_dram, r_dram, w_out_t, b_out, x_out = attn
        R_COLS = SEQ * HEADS // P
        sums = sb("sums", [P, BATCH, R_COLS])
        recips = sb("recips", [P, BATCH, R_COLS])
        oT = two("oT", [P, DC, W])
        rT = two("rT", [P, DC, W])
        onT = two("onT", [P, DC, W])
        wo = sb("wo", [P, DC, D])
        bo = sb("bo", [rows, D])
        xb = two("xb", [rows, TPB, D])
        x1 = two("x1", [rows, TPB, D])
        psY = [ps(f"psY{u}", [rows, TPB, D]) for u in range(2)]
        sums_loaded = sem("sums_loaded")
        recips_ready = sem("recips_ready")
        recips_stored = sem("recips_stored")
        o_loaded = sems("o_loaded")
        on_ready = sems("on_ready")
        projected = sems("projected")
        xb_ready = sems("xb_ready")
        x1_ready = sems("x1_ready")
        x1_stored = sems("x1_stored")
        n_consts += 2
        R_ROWS = P // DH
        O_LOADS = 16 * (1 + R_ROWS)
        assert SEQ == 2 * W

        def entries(ap, first, last):
            return ap[first:last].rearrange("b h (q n) -> (h q) b n", n=R_COLS)
    x_ln = x1 if attn else x_sb
    if qk:
        w_qk = sb("w_qk", [P, DC, QC * P])
        b_qk = sb("b_qk", [P, QC])
        qf = two("qf", [P, QC, W])
        rest = two("rest", [P, QC, W])
        part = [two(f"part{i}_", [P, QC, W], BF16) for i in range(PARTS)]
        psQK = ps("psQK", [P, 2, 512])
        qk_done = sems("qk_done")
        cut0 = sems("cut0")
        rest_ready = sems("rest_ready")
        parts_ready = sems("parts_ready")
        parts_stored = sems("parts_stored")
        n_late += 2
    if v:
        w_v = sb("w_v", [P, DC, D])
        b_v = sb("b_v", [rows, D])
        v_sb = two("v_sb", [rows, TPB, HEADS, VW])
        psV = ps("psV", [rows, TPB, D])
        v_done = sems("v_done")
        v_ones = sem("v_ones")
        v_ready = sems("v_ready")
        v_stored = sems("v_stored")
        n_late += 2
    if router:
        w_r = sb("w_r", [P, DC, E])
        b_r = sb("b_r", [rows, E])
        psL = ps("psL", [rows, TPB, E])
        logits_done = sems("logits_done")
        logits_ready = sems("logits_ready")
        xhat_kept = sems("xhat_kept")
        n_late += 2
    if weights:
        assert blocks == E
        w_stage = two("w_stage", [P, DC, F])
        w_loaded = sems("w_loaded")
        w_high = sems("w_high")
        w_low = sems("w_low")

        def piece(w, e, c):
            return w[:].rearrange("p e n -> p (e n)")[:, bass.ds(e * (DC * F) + c * F, F)]
    before = psum["read"]
    end_i, end_u = divmod(blocks - 1, 2)
    psum["read"] = {"psT": (xT_ready[end_u], (end_i + 1) * DC)}
    if qk:
        psum["read"]["psQK"] = (cut0[end_u], (end_i + 1) * QC)
    if v:
        psum["read"]["psV"] = (v_ready[end_u], (end_i + 1) * TPB)
    VAR_AT = TPB + 7
    LN_OPS = VAR_AT + 5

    def steps(engine, step):
        inner = range(1, blocks // 2 - 1) if blocks % 2 == 0 else range(0)
        lo, hi = (2 * inner.start, 2 * inner.stop) if len(inner) > 1 else (blocks, blocks)

        def peeled(ts):
            for t in ts:
                step(divmod(t, 2), lambda d, t=t: 0 <= t + d < blocks)

        peeled(range(-2, min(lo, blocks + 2)))
        if len(inner) > 1:
            with engine.Fori(inner.start, inner.stop) as i:
                for u in range(2):
                    step((i, u), lambda d: True)
        peeled(range(hi, blocks + 2))

    def at(t, d):
        i, u = t
        return i + (u + d) // 2, (u + d) % 2

    def in_slot(u):
        return (blocks + 1 - u) // 2

    def number(i, u):
        return 2 * i + u

    x_rows = x_dram.rearrange("(b t p) d -> b p t d", p=rows, t=TPB)

    def load_x(sp, b):
        sp.dma_start(x_sb[b[1]][:], x_rows[bass.ds(number(*b), 1)].rearrange(
            "b p t d -> p (b t) d")).then_inc(x_loaded[b[1]], 16)

    def load_o(sp, b):
        u = b[1]
        sp.dma_start(oT[u][:], o_dram.rearrange("(c p) n -> p c n", p=P)[
            :, :, bass.ds(number(*b) * W, W)]).then_inc(o_loaded[u], 16)

    def load_r(sp, b):
        u = b[1]
        r_rows = r_dram.rearrange("b (c h) (q n) -> h q b c n", c=DC, n=W)
        for h in range(R_ROWS):
            sp.dma_start(rT[u][h * DH:(h + 1) * DH, :, :],
                         r_rows[h:h + 1, u, bass.ds(b[0], 1)].rearrange(
                             "h b c n -> (h b) c n").broadcast_to([DH, DC, W])
                         ).then_inc(o_loaded[u], 16)

    def load_weights(sp, b):
        sp.dma_start(w_stage[b[1]][:], weights[0].rearrange("e (c p) n -> e p c n", p=P)[
            bass.ds(number(*b), 1)].rearrange("e p c n -> p (e c) n")
        ).then_inc(w_loaded[b[1]], 16)

    @block.sync
    def _(sp):
        if attn:
            sp.dma_start(sums[:], entries(sums_dram, 0, BATCH)).then_inc(sums_loaded, 16)
        load_x(sp, (0, 0))
        sp.dma_start(ident[:], ident_dram).then_inc(consts, 16)
        sp.dma_start(g_col[:], ln_g).then_inc(consts, 16)
        sp.dma_start(b_col[:], ln_b).then_inc(consts, 16)

        def wide(dst, vec, loaded):
            sp.dma_start(dst, vec.rearrange("(a n) -> a n", a=1).broadcast_to(
                [rows, vec.shape[0]])).then_inc(loaded, 16)

        if attn:
            sp.dma_start(wo[:], w_out_t.rearrange("(c p) n -> p c n", p=P)).then_inc(consts, 16)
            wide(bo[:], b_out, consts)
            load_o(sp, (0, 0))
            sp.wait_ge(recips_ready, 1)
            sp.dma_start(entries(r_dram, 0, 1), recips[:, 0:1]).then_inc(recips_stored, 16)
        if qk:
            sp.dma_start(w_qk[:], qk[0].rearrange("(c p) n -> p c n", p=P)).then_inc(late_consts, 16)
            sp.dma_start(b_qk[:], qk[1]).then_inc(late_consts, 16)
        if v:
            sp.dma_start(w_v[:], v[0].rearrange("(c p) n -> p c n", p=P)).then_inc(late_consts, 16)
            wide(b_v[:], v[1], late_consts)
        if router:
            sp.dma_start(w_r[:], router[0].rearrange("(c p) n -> p c n", p=P)
                         ).then_inc(late_consts, 16)
            wide(b_r[:], router[1], late_consts)
        if attn:
            sp.wait_ge(recips_stored, 16)
            load_r(sp, (0, 0))
        if blocks > 1:
            load_x(sp, (0, 1))
        if attn:
            load_o(sp, (0, 1))
            load_r(sp, (0, 1))
            sp.wait_ge(recips_ready, 2)
            sp.dma_start(entries(r_dram, 1, BATCH), recips[:, 1:BATCH]).then_inc(recips_stored, 16)
            sp.wait_ge(recips_stored, 32)
        if weights:
            for t in range(2):
                load_weights(sp, divmod(t, 2))

    yield

    @block.sync
    def _(sp):
        def step(t, has):
            if has(0) and has(2):
                i, u = t
                if attn:
                    sp.wait_ge(xb_ready[u], i + 1)
                    load_x(sp, at(t, 2))
                    sp.wait_ge(on_ready[u], i + 1)
                    load_o(sp, at(t, 2))
                    load_r(sp, at(t, 2))
                else:
                    sp.wait_ge(xhat_ready[u], i * TPB + TPB)
                    load_x(sp, at(t, 2))
            if attn and has(0):
                i, u = t
                sp.wait_ge(x1_ready[u], i + 1)
                sp.dma_start(x_out.rearrange("(b t p) d -> b p t d", p=rows, t=TPB)[
                    bass.ds(number(i, u), 1)].rearrange("b p t d -> p (b t) d"), x1[u][:]
                ).then_inc(x1_stored[u], 16)
            if weights and has(-1) and has(1):
                i, u = at(t, 1)
                sp.wait_ge(w_low[u], i * DC)
                load_weights(sp, (i, u))
            if router and has(0):
                i, u = t
                sp.wait_ge(xhat_ready[u], i * TPB + TPB)
                sp.dma_start(router[3].rearrange("(b t p) d -> b p t d", p=rows, t=TPB)[
                    bass.ds(number(i, u), 1)].rearrange("b p t d -> p (b t) d"), xhat[u][:]
                ).then_inc(xhat_kept[u], 16)
            if v and has(-2):
                i, u = at(t, -2)
                sp.wait_ge(v_ready[u], i * TPB + TPB)
                sp.dma_start(v[2].rearrange("(b t p) n -> b p t n", p=rows, t=TPB)[
                    bass.ds(number(i, u), 1)].rearrange("b p t n -> p (b t) n"),
                    v_sb[u][:].rearrange("p t h w -> p t (h w)")).then_inc(v_stored[u], 16)
            if qk and has(-2):
                i, u = at(t, -2)
                for n in range(PARTS):
                    if n == 0:
                        sp.wait_ge(cut0[u], i * QC + QC)
                    else:
                        sp.wait_ge(parts_ready[u], i * (PARTS - 1) + n)
                    sp.dma_start(qk[2][n].rearrange("(c p) n -> p c n", p=P)[
                        :, :, bass.ds(number(i, u) * W, W)], part[n][u][:]
                    ).then_inc(parts_stored[u], 16)
        steps(sp, step)
        for u in range(2):
            if v and in_slot(u):
                sp.wait_ge(v_stored[u], 16 * in_slot(u))
            if router:
                sp.wait_ge(xhat_kept[u], 16 * in_slot(u))
            if attn:
                sp.wait_ge(x1_stored[u], 16 * in_slot(u))
            if qk and in_slot(u):
                sp.wait_ge(parts_stored[u], 16 * PARTS * in_slot(u))

    @block.gpsimd
    def _(pool):
        if v:
            for u in range(min(2, blocks)):
                pool.memset(v_sb[u][:], 1.0).then_inc(v_ones, 1)
                pool.wait_ge(v_ones, u + 1)
        if attn:
            pool.wait_ge(consts, 16 * n_consts)

        def step(t, has):
            if attn and has(1):
                i, u = at(t, 1)
                pool.wait_ge(x1_ready[u], i)
                pool.wait_ge(x_loaded[u], i * 16 + 16)
                pool.tensor_tensor(xb[u][:], x_sb[u][:], bo[:, None, :].broadcast_to([rows, TPB, D]),
                                   ALU.add).then_inc(xb_ready[u], 1)
            if attn and has(2):
                i, u = at(t, 2)
                pool.wait_ge(projected[u], i)
                pool.wait_ge(o_loaded[u], i * O_LOADS + O_LOADS)
                pool.tensor_tensor(onT[u][:], oT[u][:], rT[u][:], ALU.mult).then_inc(on_ready[u], 1)
        steps(pool, step)

    @block.vector
    def _(dv):
        if attn:
            dv.wait_ge(sums_loaded, 16)
            dv.reciprocal(recips[:, 0:1], sums[:, 0:1]).then_inc(recips_ready, 1)
            dv.reciprocal(recips[:, 1:BATCH], sums[:, 1:BATCH]).then_inc(recips_ready, 1)

        def cut_low(i, u):
            for c in range(DC):
                dv.wait_ge(w_high[u], i * DC + c + 1)
                dv.scalar_tensor_tensor(piece(weights[2], number(i, u), c), w_stage[u][:, c, :],
                                        W_SCALE, piece(weights[1], number(i, u), c),
                                        ALU.mult, ALU.subtract).then_inc(w_low[u], 1)

        def norm(i, u):
            if attn:
                dv.wait_ge(x1_stored[u], i * 16)
                dv.wait_ge(xb_ready[u], i + 1)
                dv.wait_ge(projected[u], i + 1)
                dv.tensor_tensor(x1[u][:], psY[u][:], xb[u][:], ALU.add).then_inc(x1_ready[u], 1)
                dv.wait_ge(x1_ready[u], i + 1)
            else:
                dv.wait_ge(x_loaded[u], i * 16 + 16)
            k = 0

            def op(ins):
                nonlocal k
                k += 1
                ins.then_inc(ln[u], 1)

            def own():
                dv.wait_ge(ln[u], i * LN_OPS + k)
            for j in range(TPB):
                op(dv.bn_stats(stats[u][:, j, :], x_ln[u][:, j, :]))
            own()
            s = stats[u]
            op(dv.tensor_tensor(mean2[u][:], s[:, :, 1], s[:, :, 4], ALU.add))
            op(dv.tensor_tensor(diff[u][:], s[:, :, 1], s[:, :, 4], ALU.subtract))
            op(dv.tensor_tensor(m2[u][:], s[:, :, 2], s[:, :, 5], ALU.add))
            own()
            op(dv.tensor_scalar(mean[u][:], mean2[u][:], 0.5, None, ALU.mult))
            op(dv.scalar_tensor_tensor(dd[u][:], diff[u][:], D / 4, diff[u][:], ALU.mult, ALU.mult))
            own()
            op(dv.tensor_tensor(var_sum[u][:], dd[u][:], m2[u][:], ALU.add))
            own()
            op(dv.tensor_scalar(var[u][:], var_sum[u][:], 1.0 / D, EPS, ALU.mult, ALU.add))
            assert k == VAR_AT
            dv.wait_ge(std_ready[u], i + 1)
            op(dv.reciprocal(r0[u][:], std[u][:]))
            own()
            op(dv.tensor_tensor(r0sq[u][:], r0[u][:], r0[u][:], ALU.mult))
            own()
            op(dv.tensor_tensor(newton[u][:], r0sq[u][:], var[u][:], ALU.mult))
            own()
            op(dv.tensor_scalar(newton2[u][:], newton[u][:], -0.5, 1.5, ALU.mult, ALU.add))
            own()
            op(dv.tensor_tensor(rstd[u][:], newton2[u][:], r0[u][:], ALU.mult))
            own()
            assert k == LN_OPS
            dv.wait_ge(transposed[u], i)
            if router:
                dv.wait_ge(xhat_kept[u], i * 16)
            for j in range(TPB):
                dv.tensor_scalar(xhat[u][:, j, :], x_ln[u][:, j, :], mean[u][:, j:j + 1],
                                 rstd[u][:, j:j + 1], ALU.subtract, ALU.mult
                                 ).then_inc(xhat_ready[u], 1)

        def finish(i, u):
            if v:
                dv.wait_ge(v_stored[u], i * 16)
                dv.wait_ge(v_done[u], i + 1)
                for j in range(TPB):
                    dv.tensor_tensor(
                        v_sb[u][:, j, :, 0:DH], psV[:, j, :].rearrange("p (h w) -> p h w", h=HEADS),
                        b_v[:].rearrange("p (h w) -> p h w", h=HEADS), ALU.add
                    ).then_inc(v_ready[u], 1)
            if qk:
                dv.wait_ge(parts_stored[u], i * 16 * PARTS)
                dv.wait_ge(cut0[u], i * QC + QC)
                dv.tensor_tensor(rest[u][:], qf[u][:], part[0][u][:], ALU.subtract
                                 ).then_inc(rest_ready[u], 1)
                dv.wait_ge(rest_ready[u], i + 1)
                dv.tensor_copy(part[1][u][:], rest[u][:]).then_inc(parts_ready[u], 1)
                dv.wait_ge(parts_ready[u], i * (PARTS - 1) + 1)
                dv.tensor_tensor(part[2][u][:], rest[u][:], part[1][u][:], ALU.subtract
                                 ).then_inc(parts_ready[u], 1)
            if router:
                dv.wait_ge(logits_done[u], i + 1)
                dv.tensor_tensor(router[2][:, bass.ds(number(i, u) * TPB, TPB), :], psL[:],
                                 b_r[:, None, :].broadcast_to([rows, TPB, E]), ALU.add
                                 ).then_inc(logits_ready[u], 1)

        def step(t, has):
            if has(0):
                norm(*t)
            if weights and has(0):
                cut_low(*t)
            if has(-2):
                finish(*at(t, -2))
            if has(-1) and not has(-2):
                dv.wait_ge(late_consts, 16 * n_late)
                if v:
                    dv.wait_ge(v_ones, min(2, blocks))
        steps(dv, step)

    @block.scalar
    def _(act):
        act.preload_act_table(ACT.Sqrt)
        act.wait_ge(consts, 16 * n_consts)

        def cut_high(i, u):
            for c in range(DC):
                act.activation(piece(weights[1], number(i, u), c), w_stage[u][:, c, :], ACT.Copy,
                               scale=W_SCALE).then_inc(w_high[u], 1)

        def root(i, u):
            if weights:
                act.wait_ge(w_loaded[u], i * 16 + 16)
            act.wait_ge(ln[u], i * LN_OPS + VAR_AT)
            act.activation(std[u][:], var[u][:], ACT.Sqrt).then_inc(std_ready[u], 1)

        def scale(i, u):
            act.wait_ge(transposed[u], i + 1)
            if v:
                act.wait_ge(v_done[u], i)
            elif qk:
                act.wait_ge(qk_done[u], i * QC)
            if router:
                act.wait_ge(logits_done[u], i)
            for c in range(DC):
                act.activation(xT[u][:, c, :], psT[:, c, 0:W], ACT.Identity, bias=b_col[:, c:c + 1],
                               scale=g_col[:, c:c + 1]).then_inc(xT_ready[u], 1)

        def evacuate(i, u, s, first):
            if first and s == 0:
                act.wait_ge(late_consts, 16 * n_late)
            if s == 0:
                act.wait_ge(parts_ready[u], i * (PARTS - 1))
                act.wait_ge(parts_stored[u], i * 16 * PARTS)
            act.wait_ge(qk_done[u], i * QC + s + 1)
            act.activation(qf[u][:, s, :], psQK[:, s % 2, 0:W], ACT.Identity, bias=b_qk[:, s:s + 1])
            act.activation(part[0][u][:, s, :], psQK[:, s % 2, 0:W], ACT.Identity,
                           bias=b_qk[:, s:s + 1]).then_inc(cut0[u], 1)

        def step(t, has):
            if has(0):
                scale(*t)
            if has(-1):
                for s in range(QC // 2):
                    evacuate(*at(t, -1), s, not has(-2))
            if has(1):
                root(*at(t, 1))
                if weights:
                    cut_high(*at(t, 1))
            if has(-1):
                for s in range(QC // 2, QC):
                    evacuate(*at(t, -1), s, not has(-2))
        steps(act, step)

    @block.tensor
    def _(pe):
        pe.wait_ge(consts, 16 * n_consts)

        def rows_of(psum, lhs, w, done):
            for j in range(TPB):
                for c in range(DC):
                    mm = pe.matmul(psum[:, j, :], lhs[:, c, j * rows:(j + 1) * rows], w[:, c, :],
                                   start=(c == 0), stop=(c == DC - 1))
            mm.then_inc(done, 1)

        def read_before(n):
            if n in before:
                pe.wait_ge(*before[n])

        def turn(i, u, first):
            pi, pu = at((i, u), -1)
            if first:
                read_before("psT")
            else:
                pe.wait_ge(xT_ready[pu], pi * DC + DC)
            for j in range(TPB):
                pe.wait_ge(xhat_ready[u], i * TPB + j + 1)
                for c in range(DC):
                    mm = pe.transpose(psT[:, c, j * rows:(j + 1) * rows],
                                      xhat[u][:, j, c * P:(c + 1) * P], ident[0:rows, 0:rows])
            mm.then_inc(transposed[u], 1)

        def project(i, u, first):
            pi, pu = at((i, u), -1)
            if first:
                pe.wait_ge(late_consts, 16 * n_late)
                read_before("psQK")
                read_before("psV")
            pe.wait_ge(xT_ready[u], i * DC + DC)
            for s in range(QC):
                if s >= 2:
                    pe.wait_ge(cut0[u], i * QC + s - 1)
                elif not first:
                    pe.wait_ge(cut0[pu], pi * QC + QC - 1 + s)
                for c in range(DC):
                    mm = pe.matmul(psQK[:, s % 2, 0:W], w_qk[:, c, s * P:(s + 1) * P], xT[u][:, c, :],
                                   start=(c == 0), stop=(c == DC - 1))
                mm.then_inc(qk_done[u], 1)
            if v:
                if not first:
                    pe.wait_ge(v_ready[pu], pi * TPB + TPB)
                rows_of(psV, xT[u], w_v, v_done[u])
            if router:
                if not first:
                    pe.wait_ge(logits_ready[pu], pi + 1)
                rows_of(psL, xT[u], w_r, logits_done[u])

        def step(t, has):
            if attn and has(1):
                i, u = at(t, 1)
                pe.wait_ge(x1_ready[u], i)
                pe.wait_ge(on_ready[u], i + 1)
                rows_of(psY[u], onT[u], wo, projected[u])
            if has(0):
                turn(*t, not has(-1))
            if has(-1):
                project(*at(t, -1), not has(-2))
        steps(pe, step)


def tokens_phase(nc, *programs):
    with ExitStack() as ctx:
        psum = {"read": {}}
        with nc.Block() as block:
            made = [tokens_program(nc, ctx, block, psum, *args, **options) for args, options in programs]
            for stage in range(2):
                for program in made:
                    next(program, None)


def attention_phase(nc, name, q_parts, k_parts, v_dram, o_dram, sums_dram, ident_dram, *, keys, key_tiles):
    kp = keys // key_tiles
    q_tiles = SEQ // P
    HALF = SEQ // 2
    batches = key_tiles * 2
    steps = batches * HG
    fills = steps // 2
    entries = 1 if key_tiles > 1 else 2
    groups = entries * HEADS // HG
    bodies = BATCH // entries
    loads_heads = HG if key_tiles > 1 else HEADS
    slots = groups * HG // loads_heads
    row_lead = 4
    lead = fills + row_lead
    fill_tiles = HG * q_tiles // fills
    PSLOTS = 4
    assert fills % 2 == 0 and fill_tiles * keys <= SEQ
    with ExitStack() as ctx:
        def sb(n, shape, dt):
            return ctx.enter_context(nc.sbuf_tensor(f"{name}_{n}", shape, dt))

        def ps(n, shape):
            return ctx.enter_context(nc.psum_tensor(f"{name}_{n}", shape, F32))

        sem = ctx.enter_context(semaphores(nc, name))

        def sems(n, count=2):
            return [sem(f"{n}{z}") for z in range(count)]

        ident = sb("ident", [P, P], F32)
        q_st = [sb(f"q{u}", [SR + 1, loads_heads, SEQ], BF16) for u in range(slots)]
        k_st = [sb(f"k{u}", [SR + 1, loads_heads, keys], BF16) for u in range(slots)]
        v_st = [sb(f"v{u}", [kp, key_tiles, loads_heads * VW], F32) for u in range(slots)]
        maxs = [sb(f"maxs{z}", [P, HG * q_tiles], F32) for z in range(2)]
        max_row = [sb(f"max_row{z}", [HG * q_tiles, P], BF16) for z in range(2)]
        probs = [[sb(f"p{z}_{h}", [kp, HALF], F32) for h in range(HG)] for z in range(PSLOTS)]
        o_sb = [sb(f"o{e}", [P, HEADS // HG, SEQ], F32) for e in range(entries)]
        ps_s = [ps(f"pss{z}", [kp, HALF]) for z in range(2)]
        ps_m = [ps(f"psm{z}", [P, 2, 512]) for z in range(2)]
        ps_o = [ps(f"pso{half}", [P, HALF]) for half in range(2)]

        consts = sem("consts")
        ones = sem("ones")
        loaded = sems("loaded", slots)
        filled = sem("filled")
        taken = sems("taken")
        turned = sem("turned")
        row_ready = sem("row_ready")
        row_placed = sems("row_placed")
        scored = sem("scored")
        exps = sems("exps")
        weighted = sems("weighted", PSLOTS)
        o_taken = sems("o_taken")
        stored = sems("stored", entries)

        LOADS = 16 * (2 * len(Q_STACK) + 1)
        STORES = 16 * 2 * HG
        G_BATCHES = groups * batches

        def count(body, n, per_body, turns):
            assert per_body % turns == 0
            return body * (per_body // turns) + n // turns

        def home(G):
            at = G * HG // loads_heads
            return at % slots, G * HG % loads_heads

        def loop(eng, body):
            if bodies > 2:
                with eng.Fori(0, bodies - 1) as i:
                    body(i, False)
            else:
                for i in range(bodies - 1):
                    body(i, False)
            body(bodies - 1, True)

        with nc.Block() as block:

            @block.sync
            def _(sp):
                sp.dma_start(ident[:], ident_dram).then_inc(consts, 16)

                def load(b, hg, u):
                    for s in range(len(Q_STACK)):
                        for st, parts, stack, width in ((q_st, q_parts, Q_STACK, SEQ),
                                                        (k_st, k_parts, K_STACK, keys)):
                            rows = parts[stack[s]][hg * HG * DH:(hg * HG + loads_heads) * DH,
                                                   bass.ds(b * width, width)]
                            sp.dma_start(st[u][s * DH:(s + 1) * DH, :, :],
                                         rows.rearrange("(h d) n -> d h n", d=DH)).then_inc(loaded[u], 16)
                    sp.dma_start(
                        v_st[u][:], v_dram.rearrange("(b t p) n -> b p t n", t=key_tiles, p=kp)[
                            bass.ds(b, 1), :, :, hg * HG * VW:(hg * HG + loads_heads) * VW].rearrange(
                                "b p t n -> p (b t) n")).then_inc(loaded[u], 16)

                def place_row(body, G):
                    u, h0 = home(G)
                    sp.wait_ge(row_ready, body * groups + G + 1)
                    sp.dma_start(q_st[u][SR:SR + 1, h0:h0 + HG, :].rearrange("a h n -> a (h n)"),
                                 max_row[G % 2][:]).then_inc(row_placed[G % 2], 16)

                def store(body, e):
                    for half in range(2):
                        sp.wait_ge(o_taken[half], (body * entries + e + 1) * (HEADS // HG))
                    for h in range(HG):
                        top = h * VW
                        sp.dma_start(
                            o_dram.rearrange("(g h d) n -> d h g n", h=HG, d=DH)[
                                :, h, :, bass.ds((body * entries + e) * SEQ, SEQ)],
                            o_sb[e][top:top + DH, :, :]).then_inc(stored[e], 16)
                        sp.dma_start(
                            sums_dram.rearrange("b (g h) n -> h b g n", h=HG)[
                                h:h + 1, bass.ds(body * entries + e, 1)].rearrange("h b g n -> (h b) g n"),
                            o_sb[e][top + DH:top + DH + 1, :, :]).then_inc(stored[e], 16)

                groups_per_load = loads_heads // HG
                for u in range(slots):
                    load(u * groups_per_load // (HEADS // HG), u * groups_per_load % (HEADS // HG), u)
                ahead = lead // fills
                for G in range(ahead):
                    place_row(0, G)

                def body(i, last):
                    for G in range(groups):
                        if not last or G + ahead < groups:
                            place_row(i, G + ahead)
                        if not last and (G + 1) % groups_per_load == 0:
                            n = (G + 1) * batches - 1
                            sp.wait_ge(weighted[n % PSLOTS], count(i, n, G_BATCHES, PSLOTS) + 1)
                            load(i * entries + entries + G // (HEADS // HG),
                                 (G + 1 - groups_per_load) % (HEADS // HG), home(G)[0])
                        if (G + 1) % (HEADS // HG) == 0:
                            store(i, G // (HEADS // HG))
                loop(sp, body)
                for e in range(entries):
                    sp.wait_ge(stored[e], STORES * bodies)

            @block.gpsimd
            def _(pool):
                for u in range(slots):
                    pool.memset(k_st[u][SR:SR + 1, :, :], 1.0).then_inc(ones, 1)

            @block.tensor
            def _(pe):
                pe.wait_ge(consts, 16)

                def fill(body, n):
                    G, f = divmod(n, fills)
                    u, h0 = home(G)
                    if f == 0 and h0 == 0:
                        pe.wait_ge(loaded[u], (body + G // groups) * LOADS + LOADS)
                    if f == 1:
                        pe.wait_ge(row_ready, body * groups + G)
                    z = n % 2
                    pe.wait_ge(taken[z], count(body, n, groups * fills, 2))
                    for j in range(fill_tiles):
                        h, qt = divmod(f * fill_tiles + j, q_tiles)
                        lhs = q_st[u][0:SR, h0 + h, qt * P:(qt + 1) * P]
                        if key_tiles > 1:
                            for half in range(2):
                                mm = pe.matmul(ps_m[z][:, half, :], lhs,
                                               k_st[u][0:SR, h0 + h, half * HALF:(half + 1) * HALF],
                                               start=True, stop=True)
                        else:
                            bank, at = divmod(j, fill_tiles // 2)
                            mm = pe.matmul(ps_m[z][:, bank, at * keys:(at + 1) * keys], lhs,
                                           k_st[u][0:SR, h0 + h, :], start=True, stop=True)
                    mm.then_inc(filled, 1)

                def turn(body, G):
                    for n in ((G + 1) * fills - 2, (G + 1) * fills - 1):
                        pe.wait_ge(taken[n % 2], count(body, n, groups * fills, 2) + 1)
                    pe.transpose(ps_m[1][0:HG * q_tiles, 0, 0:P], maxs[G % 2][:], ident[:]
                                 ).then_inc(turned, 1)

                def advance(body, n, last):
                    if not last or n < groups * fills:
                        fill(body, n)
                    if n % fills == 0 and n > 0 and (not last or n <= groups * fills):
                        turn(body, n // fills - 1)

                def score(body, S):
                    G, s = divmod(S, steps)
                    u, h0 = home(G)
                    kt, half, h = s // (2 * HG), s // HG % 2, s % HG
                    if s == 0:
                        pe.wait_ge(row_placed[G % 2], count(body, G, groups, 2) * 16 + 16)
                    z = S % 2
                    pe.wait_ge(exps[z], count(body, S, groups * steps, 2))
                    pe.matmul(ps_s[z][:], k_st[u][:, h0 + h, kt * kp:(kt + 1) * kp],
                              q_st[u][:, h0 + h, half * HALF:(half + 1) * HALF],
                              start=True, stop=True).then_inc(scored, 1)

                def weigh(body, n):
                    G, bt = divmod(n, batches)
                    u, h0 = home(G)
                    kt, half = divmod(bt, 2)
                    if kt == 0:
                        pe.wait_ge(o_taken[half], body * groups + G)
                    for S in (n * HG + HG - 2, n * HG + HG - 1):
                        pe.wait_ge(exps[S % 2], count(body, S, groups * steps, 2) + 1)
                    for h in range(HG):
                        mm = pe.matmul(ps_o[half][h * VW:(h + 1) * VW, :],
                                       v_st[u][:, kt, (h0 + h) * VW:(h0 + h + 1) * VW],
                                       probs[n % PSLOTS][h][:], start=(kt == 0), stop=(kt == key_tiles - 1))
                    mm.then_inc(weighted[n % PSLOTS], 1)

                for n in range(lead):
                    advance(0, n, False)
                pe.wait_ge(ones, slots)

                def body(i, last):
                    for n in range(G_BATCHES):
                        for h in range(HG // 2):
                            score(i, n * HG + h)
                        if n > 0:
                            weigh(i, n - 1)
                        if key_tiles == 1:
                            advance(i, n * HG // 2 + lead, last)
                        for h in range(HG // 2, HG):
                            score(i, n * HG + h)
                        if key_tiles > 1:
                            advance(i, n * HG // 2 + lead, last)
                        advance(i, n * HG // 2 + 1 + lead, last)
                    weigh(i, G_BATCHES - 1)
                loop(pe, body)

            @block.scalar
            def _(act):
                act.preload_act_table(ACT.Exp)

                def evacuate(body, G, half):
                    n = G * batches + batches - 2 + half
                    e, hg = divmod(G, HEADS // HG)
                    act.wait_ge(stored[e], body * STORES)
                    act.wait_ge(weighted[n % PSLOTS], count(body, n, G_BATCHES, PSLOTS) + 1)
                    act.activation(o_sb[e][:, hg, half * HALF:(half + 1) * HALF], ps_o[half][:], ACT.Copy
                                   ).then_inc(o_taken[half], 1)

                def body(i, last):
                    for S in range(groups * steps):
                        n, h = divmod(S, HG)
                        if h == 0:
                            act.wait_ge(weighted[n % PSLOTS], count(i, n, G_BATCHES, PSLOTS))
                        act.wait_ge(scored, i * (groups * steps) + S + 1)
                        act.activation(probs[n % PSLOTS][h][:], ps_s[S % 2][:], ACT.Exp,
                                       scale=float(DH) ** -0.5).then_inc(exps[S % 2], 1)
                        G, s = divmod(S, steps)
                        if s == steps - 1:
                            evacuate(i, G, 0)
                        if s == HG - 1 and G > 0:
                            evacuate(i, G - 1, 1)
                    evacuate(i, groups - 1, 1)
                loop(act, body)

            @block.vector
            def _(dv):
                def take(body, n):
                    G, f = divmod(n, fills)
                    z = n % 2
                    dv.wait_ge(filled, body * (groups * fills) + n + 1)
                    if key_tiles > 1:
                        dv.tensor_reduce(maxs[G % 2][:, f:f + 1], ps_m[z][:].rearrange("p b k -> p (b k)"),
                                         AX_X, ALU.max).then_inc(taken[z], 1)
                    else:
                        half = fill_tiles // 2
                        dv.tensor_reduce(
                            maxs[G % 2][:, f * fill_tiles:(f + 1) * fill_tiles].rearrange(
                                "p (b t) -> p b t", b=2),
                            ps_m[z][:, :, 0:half * keys].rearrange("p b (t k) -> p b t k", k=keys),
                            AX_X, ALU.max).then_inc(taken[z], 1)

                def negate(body, G):
                    dv.wait_ge(turned, body * groups + G + 1)
                    dv.wait_ge(row_placed[G % 2], count(body, G, groups, 2) * 16)
                    dv.tensor_scalar(max_row[G % 2][:], ps_m[1][0:HG * q_tiles, 0, 0:P], -1.0, None,
                                     ALU.mult).then_inc(row_ready, 1)

                def advance(body, n, last):
                    if n % fills == 0 and n > 0 and (not last or n <= groups * fills):
                        negate(body, n // fills - 1)
                    if not last or n < groups * fills:
                        take(body, n)

                for n in range(lead):
                    advance(0, n, False)

                def body(i, last):
                    for S in range(0, groups * steps, 2):
                        advance(i, S // 2 + lead, last)
                loop(dv, body)

def route_phase(nc, logits, gates, tokens, targets, tile_expert, c_dram, w_dram, w_parts):
    with ExitStack() as ctx:
        def sb(n, shape, dt=F32):
            return ctx.enter_context(nc.sbuf_tensor(f"route_{n}", shape, dt))

        sem = ctx.enter_context(semaphores(nc, "route"))

        TE = [P, NT, E]
        rev = sb("rev", [P, E])
        tri = sb("tri", [P, P])
        ones = sb("ones", [P, P])
        tile_no = sb("tile_no", [1, SLOT_TILES])
        zeros = sb("zeros", [P, NT])
        best = [sb(f"best{k}", [P, NT]) for k in range(TOP)]
        tie = sb("tie", TE)
        cand = sb("cand", TE)
        first = sb("first", [P, NT])
        sel = [sb(f"sel{k}", TE) for k in range(TOP)]
        others = sb("others", TE)
        chosen = sb("chosen", [P, NT * E])
        gap = sb("gap", [P, NT])
        gap_exp = sb("gap_exp", [P, NT])
        gap_sum = sb("gap_sum", [P, NT])
        totals = sb("totals", TE)
        upto = sb("upto", TE)
        before = sb("before", TE)
        padded = sb("padded", [P, E])
        padded_i = sb("padded_i", [P, E], I32)
        tiles_i = sb("tiles_i", [P, E], I32)
        tiles = sb("tiles", [P, E])
        tile_end = sb("tile_end", [P, E])
        tile_start = sb("tile_start", [P, E])
        slot_start = sb("slot_start", [P, E])
        place = sb("place", TE)
        place2 = sb("place2", TE)
        picked = [sb(f"picked{k}", TE) for k in range(TOP)]
        slot_f = sb("slot_f", [P, TOP, NT])
        slots = sb("slots", [P, TOP, NT], I32)
        past = sb("past", [1, SLOT_TILES, E])
        past_n = sb("past_n", [1, SLOT_TILES])
        past_c = sb("past_c", [1, SLOT_TILES])
        ps_rank = ctx.enter_context(nc.psum_tensor("route_rank", [P, 512], F32))
        ps_total = ctx.enter_context(nc.psum_tensor("route_total", [P, 512], F32))
        consts = sem("consts")
        zeroed = sem("zeroed")
        dve = sem("dve")
        counted = sem("counted")
        gap_ready = sem("gap_ready")
        chosen_ready = sem("chosen_ready")
        exp_ready = sem("exp_ready")
        CHUNK = NT // 2
        chunks = [(c, t0) for c in range(TOP) for t0 in range(0, NT, CHUNK)]
        token_p = sb("token_p", [P, 1])
        token_t = sb("token_t", [P, TOP, NT])
        spare = sb("spare", [P, ROWS])
        row_no = sb("row_no", [P, ROWS])
        place_no = sb("place_no", [P, P])
        row_i = sb("row_i", [P, TOP, NT], I32)
        place_i = sb("place_i", [P, TOP, NT], I32)
        row_f = sb("row_f", [P, TOP, NT])
        place_f = sb("place_f", [P, TOP, NT])
        at_row = [sb(f"at_row{z}", [P, CHUNK, ROWS], BF16) for z in range(2)]
        at_place = [sb(f"at_place{z}", [P, CHUNK, P], BF16) for z in range(2)]
        ids = [sb(f"ids{z}", [P, CHUNK, 2, ROWS], BF16) for z in range(2)]
        tile_part = sb("tile_part", [P, ROWS])
        number, row_to, spare_to, target_f = (sb(n, [P, ROWS]) for n in ("number", "row_to", "spare_to",
                                                                          "target_f"))
        numbers_i = sb("numbers_i", [P, ROWS], I32)
        ps_ids = ctx.enter_context(nc.psum_tensor("route_ids", [P, 512], F32))
        marked = sem("marked")
        gathered = sem("gathered")

        PIECE = 1024
        STAGES = 4
        EARLY = STAGES
        stage = [sb(f"stage{z}", [P, PIECE]) for z in range(STAGES)]
        w_loaded = [sem(f"w_loaded{z}") for z in range(STAGES)]
        high = sem("high")
        scaled = sem("scaled")
        low = sem("low")
        pieces = [(e, at) for e in range(E) for at in range(0, DC * F, PIECE)]

        def load_weights(sp):
            for n, (e, at) in enumerate(pieces):
                if n >= STAGES:
                    sp.wait_ge(low, n - STAGES + 1)
                rows = w_dram[e].rearrange("(c p) n -> p c n", p=P)
                width = rows.shape[2]
                sp.dma_start(stage[n % STAGES][:].rearrange("p (c n) -> p c n", n=width),
                             rows[:, at // width:(at + PIECE) // width, :]).then_inc(w_loaded[n % STAGES], 16)

        def cut_high(act, first, last):
            for n, (e, at) in list(enumerate(pieces))[first:last]:
                act.wait_ge(w_loaded[n % STAGES], 16 * (n // STAGES + 1))
                act.activation(w_parts[0][:, e, at:at + PIECE], stage[n % STAGES][:], ACT.Copy,
                               scale=W_SCALE).then_inc(high, 1)
                act.wait_ge(high, n + 1)
                act.activation(stage[n % STAGES][:], stage[n % STAGES][:], ACT.Copy,
                               scale=W_SCALE).then_inc(scaled, 1)

        def wide_e(ap):
            return ap[:, :, None].broadcast_to(TE)

        def wide_t(ap):
            return ap[:, None, :].broadcast_to(TE)

        with nc.Block() as block:

            @block.sync
            def _(sp):
                for dst, key in ((rev, "rev"), (tri, "tri"), (ones, "ones"), (tile_no, "tile_no"),
                                 (token_p, "token_p"), (token_t, "token_t"), (row_no, "row_no"),
                                 (place_no, "place_no"), (spare, "spare")):
                    sp.dma_start(dst[:], c_dram[key]).then_inc(consts, 16)
                load_weights(sp)

            @block.scalar
            def _(act):
                act.preload_act_table(ACT.Exp)
                cut_high(act, 0, EARLY)
                act.wait_ge(gap_ready, 1)
                act.activation(gap_exp[:], gap[:], ACT.Exp).then_inc(exp_ready, 1)
                cut_high(act, EARLY, len(pieces))

            @block.tensor
            def _(pe):
                pe.wait_ge(chosen_ready, 1)
                pe.matmul(ps_rank[:, 0:NT * E], tri[:], chosen[:], start=True, stop=True)
                pe.matmul(ps_total[:, 0:NT * E], ones[:], chosen[:], start=True, stop=True
                          ).then_inc(counted, 1)
                for n in range(len(chunks)):
                    pe.wait_ge(marked, n + 1)
                    for t in range(CHUNK):
                        mm = pe.matmul(ps_ids[:, 0:2 * ROWS], at_place[n % 2][:, t, :],
                                       ids[n % 2][:, t].rearrange("p k r -> p (k r)"),
                                       start=(n == 0 and t == 0),
                                       stop=(n == len(chunks) - 1 and t == CHUNK - 1))
                    mm.then_inc(gathered, 1)

            @block.vector
            def _(dv):
                k = 0

                def step(ins):
                    nonlocal k
                    k += 1
                    ins.then_inc(dve, 1)

                def own():
                    dv.wait_ge(dve, k)

                dv.memset(zeros[:], 0.0).then_inc(zeroed, 1)
                dv.wait_ge(zeroed, 1)
                dv.wait_ge(consts, 16 * 9)
                src = logits
                for c in range(TOP):
                    step(dv.tensor_reduce(best[c][:], src[:], AX_X, ALU.max))
                    own()
                    step(dv.tensor_tensor(tie[:], src[:], wide_e(best[c]), ALU.is_equal))
                    own()
                    step(dv.tensor_tensor(cand[:], tie[:], wide_t(rev), ALU.mult))
                    own()
                    step(dv.tensor_reduce(first[:], cand[:], AX_X, ALU.max))
                    own()
                    step(dv.tensor_tensor(sel[c][:], wide_t(rev), wide_e(first), ALU.is_equal))
                    own()
                    if c == 0:
                        step(dv.scalar_tensor_tensor(others[:], sel[0][:], -BIG, src[:], ALU.mult, ALU.add))
                        own()
                        src = others
                dv.tensor_tensor(gap[:], best[1][:], best[0][:], ALU.subtract).then_inc(gap_ready, 1)
                dv.tensor_tensor(chosen[:].rearrange("p (t e) -> p t e", e=E), sel[0][:], sel[1][:], ALU.add
                                 ).then_inc(chosen_ready, 1)
                dv.wait_ge(exp_ready, 1)
                step(dv.tensor_scalar(gap_sum[:], gap_exp[:], 1.0, None, ALU.add))
                own()
                step(dv.reciprocal(gates[:, 0, :], gap_sum[:]))
                own()
                step(dv.tensor_tensor(gates[:, 1, :], gates[:, 0, :], gap_exp[:], ALU.mult))
                dv.wait_ge(counted, 1)
                step(dv.tensor_copy(totals[:], ps_total[:, 0:NT * E].rearrange("p (t e) -> p t e", e=E)))
                own()
                for e in range(E):
                    step(dv.tensor_tensor_scan(upto[:, :, e], totals[:, :, e], zeros[:, 0:NT], 0.0,
                                               ALU.add, ALU.add))
                own()
                step(dv.tensor_tensor(before[:], upto[:], totals[:], ALU.subtract))
                step(dv.tensor_scalar(padded[:], upto[:, NT - 1, :], float(ST - 1), None, ALU.add))
                own()
                step(dv.tensor_copy(padded_i[:], padded[:]))
                own()
                step(dv.tensor_scalar(tiles_i[:], padded_i[:], ST.bit_length() - 1, None,
                                      ALU.logical_shift_right))
                own()
                step(dv.tensor_copy(tiles[:], tiles_i[:]))
                own()
                step(dv.tensor_tensor_scan(tile_end[:], tiles[:], zeros[:, 0:E], 0.0, ALU.add, ALU.add))
                own()
                step(dv.tensor_tensor(tile_start[:], tile_end[:], tiles[:], ALU.subtract))
                own()
                step(dv.tensor_scalar(slot_start[:], tile_start[:], float(ST), None, ALU.mult))
                own()
                step(dv.tensor_tensor(place[:], ps_rank[:, 0:NT * E].rearrange("p (t e) -> p t e", e=E),
                                      before[:], ALU.add))
                own()
                step(dv.tensor_tensor(place2[:], place[:], wide_t(slot_start), ALU.add))
                own()
                for c in range(TOP):
                    step(dv.tensor_tensor(picked[c][:], sel[c][:], place2[:], ALU.mult))
                own()
                for c in range(TOP):
                    step(dv.tensor_reduce(slot_f[:, c, :], picked[c][:], AX_X, ALU.add))
                own()
                step(dv.tensor_copy(slots[:], slot_f[:]))
                own()
                step(dv.tensor_scalar(row_i[:], slots[:], P.bit_length() - 1, None, ALU.logical_shift_right))
                step(dv.tensor_scalar(place_i[:], slots[:], P - 1, None, ALU.bitwise_and))
                own()
                step(dv.tensor_copy(row_f[:], row_i[:]))
                step(dv.tensor_copy(place_f[:], place_i[:]))
                own()
                for n, (c, t0) in enumerate(chunks):
                    z = n % 2
                    tiles_of = slice(t0, t0 + CHUNK)
                    RC, PC = [P, CHUNK, ROWS], [P, CHUNK, P]
                    if n >= 2:
                        dv.wait_ge(gathered, n - 1)
                    step(dv.tensor_tensor(at_row[z][:], row_no[:, None, :].broadcast_to(RC),
                                          row_f[:, c, tiles_of, None].broadcast_to(RC), ALU.is_equal))
                    own()
                    step(dv.tensor_scalar(ids[z][:, :, 0, :], at_row[z][:], token_p[:, 0:1], None, ALU.mult))
                    step(dv.tensor_tensor(ids[z][:, :, 1, :], at_row[z][:],
                                          token_t[:, c, tiles_of, None].broadcast_to(RC), ALU.mult))
                    own()
                    dv.tensor_tensor(at_place[z][:], place_no[:, None, :].broadcast_to(PC),
                                     place_f[:, c, tiles_of, None].broadcast_to(PC), ALU.is_equal
                                     ).then_inc(marked, 1)
                step(dv.tensor_tensor(past[:], tile_no[:, :, None].broadcast_to([1, SLOT_TILES, E]),
                                      tile_end[0:1, None, :].broadcast_to([1, SLOT_TILES, E]), ALU.is_ge))
                own()
                step(dv.tensor_reduce(past_n[:], past[:], AX_X, ALU.add))
                own()
                step(dv.tensor_scalar(past_c[:], past_n[:], float(E - 1), None, ALU.min))
                own()
                step(dv.tensor_copy(tile_expert[:], past_c[:]))
                dv.wait_ge(gathered, len(chunks))
                step(dv.tensor_scalar(tile_part[:], ps_ids[:, ROWS:2 * ROWS], float(P), None, ALU.mult))
                own()
                step(dv.tensor_tensor(number[:], tile_part[:], ps_ids[:, 0:ROWS], ALU.add))
                own()
                step(dv.tensor_scalar(row_to[:], number[:], float(-P), 0.0, ALU.add, ALU.max))
                step(dv.scalar_tensor_tensor(spare_to[:], number[:], 0.0, spare[:], ALU.is_equal, ALU.mult))
                own()
                step(dv.tensor_copy(numbers_i[:], row_to[:]))
                step(dv.tensor_tensor(target_f[:], row_to[:], spare_to[:], ALU.add))
                own()
                step(dv.tensor_scalar(tokens[:], numbers_i[:], N - 1, None, ALU.bitwise_and))
                step(dv.tensor_copy(targets[:], target_f[:]))
                own()

            @block.gpsimd
            def _(pool):
                for n, (e, at) in enumerate(pieces):
                    pool.wait_ge(scaled, n + 1)
                    pool.tensor_tensor(w_parts[1][:, e, at:at + PIECE], stage[n % STAGES][:],
                                       w_parts[0][:, e, at:at + PIECE], ALU.subtract).then_inc(low, 1)


def expert_phase(nc, x_dram, tokens, targets, eo_dram, tile_expert, w_parts, b1_dram, b2_dram,
                 ln_g, ln_b, ident_dram):
    (w1h, w1l), (w2h, w2l) = w_parts
    JT = ST // P
    HC = FC // 2
    with ExitStack() as ctx:
        def sb(n, shape, dt=F32):
            return ctx.enter_context(nc.sbuf_tensor(f"moe_{n}", shape, dt))

        def two(n, shape, dt=F32):
            return [sb(f"{n}{u}", shape, dt) for u in range(2)]

        def ps(n, shape):
            return [ctx.enter_context(nc.psum_tensor(f"moe_{n}{u}", shape, F32)) for u in range(2)]

        sem = ctx.enter_context(semaphores(nc, "moe"))

        def sems(n):
            return [sem(f"{n}{u}") for u in range(2)]

        ident = sb("ident", [P, P])
        g_col = sb("g_col", [P, DC])
        b_col = sb("b_col", [P, DC])
        xs = two("xs", [P, JT, D])
        b1 = two("b1", [P, FC])
        b2 = two("b2", [P, D])
        hf = two("hf", [P, DC, ST])
        hh = two("hh", [P, DC, ST], F16)
        hl = two("hl", [P, DC, ST], F16)
        h1 = two("h1", [P, FC, ST])
        h1h = two("h1h", [P, FC, ST], F16)
        h1l = two("h1l", [P, FC, ST], F16)
        eo = two("eo", [P, JT, D])
        ps_x = ps("psx", [P, DC, ST])
        ps_h = ps("psh", [P, HC, ST])
        ps_e = ps("pse", [P, JT, D])
        consts = sem("consts")
        xs_loaded = sems("xs_loaded")
        b1_loaded = sems("b1_loaded")
        b2_loaded = sems("b2_loaded")
        turned = sems("turned")
        hf_ready = sems("hf_ready")
        hh_ready = sems("hh_ready")
        h_ready = sems("h_ready")
        up = sems("up")
        gelus = sems("gelus")
        h1h_ready = sems("h1h_ready")
        h1_ready = sems("h1_ready")
        down = sems("down")
        eo_ready = sems("eo_ready")
        stored = sems("stored")

        T = SLOT_TILES
        LOOPS = (T - 2) // 2

        def pairs(engine, body):
            with engine.Fori(0, LOOPS) as i:
                for u in range(2):
                    body(i, u, True, True)
            for t in range(2 * LOOPS, T):
                body(t // 2, t % 2, t + 2 < T, t + 1 < T)

        with nc.Block() as block:

            @block.sync
            def _(sp):
                sp.dma_start(ident[:], ident_dram).then_inc(consts, 16)
                sp.dma_start(g_col[:], ln_g).then_inc(consts, 16)
                sp.dma_start(b_col[:], ln_b).then_inc(consts, 16)

                def expert_of(t):
                    return sp.value_load(tile_expert[0:1, bass.ds(t, 1)], min_val=0, max_val=E - 1)

                def load_b1(e, u):
                    sp.dma_start(b1[u][:], b1_dram[bass.ds(e, 1)].rearrange("e p c -> p (e c)")
                                 ).then_inc(b1_loaded[u], 16)

                def load_b2(e, u):
                    sp.dma_start(b2[u][:], b2_dram[bass.ds(e, 1), :].broadcast_to([P, D])
                                 ).then_inc(b2_loaded[u], 16)

                load_b1(expert_of(0), 0)
                load_b1(expert_of(1), 1)
                load_b2(expert_of(0), 0)

                def body(i, u, more2, more1):
                    if more2:
                        e = expert_of(2 * i + u + 2)
                        sp.wait_ge(gelus[u], (i + 1) * FC)
                        load_b1(e, u)
                    if more1:
                        e = expert_of(2 * i + u + 1)
                        sp.wait_ge(eo_ready[1 - u], i + u)
                        load_b2(e, 1 - u)

                pairs(sp, body)

            @block.gpsimd
            def _(pool):
                def gather(t):
                    u = t % 2
                    if t >= 2:
                        pool.wait_ge(turned[u], t // 2)
                    for j in range(JT):
                        pool.indirect_dma_start(
                            out=xs[u][:, j, :], out_offset=None, in_=x_dram,
                            in_offset=bass.IndirectOffsetOnAxis(
                                ap=tokens[:, t * JT + j:t * JT + j + 1], axis=0)
                        ).then_inc(xs_loaded[u], 16)

                def scatter(t):
                    u = t % 2
                    pool.wait_ge(eo_ready[u], t // 2 + 1)
                    for j in range(JT):
                        pool.indirect_dma_start(
                            out=eo_dram, out_offset=bass.IndirectOffsetOnAxis(
                                ap=targets[:, t * JT + j:t * JT + j + 1], axis=0),
                            in_=eo[u][:, j, :], in_offset=None).then_inc(stored[u], 16)

                AHEAD = 3
                for t in range(T + AHEAD):
                    if t < T:
                        gather(t)
                    if t >= AHEAD:
                        scatter(t - AHEAD)
                for u in range(2):
                    pool.wait_ge(stored[u], 16 * JT * ((T + 1 - u) // 2))

            @block.tensor
            def _(pe):
                pe.wait_ge(consts, 48)

                def turn(i, u):
                    pe.wait_ge(hf_ready[u], i)
                    pe.wait_ge(xs_loaded[u], i * 16 * JT + 16 * JT)
                    for j in range(JT):
                        for c in range(DC):
                            mm = pe.transpose(ps_x[u][:, c, j * P:(j + 1) * P],
                                              xs[u][:, j, c * P:(c + 1) * P], ident[:])
                    mm.then_inc(turned[u], 1)

                def layer1(i, u, e):
                    for fc in range(FC):
                        for c in range(DC):
                            at = bass.ds(e * (DC * F) + (c * F + fc * P), P)
                            w_high = w1h[:].rearrange("p e n -> p (e n)")[:, at]
                            w_low = w1l[:].rearrange("p e n -> p (e n)")[:, at]
                            out = ps_h[fc // HC][:, fc % HC, :]
                            pe.matmul(out, w_high, hh[u][:, c, :], start=(c == 0), stop=False)
                            pe.matmul(out, w_high, hl[u][:, c, :], start=False, stop=False)
                            mm = pe.matmul(out, w_low, hh[u][:, c, :], start=False, stop=(c == DC - 1))
                        if fc % HC == HC - 1:
                            mm.then_inc(up[u], 1)

                def layer2(i, u, e):
                    pe.wait_ge(eo_ready[u], i)
                    pe.wait_ge(h1_ready[u], i + 1)
                    for j in range(JT):
                        row = slice(j * P, (j + 1) * P)
                        for fc in range(FC):
                            at = bass.ds(e * (FC * D) + fc * D, D)
                            w_high = w2h[:].rearrange("p e n -> p (e n)")[:, at]
                            w_low = w2l[:].rearrange("p e n -> p (e n)")[:, at]
                            out = ps_e[u][:, j, :]
                            pe.matmul(out, h1h[u][:, fc, row], w_high, start=(fc == 0), stop=False)
                            pe.matmul(out, h1h[u][:, fc, row], w_low, start=False, stop=False)
                            mm = pe.matmul(out, h1l[u][:, fc, row], w_high, start=False, stop=(fc == FC - 1))
                    mm.then_inc(down[u], 1)

                def experts_of(i, count):
                    _, experts = nc.values_load_multi_w_load_instructions(
                        tile_expert[0:1, bass.ds(2 * i, count)], engines=[mybir.EngineType.PE],
                        min_val=0, max_val=E - 1)
                    return experts

                turn(0, 0)
                turn(0, 1)
                first, = experts_of(0, 1)
                pe.wait_ge(h_ready[0], 1)
                layer1(0, 0, first)

                def body(i, u, e, more2, more1):
                    if more1:
                        pe.wait_ge(h_ready[1 - u], i + u + 1)
                        pe.wait_ge(gelus[u], (i + 1) * FC)
                    if more2:
                        turn(i + 1, u)
                    if more1:
                        layer1(i + u, 1 - u, e[u + 1])
                    layer2(i, u, e[u])

                with pe.Fori(0, LOOPS) as i:
                    e = experts_of(i, 3)
                    for u in range(2):
                        body(i, u, e, True, True)
                e = experts_of(LOOPS, T - 2 * LOOPS)
                for t in range(2 * LOOPS, T):
                    i, u = divmod(t, 2)
                    body(i, u, e[t - 2 * LOOPS - u:], t + 2 < T, t + 1 < T)

            @block.scalar
            def _(act):
                act.preload_act_table(ACT.Gelu)

                def body(i, u, more2, more1):
                    act.wait_ge(h1_ready[u], i)
                    act.wait_ge(b1_loaded[u], i * 16 + 16)
                    for fc in range(FC):
                        if fc % HC == 0:
                            act.wait_ge(up[u], i * 2 + fc // HC + 1)
                        act.activation(h1[u][:, fc, :], ps_h[fc // HC][:, fc % HC, :], ACT.Gelu,
                                       bias=b1[u][:, fc:fc + 1], scale=1.0 / W_SCALE).then_inc(gelus[u], 1)
                pairs(act, body)

            @block.vector
            def _(dv):
                dv.wait_ge(consts, 48)

                def normed(i, u):
                    dv.wait_ge(turned[u], i + 1)
                    for c in range(DC):
                        mm = dv.tensor_scalar(hf[u][:, c, :], ps_x[u][:, c, :], g_col[:, c:c + 1],
                                              b_col[:, c:c + 1], ALU.mult, ALU.add)
                    mm.then_inc(hf_ready[u], 1)
                    dv.wait_ge(hf_ready[u], i + 1)
                    dv.wait_ge(up[u], 2 * i)
                    dv.tensor_copy(hh[u][:], hf[u][:]).then_inc(hh_ready[u], 1)
                    dv.wait_ge(hh_ready[u], i + 1)
                    dv.tensor_tensor(hl[u][:], hf[u][:], hh[u][:], ALU.subtract).then_inc(h_ready[u], 1)

                def hidden(i, u):
                    dv.wait_ge(down[u], i)
                    dv.wait_ge(gelus[u], i * FC + FC)
                    dv.tensor_copy(h1h[u][:], h1[u][:]).then_inc(h1h_ready[u], 1)
                    dv.wait_ge(h1h_ready[u], i + 1)
                    dv.tensor_tensor(h1l[u][:], h1[u][:], h1h[u][:], ALU.subtract).then_inc(h1_ready[u], 1)

                def output(i, u):
                    dv.wait_ge(stored[u], i * 16 * JT)
                    dv.wait_ge(b2_loaded[u], i * 16 + 16)
                    dv.wait_ge(down[u], i + 1)
                    dv.scalar_tensor_tensor(eo[u][:], ps_e[u][:], 1.0 / W_SCALE,
                                            b2[u][:, None, :].broadcast_to([P, JT, D]),
                                            ALU.mult, ALU.add).then_inc(eo_ready[u], 1)

                normed(0, 0)
                normed(0, 1)
                hidden(0, 0)

                def body(i, u, more2, more1):
                    if more2:
                        normed(i + 1, u)
                    if more1:
                        hidden(i + u, 1 - u)
                    output(i, u)

                pairs(dv, body)


def combine_phase(nc, x_dram, eo_dram, gates, out_dram):
    with ExitStack() as ctx:
        DEPTH = 3
        BLOCKS = NT // TPB

        def deep(n):
            return [ctx.enter_context(nc.sbuf_tensor(f"mix_{n}{z}", [P, TPB, D], F32)) for z in range(DEPTH)]
        x_sb, out_sb, first, second = deep("x"), deep("out"), deep("first"), deep("second")
        half = ctx.enter_context(nc.sbuf_tensor("mix_half", [P, 2, D], F32))

        sem = ctx.enter_context(semaphores(nc, "mix"))
        loaded = [sem(f"loaded{z}") for z in range(DEPTH)]
        half_ready = sem("half_ready")
        mixed = sem("mixed")
        stored = [sem(f"stored{z}") for z in range(DEPTH)]

        def block_of(ap, b):
            return ap.rearrange("(b t p) d -> b p t d", t=TPB, p=P)[b]
        with nc.Block() as block:

            @block.sync
            def _(sp):
                for b in range(BLOCKS):
                    if b >= DEPTH:
                        sp.wait_ge(mixed, (b - DEPTH + 1) * TPB)
                    for dst, src in ((x_sb, x_dram), (first, eo_dram[0:N]), (second, eo_dram[N:2 * N])):
                        sp.dma_start(dst[b % DEPTH][:], block_of(src, b)).then_inc(loaded[b % DEPTH], 16)

            @block.scalar
            def _(act):
                for b in range(BLOCKS):
                    act.wait_ge(mixed, (b + 1) * TPB)
                    act.dma_start(block_of(out_dram, b), out_sb[b % DEPTH][:]).then_inc(stored[b % DEPTH], 16)
                for z in range(DEPTH):
                    act.wait_ge(stored[z], 16 * len(range(z, BLOCKS, DEPTH)))

            @block.vector
            def _(dv):
                for t in range(NT):
                    b, j = divmod(t, TPB)
                    z = b % DEPTH
                    if j == 0:
                        dv.wait_ge(loaded[z], 16 * 3 * (b // DEPTH + 1))
                        if b >= DEPTH:
                            dv.wait_ge(stored[z], 16 * (b // DEPTH))
                    dv.scalar_tensor_tensor(half[:, t % 2, :], first[z][:, j, :], gates[:, 0, t:t + 1],
                                            x_sb[z][:, j, :], ALU.mult, ALU.add).then_inc(half_ready, 1)
                    dv.wait_ge(half_ready, t + 1)
                    dv.scalar_tensor_tensor(out_sb[z][:, j, :], second[z][:, j, :], gates[:, 1, t:t + 1],
                                            half[:, t % 2, :], ALU.mult, ALU.add).then_inc(mixed, 1)


def build(nc, a, out):
    def scratch(name, shape, dt):
        return nc.dram_tensor("dram_" + name, shape, dt, kind="Internal").ap()

    q1 = scratch("sa_qk_parts", (PARTS, 2 * D, N), BF16)
    v1 = scratch("sa_v", (N, HEADS * VW), F32)
    k2 = scratch("ca_k_parts", (PARTS, D, BATCH * CTX), BF16)
    v2 = scratch("ca_v", (BATCH * CTX, HEADS * VW), F32)
    q2 = scratch("ca_q_parts", (PARTS, D, N), BF16)
    o1 = scratch("sa_o", (D, N), F32)
    o2 = scratch("ca_o", (D, N), F32)
    sums1, r1, sums2, r2 = (scratch(n, (BATCH, HEADS, SEQ), F32)
                            for n in ("sa_sums", "sa_recips", "ca_sums", "ca_recips"))
    x1 = scratch("x1", (N, D), F32)
    x2 = scratch("x2", (N, D), F32)
    xhat = scratch("xhat", (N, D), F32)
    eo = scratch("expert_outputs", (TOP * N + SLOTS, D), F32)
    ident = a["ident"]

    tokens_phase(
        nc,
        (("kv", a["ctx"], CTX, 1), dict(
            ln_g=a["ca_kv_ln_g"], ln_b=a["ca_kv_ln_b"], ident_dram=ident,
            qk=(a["ca_wk"], a["ca_bk"], k2), v=(a["ca_wv"], a["ca_bv"], v2))),
        (("qkv", a["x"], P, N // (TPB * P)), dict(
            ln_g=a["sa_ln_g"], ln_b=a["sa_ln_b"], ident_dram=ident,
            qk=(a["sa_wqk"], a["sa_bqk"], q1), v=(a["sa_wv"], a["sa_bv"], v1))))
    attention_phase(nc, "sa", q1[:, 0:D, :], q1[:, D:2 * D, :], v1, o1, sums1, ident, keys=SEQ,
                    key_tiles=SEQ // P)
    tokens_phase(
        nc,
        (("mid", a["x"], P, N // (TPB * P)), dict(
            ln_g=a["ca_q_ln_g"], ln_b=a["ca_q_ln_b"], ident_dram=ident,
            attn=(o1, sums1, r1, a["sa_wo"], a["sa_bo"], x1), qk=(a["ca_wq"], a["ca_bq"], q2))))
    attention_phase(nc, "ca", q2, k2, v2, o2, sums2, ident, keys=CTX, key_tiles=1)
    with ExitStack() as ctx:
        gates = ctx.enter_context(nc.sbuf_tensor("gates", [P, TOP, NT], F32))
        tile_expert = ctx.enter_context(nc.sbuf_tensor("tile_expert", [1, SLOT_TILES], I32))
        tokens = ctx.enter_context(nc.sbuf_tensor("tokens", [P, ROWS], I32))
        targets = ctx.enter_context(nc.sbuf_tensor("targets", [P, ROWS], I32))
        logits = ctx.enter_context(nc.sbuf_tensor("logits", [P, NT, E], F32))
        with ExitStack() as wctx:
            def parts_of(w):
                return [wctx.enter_context(nc.sbuf_tensor(f"w{w}_{part}", [P, E, DC * F], F16))
                        for part in ("high", "low")]
            w1 = parts_of(1)
            tokens_phase(
                nc,
                (("last", x1, P, N // (TPB * P)), dict(
                    ln_g=a["moe_ln_g"], ln_b=a["moe_ln_b"], ident_dram=ident,
                    attn=(o2, sums2, r2, a["ca_wo"], a["ca_bo"], x2),
                    router=(a["w_r"], a["b_r"], logits, xhat), weights=(a["w1"], *w1))))
            w2 = parts_of(2)
            route_phase(nc, logits, gates, tokens, targets, tile_expert, a, a["w2"], w2)
            expert_phase(nc, xhat, tokens, targets, eo, tile_expert, (w1, w2), a["b1"], a["b2"],
                         a["moe_ln_g"], a["moe_ln_b"], ident)
        combine_phase(nc, x2, eo, gates, out)


def laid_out(inputs):
    a = {n.removeprefix("L0_xattn_"): np.asarray(v) for n, v in inputs.items()}

    def column(v):
        return v.reshape(-1, P).T
    out = {"x": a["x"].reshape(N, D), "ctx": a["ctx_1024"].reshape(BATCH * CTX, D)}
    for n in ("sa_ln_g", "sa_ln_b", "ca_q_ln_g", "ca_q_ln_b", "ca_kv_ln_g", "ca_kv_ln_b", "moe_ln_g",
              "moe_ln_b"):
        out[n] = column(a[n])
    out["sa_wqk"], out["sa_bqk"] = a["sa_in_w"][:2 * D].T, column(a["sa_in_b"][:2 * D])
    out["ca_wq"], out["ca_bq"] = a["ca_in_w"][:D].T, column(a["ca_in_b"][:D])
    out["ca_wk"], out["ca_bk"] = a["ca_in_w"][D:2 * D].T, column(a["ca_in_b"][D:2 * D])
    for n in ("sa", "ca"):
        out[n + "_wv"], out[n + "_bv"] = a[n + "_in_w"][2 * D:].T, a[n + "_in_b"][2 * D:]
        out[n + "_wo"], out[n + "_bo"] = a[n + "_out_w"].T, a[n + "_out_b"]
    out["w_r"], out["b_r"] = a["router_w"].T, a["router_b"]
    out["w1"], out["w2"] = a["e_fc1_w"].transpose(0, 2, 1), a["e_fc2_w"].transpose(0, 2, 1)
    out["b1"], out["b2"] = a["e_fc1_b"].reshape(E, FC, P).transpose(0, 2, 1), a["e_fc2_b"]
    return out


def constants():
    return {
        "ident": np.eye(P, dtype=np.float32),
        "rev": np.tile(np.arange(E, 0, -1, dtype=np.float32), (P, 1)),
        "tri": np.triu(np.ones((P, P), np.float32), 1),
        "ones": np.ones((P, P), np.float32),
        "tile_no": np.arange(SLOT_TILES, dtype=np.float32)[None, :],
        "token_p": np.arange(P, dtype=np.float32)[:, None],
        "token_t": np.tile(np.arange(1, TOP * NT + 1, dtype=np.float32).reshape(TOP, NT), (P, 1, 1)),
        "spare": TOP * N + np.arange(ROWS, dtype=np.float32)[None, :] * P + np.arange(P)[:, None].astype(
            np.float32),
        "row_no": np.tile(np.arange(ROWS, dtype=np.float32), (P, 1)),
        "place_no": np.tile(np.arange(P, dtype=np.float32), (P, 1)),
    }


def kernel(**inputs):
    import concourse.bacc as bacc
    from concourse.bass_utils import run_bass_kernel_spmd

    nc = bacc.Bacc("TRN2", target_bir_lowering=False, num_devices=1)
    arrays, aps = {}, {}
    for name, value in (laid_out(inputs) | constants()).items():
        value = np.ascontiguousarray(value)
        arrays[f"in_{name}"] = value
        aps[name] = nc.dram_tensor(f"in_{name}", value.shape, mybir.dt.from_np(value.dtype),
                                   kind="ExternalInput").ap()
    out = nc.dram_tensor("out", (N, D), F32, kind="ExternalOutput").ap()
    build(nc, aps, out)
    got = run_bass_kernel_spmd(nc, [arrays], core_ids=[0])
    return got.results[0]["out"].reshape(BATCH, SEQ, D)
```
